# Optimizing a Trainium2 kernel written in Bass

```python
import numpy as np
import jax
import jax.numpy as jnp

def _softmax(x, axis=-1):
    return jax.nn.softmax(x, axis=axis)

def _gelu(x):
    return jax.nn.gelu(x, approximate=True)

def _silu(x):
    return jax.nn.silu(x)

def _sigmoid(x):
    return jax.nn.sigmoid(x)

def _layernorm(x, axis=-1, eps=1e-05):
    m = jnp.mean(x, axis=axis, keepdims=True)
    v = jnp.var(x, axis=axis, keepdims=True)
    return (x - m) / jnp.sqrt(v + eps)

def _scatter_add(tgt, idx, src, axis=0):
    return tgt.at[idx].add(src)

def _segment_sum(src, seg, n):
    return jax.ops.segment_sum(src, seg, n)
kernel_name = 'mk_sandwich_d1_jaxref_r8_f4ca7e'

def setup_inputs(seed: int=0):
    np.random.seed(seed)
    _w = jnp.asarray

    def _L0_attn_setup():
        import jax, jax.numpy as jnp
        import numpy as np
        import math
        B, T, C = (2, 256, 128)
        H, DK, DV = (16, 64, 64)
        key = jax.random.key(seed)
        ks = jax.random.split(key, 5)
        x = jax.random.normal(ks[0], (B, T, C), dtype=jnp.float32)
        w_q = jax.random.normal(ks[1], (H, DK, C), dtype=jnp.float32) / math.sqrt(C)
        w_k = jax.random.normal(ks[2], (H, DK, C), dtype=jnp.float32) / math.sqrt(C)
        w_v = jax.random.normal(ks[3], (H, DV, C), dtype=jnp.float32) / math.sqrt(C)
        w_o = jax.random.normal(ks[4], (H * DV, C), dtype=jnp.float32) / math.sqrt(C)
        return {'x': x, 'w_q': w_q, 'w_k': w_k, 'w_v': w_v, 'w_o': w_o}
    _L0_attn_in = _L0_attn_setup()

    def _L0_ffn_setup():
        import jax, jax.numpy as jnp
        import numpy as np
        DIM = 128
        DEPTH = 2
        HEADS = 8
        DIM_HEAD = 64
        WINDOW = 64
        INNER = HEADS * DIM_HEAD
        HID = int(DIM * 4 * 2 / 3)
        B, N = (2, 1024)
        QK_SCALE = 8.0

        def shift_token(t):
            t1, t2 = jnp.split(t, 2, axis=-1)
            t2 = jnp.pad(t2, ((0, 0), (1, 0), (0, 0)))[:, :-1]
            return jnp.concatenate([t1, t2], axis=-1)

        def l2norm(t):
            return t / jnp.clip(jnp.linalg.norm(t, axis=-1, keepdims=True), 1e-12)

        def rotate_half(x):
            x1, x2 = jnp.split(x, 2, axis=-1)
            return jnp.concatenate([-x2, x1], axis=-1)

        def rotary_xpos(q, k):
            n = q.shape[-2]
            half_idx = jnp.arange(0, DIM_HEAD, 2, dtype=jnp.float32)
            inv_freq = 1.0 / 10000.0 ** (half_idx / DIM_HEAD)
            t = jnp.arange(n, dtype=jnp.float32)
            freqs = t[:, None] * inv_freq[None, :]
            freqs = jnp.concatenate([freqs, freqs], axis=-1)
            base = (half_idx + 0.4 * DIM_HEAD) / (1.4 * DIM_HEAD)
            power = (t - n // 2) / float(WINDOW // 2)
            scale = base[None, :] ** power[:, None]
            scale = jnp.concatenate([scale, scale], axis=-1)
            cos, sin = (jnp.cos(freqs), jnp.sin(freqs))
            q = q * cos * scale + rotate_half(q) * sin * scale
            k = k * cos / scale + rotate_half(k) * sin / scale
            return (q, k)

        def local_attention(q, k, v):
            b, h, n, d = q.shape
            w = n // WINDOW
            bq = q.reshape(b, h, w, WINDOW, d) * QK_SCALE
            bk = k.reshape(b, h, w, WINDOW, d)
            bv = v.reshape(b, h, w, WINDOW, d)

            def look_around(t):
                p = jnp.pad(t, ((0, 0), (0, 0), (1, 0), (0, 0), (0, 0)))
                return jnp.concatenate([p[:, :, :w], p[:, :, 1:]], axis=3)
            bk, bv = (look_around(bk), look_around(bv))
            bt = jnp.arange(n).reshape(w, WINDOW)
            btp = jnp.pad(bt, ((1, 0), (0, 0)), constant_values=-1)
            btk = jnp.concatenate([btp[:w], btp[1:]], axis=1)
            sim = jnp.einsum('bhwid,bhwjd->bhwij', bq, bk)
            i = bt[:, :, None]
            j = btk[:, None, :]
            mask = (i < j) | (i > j + WINDOW) | (j == -1)
            sim = jnp.where(mask, -jnp.finfo(sim.dtype).max, sim)
            attn = jax.nn.softmax(sim, axis=-1)
            out = jnp.einsum('bhwij,bhwjd->bhwid', attn, bv)
            return out.reshape(b, h, n, d)

        def _layer(x, wqkv, qs, ksc, wo, lg, lb, w1, b1, w2, b2):
            b, n, _ = x.shape
            h = shift_token(x)
            qkv = h @ wqkv
            q, k, v = jnp.split(qkv, 3, axis=-1)
            to_heads = lambda t: t.reshape(b, n, HEADS, DIM_HEAD).transpose(0, 2, 1, 3)
            q, k, v = (to_heads(q), to_heads(k), to_heads(v))
            q = l2norm(q) * qs
            k = l2norm(k) * ksc
            q, k = rotary_xpos(q, k)
            o = local_attention(q, k, v)
            o = o.transpose(0, 2, 1, 3).reshape(b, n, INNER)
            x = x + o @ wo
            h = shift_token(x)
            mu = h.mean(-1, keepdims=True)
            var = h.var(-1, keepdims=True)
            h = (h - mu) / jnp.sqrt(var + 1e-05) * lg + lb
            h = h @ w1 + b1
            a, g = jnp.split(h, 2, axis=-1)
            h = a * jax.nn.gelu(g, approximate=False)
            x = x + h @ w2 + b2
            return x
        key = jax.random.key(seed)
        ks = jax.random.split(key, 6)
        return {'x': jax.random.normal(ks[0], (B, N, DIM), jnp.float32), 'wqkv': jax.random.normal(ks[1], (DEPTH, DIM, 3 * INNER), jnp.float32) * 0.02, 'q_scale': jnp.ones((DEPTH, DIM_HEAD), jnp.float32), 'k_scale': jnp.ones((DEPTH, DIM_HEAD), jnp.float32), 'wo': jax.random.normal(ks[2], (DEPTH, INNER, DIM), jnp.float32) * 0.02, 'ln_g': jnp.ones((DEPTH, DIM), jnp.float32), 'ln_b': jnp.zeros((DEPTH, DIM), jnp.float32), 'w1': jax.random.normal(ks[3], (DEPTH, DIM, 2 * HID), jnp.float32) * 0.02, 'b1': jnp.zeros((DEPTH, 2 * HID), jnp.float32), 'w2': jax.random.normal(ks[4], (DEPTH, HID, DIM), jnp.float32) * 0.02, 'b2': jnp.zeros((DEPTH, DIM), jnp.float32)}
    _L0_ffn_in = _L0_ffn_setup()
    _d = {'L0_attn_x': _L0_attn_in['x'], 'L0_attn_w_q': _L0_attn_in['w_q'], 'L0_attn_w_k': _L0_attn_in['w_k'], 'L0_attn_w_v': _L0_attn_in['w_v'], 'L0_attn_w_o': _L0_attn_in['w_o'], 'L0_ffn_wqkv': _L0_ffn_in['wqkv'], 'L0_ffn_q_scale': _L0_ffn_in['q_scale'], 'L0_ffn_k_scale': _L0_ffn_in['k_scale'], 'L0_ffn_wo': _L0_ffn_in['wo'], 'L0_ffn_ln_g': _L0_ffn_in['ln_g'], 'L0_ffn_ln_b': _L0_ffn_in['ln_b'], 'L0_ffn_w1': _L0_ffn_in['w1'], 'L0_ffn_b1': _L0_ffn_in['b1'], 'L0_ffn_w2': _L0_ffn_in['w2'], 'L0_ffn_b2': _L0_ffn_in['b2']}
    _x0 = _d['L0_attn_x']
    _d['L0_attn_x'] = jax.random.normal(jax.random.fold_in(jax.random.key(seed), 1), (8, 512, 128), dtype=_x0.dtype)
    del _x0
    return _d

def reference(L0_attn_x, L0_attn_w_q, L0_attn_w_k, L0_attn_w_v, L0_attn_w_o, L0_ffn_wqkv, L0_ffn_q_scale, L0_ffn_k_scale, L0_ffn_wo, L0_ffn_ln_g, L0_ffn_ln_b, L0_ffn_w1, L0_ffn_b1, L0_ffn_w2, L0_ffn_b2):

    def _L0_attn_ref(x, w_q, w_k, w_v, w_o):
        import jax, jax.numpy as jnp
        import numpy as np
        import math
        B, T, C = (2, 256, 128)
        H, DK, DV = (16, 64, 64)
        dk = w_q.shape[1]
        q = jnp.einsum('ntc,hdc->nhtd', x, w_q)
        k = jnp.einsum('ntc,hdc->nhtd', x, w_k)
        v = jnp.einsum('ntc,hdc->nhtd', x, w_v)
        a = jnp.einsum('nhtd,nhsd->nhts', q, k) / jnp.sqrt(jnp.asarray(dk, x.dtype))
        t = a.shape[-1]
        mask = jnp.arange(t)[:, None] < jnp.arange(t)[None, :]
        a = jnp.where(mask[None, None], jnp.asarray(-jnp.inf, a.dtype), a)
        a = jax.nn.softmax(a, axis=-1)
        y = jnp.einsum('nhts,nhsd->nthd', a, v)
        y = y.reshape(y.shape[0], y.shape[1], -1)
        return y @ w_o

    def _L0_ffn_ref(x, wqkv, q_scale, k_scale, wo, ln_g, ln_b, w1, b1, w2, b2):
        import jax, jax.numpy as jnp
        import numpy as np
        DIM = 128
        DEPTH = 2
        HEADS = 8
        DIM_HEAD = 64
        WINDOW = 64
        INNER = HEADS * DIM_HEAD
        HID = int(DIM * 4 * 2 / 3)
        B, N = (2, 1024)
        QK_SCALE = 8.0

        def shift_token(t):
            t1, t2 = jnp.split(t, 2, axis=-1)
            t2 = jnp.pad(t2, ((0, 0), (1, 0), (0, 0)))[:, :-1]
            return jnp.concatenate([t1, t2], axis=-1)

        def l2norm(t):
            return t / jnp.clip(jnp.linalg.norm(t, axis=-1, keepdims=True), 1e-12)

        def rotate_half(x):
            x1, x2 = jnp.split(x, 2, axis=-1)
            return jnp.concatenate([-x2, x1], axis=-1)

        def rotary_xpos(q, k):
            n = q.shape[-2]
            half_idx = jnp.arange(0, DIM_HEAD, 2, dtype=jnp.float32)
            inv_freq = 1.0 / 10000.0 ** (half_idx / DIM_HEAD)
            t = jnp.arange(n, dtype=jnp.float32)
            freqs = t[:, None] * inv_freq[None, :]
            freqs = jnp.concatenate([freqs, freqs], axis=-1)
            base = (half_idx + 0.4 * DIM_HEAD) / (1.4 * DIM_HEAD)
            power = (t - n // 2) / float(WINDOW // 2)
            scale = base[None, :] ** power[:, None]
            scale = jnp.concatenate([scale, scale], axis=-1)
            cos, sin = (jnp.cos(freqs), jnp.sin(freqs))
            q = q * cos * scale + rotate_half(q) * sin * scale
            k = k * cos / scale + rotate_half(k) * sin / scale
            return (q, k)

        def local_attention(q, k, v):
            b, h, n, d = q.shape
            w = n // WINDOW
            bq = q.reshape(b, h, w, WINDOW, d) * QK_SCALE
            bk = k.reshape(b, h, w, WINDOW, d)
            bv = v.reshape(b, h, w, WINDOW, d)

            def look_around(t):
                p = jnp.pad(t, ((0, 0), (0, 0), (1, 0), (0, 0), (0, 0)))
                return jnp.concatenate([p[:, :, :w], p[:, :, 1:]], axis=3)
            bk, bv = (look_around(bk), look_around(bv))
            bt = jnp.arange(n).reshape(w, WINDOW)
            btp = jnp.pad(bt, ((1, 0), (0, 0)), constant_values=-1)
            btk = jnp.concatenate([btp[:w], btp[1:]], axis=1)
            sim = jnp.einsum('bhwid,bhwjd->bhwij', bq, bk)
            i = bt[:, :, None]
            j = btk[:, None, :]
            mask = (i < j) | (i > j + WINDOW) | (j == -1)
            sim = jnp.where(mask, -jnp.finfo(sim.dtype).max, sim)
            attn = jax.nn.softmax(sim, axis=-1)
            out = jnp.einsum('bhwij,bhwjd->bhwid', attn, bv)
            return out.reshape(b, h, n, d)

        def _layer(x, wqkv, qs, ksc, wo, lg, lb, w1, b1, w2, b2):
            b, n, _ = x.shape
            h = shift_token(x)
            qkv = h @ wqkv
            q, k, v = jnp.split(qkv, 3, axis=-1)
            to_heads = lambda t: t.reshape(b, n, HEADS, DIM_HEAD).transpose(0, 2, 1, 3)
            q, k, v = (to_heads(q), to_heads(k), to_heads(v))
            q = l2norm(q) * qs
            k = l2norm(k) * ksc
            q, k = rotary_xpos(q, k)
            o = local_attention(q, k, v)
            o = o.transpose(0, 2, 1, 3).reshape(b, n, INNER)
            x = x + o @ wo
            h = shift_token(x)
            mu = h.mean(-1, keepdims=True)
            var = h.var(-1, keepdims=True)
            h = (h - mu) / jnp.sqrt(var + 1e-05) * lg + lb
            h = h @ w1 + b1
            a, g = jnp.split(h, 2, axis=-1)
            h = a * jax.nn.gelu(g, approximate=False)
            x = x + h @ w2 + b2
            return x
        for l in range(DEPTH):
            x = _layer(x, wqkv[l], q_scale[l], k_scale[l], wo[l], ln_g[l], ln_b[l], w1[l], b1[l], w2[l], b2[l])
        return x
    x = L0_attn_x
    x = x + _layernorm(_L0_attn_ref(_layernorm(x, axis=-1), L0_attn_w_q, L0_attn_w_k, L0_attn_w_v, L0_attn_w_o), axis=-1)
    x = x + _layernorm(_L0_ffn_ref(_layernorm(x, axis=-1), L0_ffn_wqkv, L0_ffn_q_scale, L0_ffn_k_scale, L0_ffn_wo, L0_ffn_ln_g, L0_ffn_ln_b, L0_ffn_w1, L0_ffn_b1, L0_ffn_w2, L0_ffn_b2), axis=-1)
    return x

_drawn_inputs = setup_inputs


def setup_inputs(seed=0):
    import zlib

    import numpy as np

    out = dict(_drawn_inputs(seed))
    spreads = {'L0_ffn_q_scale': (1.0, 0.6),
     'L0_ffn_k_scale': (1.0, 0.6),
     'L0_ffn_ln_g': (1.0, 0.6),
     'L0_ffn_ln_b': (0.0, 0.8),
     'L0_ffn_b1': (0.0, 0.8),
     'L0_ffn_b2': (0.0, 0.8)}
    factors = {'L0_ffn_w1': 7.538, 'L0_ffn_w2': 7.417}
    for name, (base, spread) in spreads.items():
        noise = np.random.default_rng([zlib.crc32(name.encode()), seed]).standard_normal(out[name].shape)
        drawn = base * np.exp(spread * noise) if base else spread * noise
        out[name] = jnp.asarray(drawn.astype(out[name].dtype))
    for name, factor in factors.items():
        out[name] = (out[name] * factor).astype(out[name].dtype)
    return out
```

```python
from contextlib import ExitStack

import numpy as np

import concourse.bass as bass
from concourse import mybir

F32 = mybir.dt.float32
F32R = mybir.dt.float32r
F16 = mybir.dt.float16
BF16 = mybir.dt.bfloat16
ALU = mybir.AluOpType
ACT = mybir.ActivationFunctionType
AX = mybir.AxisListType

P = 128
BATCH, T, C = 8, 512, 128
NT = T // P
H, DK = 16, 64
PAIRS = H // 2
DEPTH = 2
LH, LD = 8, 64
LPAIRS = LH // 2
INNER = LH * LD
WINDOW = 64
HID = int(C * 4 * 2 / 3)
HC = [(0, 128), (128, 128), (256, HID - 256)]
EPS = 1e-5
MASKED = -1e30

SW = [P * (j + 1) for j in range(NT)]
SO = [sum(SW[:j]) for j in range(NT)]
SCORES = sum(SW)
TG = [[(0, 0), (0, 1), (0, 2), (0, 3)], [(1, 1), (1, 2), (1, 3), (3, 3)], [(2, 2), (2, 3)]]
TO = {blk: 512 * g + P * n for g, blks in enumerate(TG) for n, blk in enumerate(blks)}


class Signal:

    def __init__(self, nc, ctx, name, per, credit=0):
        self.sem, self.per, self.credit = ctx.enter_context(nc.semaphore(name)), per, credit

    def at(self, it, n):
        return it * self.per + (n + self.credit)


class Steps:

    def __init__(self, eng, raised):
        self.eng, self.raised, self.n, self.it = eng, raised, 0, 0

    def start(self, it):
        self.it, self.n = it, 0

    def did(self, ins):
        ins.then_inc(self.raised.sem, 1)
        self.n += 1

    def settle(self):
        self.eng.wait_ge(self.raised.sem, self.raised.at(self.it, self.n))

    def end(self):
        assert self.n == self.raised.per, (self.n, self.raised.per)


def sandwich(nc, x, w_q, w_k, w_v, w_o, wqkv, q_scale, k_scale, wo, ln_g, ln_b, w1, b1, w2, b2,
             ident_c, causal_c, band_c, rope_cos_c, rope_sin_c, out):
    ctx = ExitStack()
    with ctx:
        def sb(name, shape, dt=F32):
            return ctx.enter_context(nc.sbuf_tensor(name, shape, dt))

        def sem(name):
            return ctx.enter_context(nc.semaphore(name))

        def sig(name, per, credit=0):
            return Signal(nc, ctx, name, per, credit)

        bank = [ctx.enter_context(nc.psum_tensor(f"bank{i}", [P, 512], F32)) for i in range(6)]
        wide = ctx.enter_context(nc.psum_tensor("wide", [P, 1024], F32))

        ypart = bank[3]

        x1 = sb("x1", [P, BATCH * NT, C])
        xf = sb("xf", [P, BATCH * NT, C])
        ident = sb("ident", [P, P])
        ident16 = sb("ident16", [P, P], BF16)
        causal = sb("causal", [P, P], BF16)
        band = sb("band", [P, 2, P + WINDOW], BF16)
        rope = sb("rope", [P, 2, NT, 2, LD])
        ropes = sb("ropes", [P, 2, NT, 2, LD])
        qks = sb("qks", [P, 2, 2, LD])
        stage = sb("stage", [P, 4096])

        big = [sb(f"big{n}", [P, 4096], F32R) for n in range(2)]
        mh = [big[0][:, H * C * n:H * C * (n + 1)].rearrange("p (h c) -> p h c", h=H) for n in range(2)]
        wv = [big[1][:, H * DK * n:H * DK * (n + 1)] for n in range(2)]
        wog = [big[1][:, 1024 * (2 + n):1024 * (3 + n)].rearrange("p (g c) -> p g c", g=PAIRS) for n in range(2)]
        wl = [sb(f"wqkv_{s}", [P, 3 * INNER], F32R) for s in ("hi", "lo")]
        wol = [sb(f"wol_{s}", [P, LPAIRS, C], F32R) for s in ("hi", "lo")]
        w1l = [sb(f"w1_{s}", [P, 2 * HID], F32R) for s in ("hi", "lo")]
        w2l = [sb(f"w2_{s}", [P, 3, C], F32R) for s in ("hi", "lo")]
        w1g = sb("w1g", [P, 2 * HID])
        cols = sb("cols", [P, 10])
        b1f = sb("b1f", [P, 6])

        stats = sb("stats", [P, NT, 6])
        mv = sb("mv", [P, NT, 2])
        vare = sb("vare", [P, NT])
        rstd = sb("rstd", [P, NT])
        mhalf = sb("mhalf", [P, 2 * LH])
        xh = sb("xh", [P, NT, C])
        xt = [sb(f"xt_{s}", [P, T], F32R) for s in ("hi", "lo")]
        mid = [sb(f"mid{n}", [P, 2048], F32R) for n in range(2)]
        zt = [mid[0][:, 1024 * n:1024 * n + 1024].rearrange("p (a t) -> p a t", a=2) for n in range(2)]
        negmax = sb("negmax", [P, 2, NT])
        rsum = sb("rsum", [P, 2, 2, NT])
        rinv = sb("rinv", [P, 2, NT])
        yt = [mid[1][:, T * n:T * n + T] for n in range(2)]
        work = sb("work", [P, 4 * SCORES])
        prob = work[:, 0:2 * SCORES].rearrange("p (a n) -> p a n", a=2)
        pt = [work[:, (2 + n) * SCORES:(3 + n) * SCORES].bitcast(F16).rearrange("p (a n) -> p a n", a=2)
              for n in range(2)]
        vv = [sb(f"v_{s}", [P, NT, H * DK], F16) for s in ("hi", "lo")]
        ysb = sb("ysb", [P, 2, NT, 2, DK])
        tail = sb("tail", [P, T])

        xs = xh
        sq, rot_a, rot_b, qk = (work[:, 2 * INNER * n:2 * INNER * (n + 1)] for n in range(4))
        ssq = sb("ssq", [P, 2 * LH])
        ssqc = sb("ssqc", [P, 2 * LH])
        rnorm = sb("rnorm", [P, 2 * LH])
        qt = [sb(f"qt_{s}", [P, LPAIRS, P], F32R) for s in ("hi", "lo")]
        kt = [big[n][:, :].rearrange("p (c e t) -> p c e t", c=LPAIRS, e=2) for n in range(2)]
        vb = [v[:, :, :].rearrange("p t (a c n) -> p (t a) c n", a=2, c=LPAIRS) for v in vv]
        lprob = work[:, 8 * INNER:8 * INNER + 12 * LD].rearrange("p (a m e n) -> p a m e n", a=2, m=3, e=2)
        lpt = [sb(f"lpt_{s}", [P, 2, 3, P], F16) for s in ("hi", "lo")]
        lneg = sb("lneg", [P, 4, 2])
        lsum = sb("lsum", [P, 2, LH])
        linv = sb("linv", [P, LH])
        osb = ysb[:, :, :, :, :].rearrange("p a j e n -> p a (j e n)")
        ot = [mid[n][:, :].rearrange("p (c t) -> p c t", c=LPAIRS) for n in range(2)]

        hs = sb("hs", [P, NT, C])
        gel = prob[:, 0, 0:1024].rearrange("p (a n) -> p a n", a=2)
        ugl = prob[:, 1, 0:1024].rearrange("p (a n) -> p a n", a=2)
        ut = [big[n][:, 0:3 * T].rearrange("p (c t) -> p c t", c=3) for n in range(2)]

        phase, held = sem("phase"), sem("held")
        s_x, s_const, s_weights, s_out = sem("x_loaded"), sem("const_loaded"), sem("weights_loaded"), sem("out_stored")
        s_lw = sem("layer_weights_loaded")
        pre_pe, pre_act, pre_dve, pre_pool = sem("pre_pe"), sem("pre_act"), sem("pre_dve"), sem("pre_pool")
        lay_pe, lay_act, lay_dve = sem("lay_pe"), sem("lay_act"), sem("lay_dve")
        a_step = sig("a_step", 3 * NT * 2 + 2 * NT + PAIRS + 1)
        xh_ready, xt_ps, xt_hi, xt_lo = sig("xh_ready", NT), sig("xt_ps", 1), sig("xt_hi", 1), sig("xt_lo", 1)
        v_ps, v_hi, v_lo = sig("v_ps", 8), sig("v_hi", 8), sig("v_lo", 8)
        z_ps, z_hi, z_lo = sig("z_ps", H), sig("z_hi", H), sig("z_lo", H)
        s_ps, s_max, s_exp = sig("scores_ps", H * NT), sig("scores_max", H * NT), sig("probs_ready", H * NT, H * NT)
        pt_ps, pt_hi, pt_lo = sig("pt_ps", 3 * H), sig("pt_hi", 3 * H), sig("pt_lo", 3 * H, 3 * H)
        y_ps, y_norm = sig("y_ps", PAIRS), sig("y_norm", PAIRS, PAIRS)
        yt_ps, yt_hi, yt_lo = sig("yt_ps", PAIRS), sig("yt_hi", PAIRS), sig("yt_lo", PAIRS)
        a_ps, a_sb, a_back = sig("a_ps", 1), sig("a_sb", 1), sig("a_back", 1)
        b_step = sig("b_step", NT * 5)
        p_step = sig("p_step", 2 * NT)
        bxs, bxt_ps, bh_hi, bh_lo = sig("bxs", 1), sig("bxt_ps", 1), sig("bh_hi", 2), sig("bh_lo", 2)
        bqk_ps, bv_ps, bsq = sig("bqk_ps", NT), sig("bv_ps", NT), sig("bsq", NT)
        brot, bqk = sig("brot", NT), sig("bqk", NT)
        bqt_ps, bqt_hi, bqt_lo = sig("bqt_ps", NT), sig("bqt_hi", 3 * NT), sig("bqt_lo", 3 * NT, 3 * NT)
        bv_hi, bv_lo = sig("bv_hi", 4 * NT), sig("bv_lo", 4 * NT, 4 * NT)
        bs_ps, bmax, bexp = sig("bs_ps", 16), sig("bmax", 16), sig("bexp", 32, 32)
        bpt_ps, bpt_hi, bpt_lo = sig("bpt_ps", 16), sig("bpt_hi", 16), sig("bpt_lo", 16, 16)
        by_ps, by_norm = sig("by_ps", NT), sig("by_norm", NT, NT)
        bot_ps, bot_hi, bot_lo = sig("bot_ps", NT), sig("bot_hi", NT), sig("bot_lo", NT)
        bo_ps, bo_sb, bo_back, bx = sig("bo_ps", 1), sig("bo_sb", 1), sig("bo_back", 1), sig("bx", 1, 1)
        c_step = sig("c_step", NT * 2)
        chs, chs_dma, chn = sig("chs", 1), sig("chs_dma", 32), sig("chn", NT, NT)
        ct_ps, ct_hi, ct_lo = sig("ct_ps", 1), sig("ct_hi", 1), sig("ct_lo", 1)
        cg_ps, ca_ps, cgel, cu = sig("cg_ps", 3), sig("ca_ps", 3), sig("cgel", 3), sig("cu", 3, 3)
        cu_hi, cu_lo = sig("cu_hi", 3), sig("cu_lo", 3)
        co_ps, co_sb, co_back, cx = sig("co_ps", 1), sig("co_sb", 1), sig("co_back", 1), sig("cx", 1, 1)
        d_step, d_out = sig("d_step", 3 * NT), sig("d_out", 1)

        a_root = sig("a_var", 3), sig("a_rstd", 3)
        c_root = sig("c_var", 1), sig("c_rstd", 1)
        d_root = sig("d_var", 1), sig("d_rstd", 1)

        def hold(eng, semaphore, value):
            eng.wait_ge(semaphore, value)
            eng.sem_inc(held, 1)

        def barrier(eng, n):
            eng.drain().then_inc(phase, 1)
            hold(eng, phase, n * 5)

        def layer_norm(dve, steps, src, root, it, k, dst, last):
            for j in range(NT):
                steps.did(dve.bn_stats(stats[:, j, :], src(j)))
            hold(dve, steps.raised.sem, steps.raised.at(steps.it, steps.n))
            for j in range(NT):
                steps.did(dve.bn_aggr(mv[:, j, :], stats[:, j, :]))
            steps.settle()
            dve.tensor_scalar(vare[:, :], mv[:, :, 1], EPS, None, ALU.add).then_inc(root[0].sem, 1)
            dve.wait_ge(root[1].sem, root[1].at(it, k + 1))
            for j in range(NT):
                ins = dve.tensor_scalar(dst(j), src(j), mv[:, j, 0:1], rstd[:, j:j + 1],
                                        ALU.subtract, ALU.mult)
                if last is None:
                    steps.did(ins)
                else:
                    ins.then_inc(last.sem, 1)

        def inverse_root(pool, root, it, k):
            pool.wait_ge(root[0].sem, root[0].at(it, k + 1))
            pool.tensor_tensor(rstd[:, :], vare[:, :], mhalf[:, 0:NT], ALU.pow).then_inc(root[1].sem, 1)

        def three(pe, acc, left, right, start=True, stop=True):
            pe.matmul(acc, left[0], right[0], start=start, stop=False)
            pe.matmul(acc, left[0], right[1], start=False, stop=False)
            return pe.matmul(acc, left[1], right[0], start=False, stop=stop)

        def cut(pair, f):
            return [f(t) for t in pair]

        block = ctx.enter_context(nc.Block())

        raw_q = stage[0:DK, 0:H * C].rearrange("d (h c) -> d h c", h=H)
        raw_k = stage[0:DK, H * C:2 * H * C].rearrange("d (h c) -> d h c", h=H)
        raw_v = sq[:, :].rearrange("p (g c) -> p g c", g=PAIRS)
        raw_o = rot_a[:, :].rearrange("p (g c) -> p g c", g=PAIRS)
        raw_causal, raw_band = rot_b[:, 0:P], rot_b[:, P:P + 2 * (P + WINDOW)]
        raw_qkv = stage[:, 0:3 * INNER]
        raw_wo = stage[:, 1536:2048].rearrange("p (g c) -> p g c", g=LPAIRS)
        raw_w1 = stage[:, 2048:2048 + 2 * HID]
        raw_w2 = stage[:, 2816:2816 + 3 * C].rearrange("p (g c) -> p g c", g=3)

        @block.sync
        def _(sp):
            sp.dma_start(ident[:, :], ident_c).then_inc(s_const, 16)
            sp.dma_start(raw_q, w_q.rearrange("h d c -> d h c")).then_inc(s_weights, 16)
            sp.dma_start(raw_k, w_k.rearrange("h d c -> d h c")).then_inc(s_weights, 16)
            sp.dma_start(raw_v, w_v.rearrange("(g a) d c -> (a d) g c", a=2)).then_inc(s_weights, 16)
            sp.dma_start(raw_o, w_o.rearrange("(g p) c -> p g c", p=P)).then_inc(s_weights, 16)
            sp.dma_start(raw_causal, causal_c).then_inc(s_const, 16)
            sp.dma_start(raw_band, band_c).then_inc(s_const, 16)
            sp.dma_start(x1[:, :, :], x.rearrange("b (j p) c -> p (b j) c", p=P)).then_inc(s_x, 16)
            sp.dma_start(rope[:, 0, :, :, :], rope_cos_c.rearrange("(j p) a d -> p j a d", p=P)).then_inc(s_const, 16)
            sp.dma_start(rope[:, 1, :, :, :], rope_sin_c.rearrange("(j p) a d -> p j a d", p=P)).then_inc(s_const, 16)
            barrier(sp, 1)
            barrier(sp, 2)
            with sp.Fori(0, DEPTH) as l:
                def layer(w, pattern="o a b -> (o a) b", **kw):
                    return w[bass.ds(l, 1)].rearrange(pattern, **kw)
                sp.dma_start(raw_qkv, layer(wqkv)).then_inc(s_lw, 16)
                sp.dma_start(raw_wo, layer(wo, "o (g p) c -> p (o g) c", p=P)).then_inc(s_lw, 16)
                sp.dma_start(raw_w1, layer(w1)).then_inc(s_lw, 16)
                for n, (r0, rows) in enumerate(HC):
                    sp.dma_start(raw_w2[0:rows, n, :], layer(w2)[r0:r0 + rows, :]).then_inc(s_lw, 16)
                for n, v in enumerate((ln_g, ln_b, b2)):
                    sp.dma_start(cols[:, n:n + 1], layer(v, "o (c k) -> (o c) k", k=1)).then_inc(s_lw, 16)
                for n in range(6):
                    r0, rows = HC[n % 3]
                    r0 += HID * (n // 3)
                    sp.dma_start(cols[0:rows, 3 + n:4 + n],
                                 layer(b1, "o (c k) -> (o c) k", k=1)[r0:r0 + rows, :]).then_inc(s_lw, 16)
                for n, v in enumerate((q_scale, k_scale)):
                    row = v[bass.ds(l, 1), :]
                    sp.dma_start(qks[:, 0, n, :], row.to_broadcast([P, LD])).then_inc(s_lw, 16)
                    sp.dma_start(qks[:, 1, n, 0:LD // 2], row[:, LD // 2:].to_broadcast([P, LD // 2])).then_inc(s_lw, 16)
                    sp.dma_start(qks[:, 1, n, LD // 2:], row[:, 0:LD // 2].to_broadcast([P, LD // 2])).then_inc(s_lw, 16)
                barrier(sp, l * 3 + 3)
                barrier(sp, l * 3 + 4)
                with sp.Fori(0, BATCH) as b:
                    it = l * BATCH + b
                    sp.wait_ge(chn.sem, chn.at(it, 0))
                    sp.dma_start(hs[1:P, :, C // 2:], xf[0:P - 1, bass.ds(b * NT, NT), C // 2:]).then_inc(chs_dma.sem, 16)
                    sp.dma_start(hs[0:1, 1:NT, C // 2:], xf[P - 1:P, bass.ds(b * NT, NT - 1), C // 2:]).then_inc(chs_dma.sem, 16)
                barrier(sp, l * 3 + 5)
            with sp.Fori(0, BATCH) as b:
                sp.wait_ge(d_out.sem, d_out.at(b, 1))
                sp.dma_start(out[bass.ds(b, 1)].rearrange("o (j p) c -> p (o j) c", p=P),
                             x1[:, bass.ds(b * NT, NT), :]).then_inc(s_out, 16)
            sp.wait_ge(s_out, 16 * BATCH)

        @block.gpsimd
        def _(pool):
            pool.memset(hs[0:1, 0:1, C // 2:], 0.0).then_inc(pre_pool, 1)
            pool.memset(mhalf[:, :], -0.5).then_inc(pre_pool, 1)
            barrier(pool, 1)
            with pool.Fori(0, BATCH) as b:
                for k in range(3):
                    inverse_root(pool, a_root, b, k)
            barrier(pool, 2)
            steps = Steps(pool, p_step)
            with pool.Fori(0, DEPTH) as l:
                for t in kt:
                    z = t[:, :, :, :].bitcast(F32)
                    pool.memset(z[0:DK, :, 1, :], 0.0).then_inc(pre_pool, 1)
                    pool.memset(z[DK:P, :, 0, :], 0.0).then_inc(pre_pool, 1)
                for t in xt:
                    pool.memset(t[DK:P, 0:1].bitcast(F32), 0.0).then_inc(pre_pool, 1)
                for t in vb:
                    pool.memset(t[0:DK, :, :, DK:P], 0.0).then_inc(pre_pool, 1)
                    pool.memset(t[DK:P, :, :, 0:DK], 0.0).then_inc(pre_pool, 1)
                barrier(pool, l * 3 + 3)
                with pool.Fori(0, BATCH) as b:
                    it = l * BATCH + b
                    pool.tensor_copy(xs[:, :, :], xf[:, bass.ds(b * NT, NT), :]).then_inc(bxs.sem, 1)
                    steps.start(it)
                    for j in range(NT):
                        pool.wait_ge(brot.sem, brot.at(it, j + 1))
                        steps.did(pool.tensor_tensor(rnorm[:, :], ssqc[:, :], mhalf[:, :], ALU.pow))
                        steps.did(pool.tensor_tensor(qk[:, :], rot_a[:, :], rot_b[:, :], ALU.add))
                        steps.settle()
                        v = qk[:, :].rearrange("p (h d) -> p h d", d=LD)
                        pool.tensor_tensor(v, v, rnorm[:, :, None].to_broadcast([P, 2 * LH, LD]),
                                           ALU.mult).then_inc(bqk.sem, 1)
                    steps.end()
                barrier(pool, l * 3 + 4)
                with pool.Fori(0, BATCH) as b:
                    it = l * BATCH + b
                    pool.wait_ge(chn.sem, chn.at(it, 0))
                    pool.tensor_copy(hs[:, :, 0:C // 2], xf[:, bass.ds(b * NT, NT), 0:C // 2]).then_inc(chs.sem, 1)
                    inverse_root(pool, c_root, it, 0)
                    for n in range(3):
                        rows = HC[n][1]
                        pool.wait_ge(cu_hi.sem, cu_hi.at(it, n + 1))
                        pool.tensor_tensor(ut[1][0:rows, n, :], ugl[0:rows, n % 2, :],
                                           ut[0][0:rows, n, :].bitcast(F32), ALU.subtract).then_inc(cu_lo.sem, 1)
                barrier(pool, l * 3 + 5)
            with pool.Fori(0, BATCH) as b:
                inverse_root(pool, d_root, b, 0)

        @block.scalar
        def _(act):
            def copy(dst, src):
                return act.activation(dst, src, ACT.Copy)

            act.wait_ge(s_const, 80)
            act.wait_ge(s_weights, 64)
            copy(ident16[:, :], ident[:, :]).then_inc(pre_act, 1)
            copy(causal[:, :], raw_causal).then_inc(pre_act, 1)
            copy(band[:, :, :].rearrange("p a n -> p (a n)"), raw_band).then_inc(pre_act, 1)
            copy(wog[0][:, :, :], raw_o).then_inc(pre_act, 1)
            for n in range(4):
                act.wait_ge(pre_pe, n + 1)
                act.activation(mh[0][:, 4 * n:4 * n + 4, :].rearrange("p h c -> p (h c)"), bank[n][:, :],
                               ACT.Copy, scale=DK ** -0.5).then_inc(pre_act, 1)
            for n in range(2):
                act.wait_ge(pre_pe, n + 5)
                copy(wv[0][:, 512 * n:512 * n + 512], bank[4 + n][:, :]).then_inc(pre_act, 1)
            barrier(act, 1)

            def a_exp(b, h, j):
                n = h * NT + j
                act.wait_ge(s_max.sem, s_max.at(b, n + 1))
                act.activation(prob[:, h % 2, SO[j]:SO[j] + SW[j]], bank[n % 3][:, 0:SW[j]], ACT.Exp,
                               bias=negmax[:, h % 2, j:j + 1],
                               accum_out=rsum[:, h // 2 % 2, h % 2, j:j + 1]).then_inc(s_exp.sem, 1)

            def a_pt(b, h, g):
                n = 3 * h + g
                w = P * len(TG[g])
                act.wait_ge(pt_ps.sem, pt_ps.at(b, n + 1))
                copy(pt[0][:, h % 2, 512 * g:512 * g + w], bank[3 + n % 2][:, 0:w]).then_inc(pt_hi.sem, 1)

            def a_z(b, h):
                act.wait_ge(z_ps.sem, z_ps.at(b, h + 1))
                copy(zt[0][:, h % 2, :], bank[5][:, :]).then_inc(z_hi.sem, 1)

            def a_yt(b, p):
                act.wait_ge(yt_ps.sem, yt_ps.at(b, p + 1))
                copy(yt[0][:, :], bank[5][:, :]).then_inc(yt_hi.sem, 1)

            act.sem_inc(s_exp.sem, s_exp.credit)
            with act.Fori(0, BATCH) as b:
                act.wait_ge(xt_ps.sem, xt_ps.at(b, 1))
                copy(xt[0][:, :], bank[5][:, :]).then_inc(xt_hi.sem, 1)
                for g in range(8):
                    act.wait_ge(v_ps.sem, v_ps.at(b, g + 1))
                    copy(vv[0][:, g // 2, 512 * (g % 2):512 * (g % 2) + 512], bank[g % 3][:, :]).then_inc(v_hi.sem, 1)
                a_z(b, 0)
                for h in range(H + 1):
                    if h + 1 < H:
                        a_z(b, h + 1)
                    for g in range(3):
                        if h < H:
                            a_exp(b, h, g)
                        if h >= 1:
                            a_pt(b, h - 1, g)
                    if h < H:
                        a_exp(b, h, 3)
                    if h >= 3 and h % 2:
                        a_yt(b, (h - 3) // 2)
                a_yt(b, PAIRS - 1)
                act.wait_ge(a_ps.sem, a_ps.at(b, 1))
                copy(tail[:, :], wide[:, 512:1024]).then_inc(a_sb.sem, 1)
            barrier(act, 2)

            def b_exp(it, j, p):
                q = j * LPAIRS + p
                act.wait_ge(bmax.sem, bmax.at(it, q + 1))
                m0 = 1 if j == 0 else 0
                w = LD * (3 - m0)
                for e in range(2):
                    act.activation(lprob[:, q % 2, m0:3, e, :],
                                   bank[q % 2][:, e * w:(e + 1) * w].rearrange("p (m n) -> p m n", n=LD), ACT.Exp,
                                   bias=lneg[:, q % 4, e:e + 1],
                                   accum_out=lsum[:, j % 2, 2 * p + e:2 * p + e + 1]).then_inc(bexp.sem, 1)

            def b_pt(it, j, p):
                q = j * LPAIRS + p
                m0 = 1 if j == 0 else 0
                act.wait_ge(bpt_ps.sem, bpt_ps.at(it, q + 1))
                copy(lpt[0][:, q % 2, m0:3, :].rearrange("p m n -> p (m n)"),
                     bank[2][:, m0 * P:3 * P]).then_inc(bpt_hi.sem, 1)

            def b_sq(it, j):
                act.wait_ge(bqk_ps.sem, bqk_ps.at(it, j + 1))
                act.activation(sq[:, :], wide[:, :], ACT.Square).then_inc(bsq.sem, 1)

            def b_v(it, j):
                act.wait_ge(bv_ps.sem, bv_ps.at(it, j + 1))
                vp = bank[4][:, :].rearrange("p (c e n) -> p c e n", c=LPAIRS, e=2)
                for r in range(2):
                    for e in range(2):
                        copy(vb[0][DK * e:DK * e + DK, 2 * j + r, :, DK * e:DK * e + DK],
                             vp[DK * r:DK * r + DK, :, e, :]).then_inc(bv_hi.sem, 1)

            def b_qt(it, j):
                act.wait_ge(bqt_ps.sem, bqt_ps.at(it, j + 1))
                copy(qt[0][:, :, :].rearrange("p c n -> p (c n)"), wide[:, 0:512]).then_inc(bqt_hi.sem, 1)
                for e in range(2):
                    copy(kt[0][DK * e:DK * e + DK, :, e, P * j:P * j + P],
                         wide[DK * e:DK * e + DK, 512:1024].rearrange("p (c n) -> p c n", c=LPAIRS)).then_inc(bqt_hi.sem, 1)

            def b_ot(it, j):
                act.wait_ge(bot_ps.sem, bot_ps.at(it, j + 1))
                copy(ot[0][:, :, P * j:P * j + P], bank[5][:, :].rearrange("p (c n) -> p c n", c=LPAIRS)).then_inc(bot_hi.sem, 1)

            act.sem_inc(bexp.sem, bexp.credit)
            with act.Fori(0, DEPTH) as l:
                act.wait_ge(s_lw, (l + 1) * 16 * 21)
                copy(wl[0][:, :], raw_qkv).then_inc(lay_act, 1)
                copy(wol[0][:, :, :], raw_wo).then_inc(lay_act, 1)
                copy(w2l[0][:, 0:2, :], raw_w2[:, 0:2, :]).then_inc(lay_act, 1)
                copy(w2l[0][0:HC[2][1], 2, :], raw_w2[0:HC[2][1], 2, :]).then_inc(lay_act, 1)
                act.wait_ge(lay_dve, l * 16 + 1)
                copy(w1l[0][:, :], w1g[:, :]).then_inc(lay_act, 1)
                barrier(act, l * 3 + 3)
                with act.Fori(0, BATCH) as b:
                    it = l * BATCH + b
                    act.wait_ge(bxt_ps.sem, bxt_ps.at(it, 1))
                    copy(xt[0][0:DK, :], bank[5][0:DK, :]).then_inc(bh_hi.sem, 1)
                    copy(xt[0][DK:P, 1:T], bank[5][DK:P, 0:T - 1]).then_inc(bh_hi.sem, 1)
                    b_sq(it, 0)
                    b_v(it, 0)
                    for j in range(NT):
                        b_qt(it, j)
                        b_exp(it, j, 0)
                        if j + 1 < NT:
                            b_sq(it, j + 1)
                            b_v(it, j + 1)
                        b_exp(it, j, 1)
                        b_pt(it, j, 0)
                        if j:
                            b_ot(it, j - 1)
                        b_exp(it, j, 2)
                        b_pt(it, j, 1)
                        b_exp(it, j, 3)
                        b_pt(it, j, 2)
                        b_pt(it, j, 3)
                    b_ot(it, NT - 1)
                    act.wait_ge(bo_ps.sem, bo_ps.at(it, 1))
                    copy(tail[:, :], bank[5][:, :]).then_inc(bo_sb.sem, 1)
                barrier(act, l * 3 + 4)
                with act.Fori(0, BATCH) as b:
                    it = l * BATCH + b
                    act.wait_ge(ct_ps.sem, ct_ps.at(it, 1))
                    copy(xt[0][:, :], bank[5][:, :]).then_inc(ct_hi.sem, 1)

                    def c_uhi(n):
                        rows = HC[n][1]
                        act.wait_ge(cu.sem, cu.at(it, n + 1))
                        copy(ut[0][0:rows, n, :], ugl[0:rows, n % 2, :]).then_inc(cu_hi.sem, 1)

                    for n in range(3):
                        rows = HC[n][1]
                        act.wait_ge(cg_ps.sem, cg_ps.at(it, n + 1))
                        act.activation(gel[0:rows, n % 2, :], bank[n % 2][0:rows, :], ACT.Gelu,
                                       bias=b1f[0:rows, 3 + n:4 + n]).then_inc(cgel.sem, 1)
                        if n:
                            c_uhi(n - 1)
                    c_uhi(2)
                    act.wait_ge(co_ps.sem, co_ps.at(it, 1))
                    act.activation(tail[:, :], bank[4][:, :], ACT.Identity, bias=cols[:, 2:3]).then_inc(co_sb.sem, 1)
                barrier(act, l * 3 + 5)

        @block.vector
        def _(dve):
            dve.wait_ge(s_const, 80)
            dve.wait_ge(s_weights, 64)
            dve.wait_ge(pre_act, 4)
            dve.tensor_tensor(wog[1][:, :, :], raw_o, wog[0][:, :, :].bitcast(F32), ALU.subtract).then_inc(pre_dve, 1)
            for n in range(4):
                dve.wait_ge(pre_act, n + 5)
                dve.scalar_tensor_tensor(mh[1][:, 4 * n:4 * n + 4, :].rearrange("p h c -> p (h c)"), bank[n][:, :],
                                         DK ** -0.5, mh[0][:, 4 * n:4 * n + 4, :].rearrange("p h c -> p (h c)").bitcast(F32),
                                         ALU.mult, ALU.subtract).then_inc(pre_dve, 1)
            for n in range(2):
                dve.wait_ge(pre_act, n + 9)
                dve.tensor_tensor(wv[1][:, 512 * n:512 * n + 512], bank[4 + n][:, :],
                                  wv[0][:, 512 * n:512 * n + 512].bitcast(F32), ALU.subtract).then_inc(pre_dve, 1)
            dve.wait_ge(s_x, 16)
            barrier(dve, 1)

            def low(dst, full, high):
                return dve.tensor_tensor(dst, full, high.bitcast(F32) if high.dtype == F32R else high, ALU.subtract)

            def a_max(b, h, j):
                n = h * NT + j
                dve.wait_ge(s_ps.sem, s_ps.at(b, n + 1))
                dve.tensor_reduce(negmax[:, h % 2, j:j + 1], bank[n % 3][:, 0:SW[j]], AX.X, ALU.max,
                                  negate=True).then_inc(s_max.sem, 1)

            def a_pt(b, h, g):
                n = 3 * h + g
                w = P * len(TG[g])
                dve.wait_ge(pt_hi.sem, pt_hi.at(b, n + 1))
                low(pt[1][:, h % 2, 512 * g:512 * g + w], bank[3 + n % 2][:, 0:w],
                    pt[0][:, h % 2, 512 * g:512 * g + w]).then_inc(pt_lo.sem, 1)

            def a_z(b, h):
                dve.wait_ge(z_hi.sem, z_hi.at(b, h + 1))
                low(zt[1][:, h % 2, :], bank[5][:, :], zt[0][:, h % 2, :]).then_inc(z_lo.sem, 1)

            def a_norm(b, p, steps):
                dve.wait_ge(y_ps.sem, y_ps.at(b, p + 1))
                steps.did(dve.reciprocal(rinv[:, :, :], rsum[:, p % 2, :, :]))
                steps.settle()
                dve.tensor_tensor(ysb[:, p % 2, :, :, :].rearrange("p j e n -> p e j n"),
                                  wide[:, 0:512].rearrange("p (e j n) -> p e j n", e=2, j=NT),
                                  rinv[:, :, :, None].to_broadcast([P, 2, NT, DK]), ALU.mult).then_inc(y_norm.sem, 1)

            def a_yt(b, p):
                dve.wait_ge(yt_hi.sem, yt_hi.at(b, p + 1))
                low(yt[1][:, :], bank[5][:, :], yt[0][:, :]).then_inc(yt_lo.sem, 1)

            dve.sem_inc(pt_lo.sem, pt_lo.credit)
            dve.sem_inc(y_norm.sem, y_norm.credit)
            steps = Steps(dve, a_step)
            with dve.Fori(0, BATCH) as b:
                steps.start(b)
                here = bass.ds(b * NT, NT)

                def tile_of(t):
                    return lambda j: t[:, bass.ds(b * NT + j, 1), :].rearrange("p o c -> p (o c)")

                layer_norm(dve, steps, tile_of(x1), a_root, b, 0, lambda j: xh[:, j, :], xh_ready)
                dve.wait_ge(xt_hi.sem, xt_hi.at(b, 1))
                low(xt[1][:, :], bank[5][:, :], xt[0][:, :]).then_inc(xt_lo.sem, 1)
                for g in range(8):
                    dve.wait_ge(v_hi.sem, v_hi.at(b, g + 1))
                    v = [t[:, g // 2, 512 * (g % 2):512 * (g % 2) + 512] for t in vv]
                    low(v[1], bank[g % 3][:, :], v[0]).then_inc(v_lo.sem, 1)
                a_z(b, 0)
                for h in range(H + 1):
                    if h + 1 < H:
                        a_z(b, h + 1)
                    for g in range(3):
                        if h < H:
                            a_max(b, h, g)
                    for g in range(3):
                        if h >= 1:
                            a_pt(b, h - 1, g)
                    if h < H:
                        a_max(b, h, 3)
                    if h >= 3 and h % 2:
                        a_yt(b, (h - 3) // 2)
                    if h >= 2 and h % 2 == 0:
                        a_norm(b, h // 2 - 1, steps)
                a_yt(b, PAIRS - 1)
                hold(dve, a_back.sem, a_back.at(b, 1))
                back = bank[5][:, :].rearrange("p (j c) -> p j c", j=NT)
                layer_norm(dve, steps, lambda j: back[:, j, :], a_root, b, 1, lambda j: xh[:, j, :], None)
                steps.settle()
                steps.did(dve.tensor_tensor(x1[:, here, :], x1[:, here, :], xh[:, :, :], ALU.add))
                hold(dve, steps.raised.sem, steps.raised.at(steps.it, steps.n))
                layer_norm(dve, steps, tile_of(x1), a_root, b, 2, tile_of(xf), None)
                steps.settle()
                steps.end()
            barrier(dve, 2)

            def b_rot(it, j, steps):
                dve.wait_ge(bsq.sem, bsq.at(it, j + 1))
                steps.did(dve.tensor_reduce(ssq[:, :], sq[:, :].rearrange("p (h d) -> p h d", d=LD), AX.X, ALU.add))
                steps.settle()
                steps.did(dve.tensor_scalar(ssqc[:, :], ssq[:, :], 1e-24, None, ALU.max))
                src = wide[:, :].rearrange("p (a h d) -> p a h d", a=2, h=LH)
                ra = rot_a[:, :].rearrange("p (a h d) -> p a h d", a=2, h=LH)
                rb = rot_b[:, :].rearrange("p (a h d) -> p a h d", a=2, h=LH)

                def table(f, lo, hi):
                    return ropes[:, f, j, :, None, lo:hi].to_broadcast([P, 2, LH, hi - lo])

                half = LD // 2
                steps.did(dve.tensor_tensor(ra, src, table(0, 0, LD), ALU.mult))
                steps.did(dve.tensor_tensor(rb[:, :, :, 0:half], src[:, :, :, half:LD], table(1, 0, half), ALU.mult))
                dve.wait_ge(b_step.sem, b_step.at(it, steps.n))
                dve.tensor_tensor(rb[:, :, :, half:LD], src[:, :, :, 0:half], table(1, half, LD), ALU.mult).then_inc(brot.sem, 1)

            def b_max(it, j, p):
                q = j * LPAIRS + p
                w = P if j == 0 else P + WINDOW
                dve.wait_ge(bs_ps.sem, bs_ps.at(it, q + 1))
                dve.tensor_reduce(lneg[:, q % 4, :], bank[q % 2][:, 0:2 * w].rearrange("p (e n) -> p e n", e=2),
                                  AX.X, ALU.max, negate=True).then_inc(bmax.sem, 1)

            def b_pt(it, j, p):
                q = j * LPAIRS + p
                m0 = 1 if j == 0 else 0
                dve.wait_ge(bpt_hi.sem, bpt_hi.at(it, q + 1))
                v = [t[:, q % 2, m0:3, :].rearrange("p m n -> p (m n)") for t in lpt]
                low(v[1], bank[2][:, m0 * P:3 * P], v[0]).then_inc(bpt_lo.sem, 1)

            def b_v(it, j):
                dve.wait_ge(bv_hi.sem, bv_hi.at(it, 4 * j + 4))
                vp = bank[4][:, :].rearrange("p (c e n) -> p c e n", c=LPAIRS, e=2)
                for r in range(2):
                    for e in range(2):
                        v = [t[DK * e:DK * e + DK, 2 * j + r, :, DK * e:DK * e + DK] for t in vb]
                        low(v[1], vp[DK * r:DK * r + DK, :, e, :], v[0]).then_inc(bv_lo.sem, 1)

            def b_qt(it, j):
                dve.wait_ge(bqt_hi.sem, bqt_hi.at(it, 3 * j + 3))
                q = [t[:, :, :].rearrange("p c n -> p (c n)") for t in qt]
                low(q[1], wide[:, 0:512], q[0]).then_inc(bqt_lo.sem, 1)
                for e in range(2):
                    k = [t[DK * e:DK * e + DK, :, e, P * j:P * j + P] for t in kt]
                    low(k[1], wide[DK * e:DK * e + DK, 512:1024].rearrange("p (c n) -> p c n", c=LPAIRS), k[0]).then_inc(bqt_lo.sem, 1)

            def b_ot(it, j):
                dve.wait_ge(bot_hi.sem, bot_hi.at(it, j + 1))
                o = [t[:, :, P * j:P * j + P] for t in ot]
                low(o[1], bank[5][:, :].rearrange("p (c n) -> p c n", c=LPAIRS), o[0]).then_inc(bot_lo.sem, 1)

            def b_norm(it, j, steps):
                dve.wait_ge(by_ps.sem, by_ps.at(it, j + 1))
                steps.did(dve.reciprocal(linv[:, :], lsum[:, j % 2, :]))
                steps.settle()
                dve.tensor_tensor(osb[:, j % 2, :].rearrange("p (h d) -> p h d", d=LD),
                                  ypart[:, :].rearrange("p (h d) -> p h d", d=LD),
                                  linv[:, :, None].to_broadcast([P, LH, LD]), ALU.mult).then_inc(by_norm.sem, 1)

            for s in (bqt_lo, bv_lo, bpt_lo, by_norm, bx, chn, cu, cx):
                dve.sem_inc(s.sem, s.credit)
            bsteps, csteps, dsteps = Steps(dve, b_step), Steps(dve, c_step), Steps(dve, d_step)
            with dve.Fori(0, DEPTH) as l:
                dve.wait_ge(s_lw, (l + 1) * 16 * 21)
                dve.tensor_scalar(w1g[:, :], raw_w1, cols[:, 0:1], None, ALU.mult).then_inc(lay_dve, 1)
                n = 1
                for f in range(2):
                    for j in range(NT):
                        dve.tensor_tensor(ropes[:, f, j, :, :], rope[:, f, j, :, :], qks[:, f, :, :], ALU.mult).then_inc(lay_dve, 1)
                        n += 1
                for k, (full, pair) in enumerate(((raw_qkv, cut(wl, lambda t: t[:, :])),
                                                  (raw_wo, cut(wol, lambda t: t[:, :, :])),
                                                  (raw_w2[:, 0:2, :], cut(w2l, lambda t: t[:, 0:2, :])),
                                                  (raw_w2[0:HC[2][1], 2, :], cut(w2l, lambda t: t[0:HC[2][1], 2, :])),
                                                  (w1g[:, :], cut(w1l, lambda t: t[:, :])))):
                    dve.wait_ge(lay_act, l * 5 + (k + 1))
                    low(pair[1], full, pair[0]).then_inc(lay_dve, 1)
                    n += 1
                dve.wait_ge(lay_pe, l + 1)
                for c0, r in ((0, P), (2, HC[2][1])):
                    w = 2 if c0 == 0 else 1
                    dve.tensor_tensor(b1f[0:r, :].rearrange("p (a c) -> p a c", a=2)[:, :, c0:c0 + w],
                                      bank[0][0:r, 0:6].rearrange("p (a c) -> p a c", a=2)[:, :, c0:c0 + w],
                                      cols[0:r, 3:9].rearrange("p (a c) -> p a c", a=2)[:, :, c0:c0 + w],
                                      ALU.add).then_inc(lay_dve, 1)
                    n += 1
                assert n == 16
                barrier(dve, l * 3 + 3)
                with dve.Fori(0, BATCH) as b:
                    it = l * BATCH + b
                    bsteps.start(it)
                    here = bass.ds(b * NT, NT)
                    dve.wait_ge(bh_hi.sem, bh_hi.at(it, 2))
                    low(xt[1][0:DK, :], bank[5][0:DK, :], xt[0][0:DK, :]).then_inc(bh_lo.sem, 1)
                    low(xt[1][DK:P, 1:T], bank[5][DK:P, 0:T - 1], xt[0][DK:P, 1:T]).then_inc(bh_lo.sem, 1)
                    b_rot(it, 0, bsteps)
                    b_v(it, 0)
                    for j in range(NT):
                        b_qt(it, j)
                        b_max(it, j, 0)
                        if j + 1 < NT:
                            b_rot(it, j + 1, bsteps)
                            b_v(it, j + 1)
                        b_max(it, j, 1)
                        b_pt(it, j, 0)
                        if j:
                            b_ot(it, j - 1)
                        b_max(it, j, 2)
                        b_pt(it, j, 1)
                        b_max(it, j, 3)
                        b_pt(it, j, 2)
                        b_pt(it, j, 3)
                        b_norm(it, j, bsteps)
                    b_ot(it, NT - 1)
                    dve.wait_ge(bo_back.sem, bo_back.at(it, 1))
                    dve.tensor_tensor(xf[:, here, :], bank[5][:, :].rearrange("p (j c) -> p j c", j=NT),
                                      xf[:, here, :], ALU.add).then_inc(bx.sem, 1)
                    bsteps.end()
                barrier(dve, l * 3 + 4)
                with dve.Fori(0, BATCH) as b:
                    it = l * BATCH + b
                    csteps.start(it)
                    here = bass.ds(b * NT, NT)
                    dve.wait_ge(chs.sem, chs.at(it, 1))
                    hold(dve, chs_dma.sem, chs_dma.at(it, 32))
                    layer_norm(dve, csteps, lambda j: hs[:, j, :], c_root, it, 0, lambda j: xh[:, j, :], chn)
                    csteps.end()
                    dve.wait_ge(ct_hi.sem, ct_hi.at(it, 1))
                    low(xt[1][:, :], bank[5][:, :], xt[0][:, :]).then_inc(ct_lo.sem, 1)
                    for n in range(3):
                        rows = HC[n][1]
                        dve.wait_ge(cgel.sem, cgel.at(it, n + 1))
                        dve.wait_ge(ca_ps.sem, ca_ps.at(it, n + 1))
                        if n == 2:
                            dve.wait_ge(cu_lo.sem, cu_lo.at(it, 1))
                        dve.scalar_tensor_tensor(ugl[0:rows, n % 2, :], bank[2 + n % 2][0:rows, :], b1f[0:rows, n:n + 1],
                                                 gel[0:rows, n % 2, :], ALU.add, ALU.mult).then_inc(cu.sem, 1)
                    dve.wait_ge(co_back.sem, co_back.at(it, 1))
                    dve.tensor_tensor(xf[:, here, :], bank[5][:, :].rearrange("p (j c) -> p j c", j=NT),
                                      xf[:, here, :], ALU.add).then_inc(cx.sem, 1)
                barrier(dve, l * 3 + 5)
            with dve.Fori(0, BATCH) as b:
                dsteps.start(b)
                here = bass.ds(b * NT, NT)
                layer_norm(dve, dsteps, lambda j: xf[:, bass.ds(b * NT + j, 1), :].rearrange("p o c -> p (o c)"), d_root, b, 0,
                           lambda j: xh[:, j, :], None)
                dsteps.settle()
                dsteps.end()
                dve.tensor_tensor(x1[:, here, :], x1[:, here, :], xh[:, :, :], ALU.add).then_inc(d_out.sem, 1)
                dve.wait_ge(d_out.sem, d_out.at(b, 1))

        @block.tensor
        def _(pe):
            pe.wait_ge(s_const, 80)
            pe.wait_ge(s_weights, 64)
            for n in range(4):
                for k in range(4):
                    h = 4 * n + k
                    mm = pe.matmul(bank[n][:, P * k:P * k + P], raw_q[:, h, :], raw_k[:, h, :], start=True, stop=True)
                mm.then_inc(pre_pe, 1)
            for n in range(2):
                for k in range(4):
                    mm = pe.transpose(bank[4 + n][:, P * k:P * k + P], raw_v[:, 4 * n + k, :], ident[:, :])
                mm.then_inc(pre_pe, 1)
            barrier(pe, 1)

            def a_z(b, h, first_free):
                pe.wait_ge(*first_free)
                three(pe, bank[5][:, :], cut(mh, lambda t: t[:, h, :]), cut(xt, lambda t: t[:, :])).then_inc(z_ps.sem, 1)

            def a_scores(b, h, j):
                n = h * NT + j
                if n >= 3:
                    pe.wait_ge(s_exp.sem, s_exp.at(b, n - 2))
                if j == 0:
                    pe.wait_ge(z_lo.sem, z_lo.at(b, h + 1))
                acc = bank[n % 3]
                z = cut(zt, lambda t: t[:, h % 2, P * j:P * j + P])
                three(pe, acc[:, 0:SW[j]], z, cut(xt, lambda t: t[:, 0:SW[j]]), stop=False)
                pe.matmul(acc[:, SW[j] - P:SW[j]], ident16[:, :], causal[:, :], start=False, stop=True).then_inc(s_ps.sem, 1)

            def a_turn(b, h, g):
                n = 3 * h + g
                if g == 0:
                    pe.wait_ge(s_exp.sem, s_exp.at(b, NT * (h + 1)))
                pe.wait_ge(pt_lo.sem, pt_lo.at(b, n - 1))
                for k, (i, j) in enumerate(TG[g]):
                    mm = pe.transpose(bank[3 + n % 2][:, P * k:P * k + P],
                                      prob[:, h % 2, SO[j] + P * i:SO[j] + P * i + P], ident[:, :])
                mm.then_inc(pt_ps.sem, 1)

            def a_pv(b, h):
                if h % 2 == 0:
                    pe.wait_ge(y_norm.sem, y_norm.at(b, h // 2))
                pe.wait_ge(pt_lo.sem, pt_lo.at(b, 3 * h + 3))
                for j in range(NT):
                    for i in range(j + 1):
                        at = TO[(i, j)]
                        acc = wide[:, 256 * (h % 2) + DK * j:256 * (h % 2) + DK * j + DK]
                        mm = three(pe, acc, cut(pt, lambda t: t[:, h % 2, at:at + P]),
                                   cut(vv, lambda t: t[:, i, DK * h:DK * h + DK]), start=i == 0, stop=i == j)
                if h % 2:
                    mm.then_inc(y_ps.sem, 1)

            def a_yturn(b, p, z_done):
                pe.wait_ge(z_lo.sem, z_lo.at(b, z_done))
                if p:
                    pe.wait_ge(yt_lo.sem, yt_lo.at(b, p))
                pe.wait_ge(y_norm.sem, y_norm.at(b, p + 1))
                for j in range(NT):
                    mm = pe.transpose(bank[5][:, P * j:P * j + P],
                                      ysb[:, p % 2, j, :, :].rearrange("p e n -> p (e n)"), ident[:, :])
                mm.then_inc(yt_ps.sem, 1)

            def a_out(b, p):
                pe.wait_ge(yt_lo.sem, yt_lo.at(b, p + 1))
                mm = three(pe, wide[:, 512:1024], cut(wog, lambda t: t[:, p, :]), cut(yt, lambda t: t[:, :]),
                           start=p == 0, stop=p == PAIRS - 1)
                if p == PAIRS - 1:
                    mm.then_inc(a_ps.sem, 1)

            with pe.Fori(0, BATCH) as b:
                pe.wait_ge(xh_ready.sem, xh_ready.at(b, NT))
                for j in range(NT):
                    mm = pe.transpose(bank[5][:, P * j:P * j + P], xh[:, j, :], ident[:, :])
                mm.then_inc(xt_ps.sem, 1)
                pe.wait_ge(xt_lo.sem, xt_lo.at(b, 1))
                for g in range(8):
                    if g < 3:
                        pe.wait_ge(s_exp.sem, s_exp.at(b, 0))
                    else:
                        pe.wait_ge(v_lo.sem, v_lo.at(b, g - 2))
                    i, n0 = g // 2, 512 * (g % 2)
                    three(pe, bank[g % 3][:, :], cut(xt, lambda t: t[:, P * i:P * i + P]),
                          cut(wv, lambda t: t[:, n0:n0 + 512])).then_inc(v_ps.sem, 1)
                a_z(b, 0, (xt_lo.sem, xt_lo.at(b, 1)))
                pe.wait_ge(v_lo.sem, v_lo.at(b, 8))
                for h in range(H + 1):
                    if h >= 4 and h % 2 == 0:
                        a_out(b, (h - 4) // 2)
                    if h + 1 < H:
                        a_z(b, h + 1, (z_lo.sem, z_lo.at(b, h + 1)))
                    if h < H:
                        for j in range(3):
                            a_scores(b, h, j)
                    if h >= 1:
                        for g in range(3):
                            a_turn(b, h - 1, g)
                    if h < H:
                        a_scores(b, h, 3)
                    if h >= 1:
                        a_pv(b, h - 1)
                    if h >= 3 and h % 2:
                        a_yturn(b, (h - 3) // 2, min(h + 2, H))
                a_yturn(b, PAIRS - 1, H)
                a_out(b, PAIRS - 1)
                pe.wait_ge(a_sb.sem, a_sb.at(b, 1))
                for j in range(NT):
                    mm = pe.transpose(bank[5][:, P * j:P * j + P], tail[:, P * j:P * j + P], ident[:, :])
                mm.then_inc(a_back.sem, 1)
            barrier(pe, 2)

            def b_qkv(it, j):
                h = cut(xt, lambda t: t[:, P * j:P * j + P])
                pe.wait_ge(bqt_lo.sem, bqt_lo.at(it, 3 * j))
                for n in range(2):
                    mm = three(pe, wide[:, 512 * n:512 * n + 512], h, cut(wl, lambda t: t[:, 512 * n:512 * n + 512]))
                mm.then_inc(bqk_ps.sem, 1)
                pe.wait_ge(bv_lo.sem, bv_lo.at(it, 4 * j))
                three(pe, bank[4][:, :], h, cut(wl, lambda t: t[:, 1024:1536])).then_inc(bv_ps.sem, 1)

            def b_turn(it, j):
                pe.wait_ge(bqk.sem, bqk.at(it, j + 1))
                for n in range(8):
                    mm = pe.transpose(wide[:, P * n:P * n + P], qk[:, P * n:P * n + P], ident[:, :])
                mm.then_inc(bqt_ps.sem, 1)

            def b_scores(it, j, p):
                q = j * LPAIRS + p
                if p == 0:
                    pe.wait_ge(bqt_lo.sem, bqt_lo.at(it, 3 * j + 3))
                pe.wait_ge(bexp.sem, bexp.at(it, 2 * q - 2))
                k0, w = (0, P) if j == 0 else (P * j - WINDOW, P + WINDOW)
                acc = bank[q % 2][:, 0:2 * w].rearrange("p (e n) -> p e n", e=2)
                three(pe, acc, cut(qt, lambda t: t[:, p, :]), cut(kt, lambda t: t[:, p, :, k0:k0 + w]), stop=False)
                pe.matmul(acc, ident16[:, :], band[:, :, P + WINDOW - w:], start=False, stop=True).then_inc(bs_ps.sem, 1)

            def b_pt(it, j, p):
                q = j * LPAIRS + p
                m0 = 1 if j == 0 else 0
                pe.wait_ge(bexp.sem, bexp.at(it, 2 * q + 2))
                pe.wait_ge(bpt_lo.sem, bpt_lo.at(it, q))
                for m in range(m0, 3):
                    mm = pe.transpose(bank[2][:, P * m:P * m + P],
                                      lprob[:, q % 2, m, :, :].rearrange("p e n -> p (e n)"), ident[:, :])
                mm.then_inc(bpt_ps.sem, 1)

            def b_pv(it, j, p):
                q = j * LPAIRS + p
                m0 = 1 if j == 0 else 0
                pe.wait_ge(bpt_lo.sem, bpt_lo.at(it, q + 1))
                pe.wait_ge(bv_lo.sem, bv_lo.at(it, 4 * j + 4))
                if p == 0:
                    pe.wait_ge(by_norm.sem, by_norm.at(it, j))
                for m in range(m0, 3):
                    mm = three(pe, ypart[:, P * p:P * p + P], cut(lpt, lambda t: t[:, q % 2, m, :]),
                               cut(vb, lambda t: t[:, 2 * j - 1 + m, p, :]), start=m == m0, stop=m == 2)
                if p == LPAIRS - 1:
                    mm.then_inc(by_ps.sem, 1)

            def b_ot(it, j):
                pe.wait_ge(by_norm.sem, by_norm.at(it, j + 1))
                if j:
                    pe.wait_ge(bot_lo.sem, bot_lo.at(it, j))
                for n in range(LPAIRS):
                    mm = pe.transpose(bank[5][:, P * n:P * n + P], osb[:, j % 2, P * n:P * n + P], ident[:, :])
                mm.then_inc(bot_ps.sem, 1)

            with pe.Fori(0, DEPTH) as l:
                pe.wait_ge(s_lw, (l + 1) * 16 * 21)
                for n in range(6):
                    r0, rows = HC[n % 3]
                    r0 += HID * (n // 3)
                    mm = pe.matmul(bank[0][0:rows, n:n + 1], raw_w1[:, r0:r0 + rows], cols[:, 1:2], start=True, stop=True)
                mm.then_inc(lay_pe, 1)
                barrier(pe, l * 3 + 3)
                with pe.Fori(0, BATCH) as b:
                    it = l * BATCH + b
                    pe.wait_ge(bxs.sem, bxs.at(it, 1))
                    pe.wait_ge(bx.sem, bx.at(it, 0))
                    for j in range(NT):
                        mm = pe.transpose(bank[5][:, P * j:P * j + P], xs[:, j, :], ident[:, :])
                    mm.then_inc(bxt_ps.sem, 1)
                    pe.wait_ge(bh_lo.sem, bh_lo.at(it, 2))
                    b_qkv(it, 0)
                    for j in range(NT):
                        b_turn(it, j)
                        b_scores(it, j, 0)
                        if j + 1 < NT:
                            b_qkv(it, j + 1)
                        b_scores(it, j, 1)
                        b_pt(it, j, 0)
                        b_pv(it, j, 0)
                        if j:
                            b_ot(it, j - 1)
                        b_scores(it, j, 2)
                        b_pt(it, j, 1)
                        b_pv(it, j, 1)
                        b_scores(it, j, 3)
                        b_pt(it, j, 2)
                        b_pv(it, j, 2)
                        b_pt(it, j, 3)
                        b_pv(it, j, 3)
                    b_ot(it, NT - 1)
                    pe.wait_ge(bot_lo.sem, bot_lo.at(it, NT))
                    for n in range(LPAIRS):
                        mm = three(pe, bank[5][:, :], cut(wol, lambda t: t[:, n, :]), cut(ot, lambda t: t[:, n, :]),
                                   start=n == 0, stop=n == LPAIRS - 1)
                    mm.then_inc(bo_ps.sem, 1)
                    pe.wait_ge(bo_sb.sem, bo_sb.at(it, 1))
                    for j in range(NT):
                        mm = pe.transpose(bank[5][:, P * j:P * j + P], tail[:, P * j:P * j + P], ident[:, :])
                    mm.then_inc(bo_back.sem, 1)
                barrier(pe, l * 3 + 4)
                with pe.Fori(0, BATCH) as b:
                    it = l * BATCH + b
                    pe.wait_ge(chn.sem, chn.at(it, NT))
                    pe.wait_ge(cx.sem, cx.at(it, 0))
                    for j in range(NT):
                        mm = pe.transpose(bank[5][:, P * j:P * j + P], xh[:, j, :], ident[:, :])
                    mm.then_inc(ct_ps.sem, 1)
                    pe.wait_ge(ct_lo.sem, ct_lo.at(it, 1))
                    for n in range(3):
                        r0, rows = HC[n]
                        if n == 2:
                            pe.wait_ge(cu.sem, cu.at(it, 1))
                        for a, s in ((HID, cg_ps), (0, ca_ps)):
                            acc = bank[(0 if a else 2) + n % 2][0:rows, :]
                            three(pe, acc, cut(w1l, lambda t: t[:, a + r0:a + r0 + rows]),
                                  cut(xt, lambda t: t[:, :])).then_inc(s.sem, 1)
                    for n in range(3):
                        rows = HC[n][1]
                        pe.wait_ge(cu_lo.sem, cu_lo.at(it, n + 1))
                        mm = three(pe, bank[4][:, :], cut(w2l, lambda t: t[0:rows, n, :]),
                                   cut(ut, lambda t: t[0:rows, n, :]), start=n == 0, stop=n == 2)
                    mm.then_inc(co_ps.sem, 1)
                    pe.wait_ge(co_sb.sem, co_sb.at(it, 1))
                    for j in range(NT):
                        mm = pe.transpose(bank[5][:, P * j:P * j + P], tail[:, P * j:P * j + P], ident[:, :])
                    mm.then_inc(co_back.sem, 1)
                barrier(pe, l * 3 + 5)


def rope_tables():
    f = np.float32
    half = np.arange(0, LD, 2, dtype=f)
    t = np.arange(T, dtype=f)
    freqs = t[:, None] * (f(1.0) / f(10000.0) ** (half / f(LD)))[None, :]
    power = (t - T // 2) / f(WINDOW // 2)
    scale = ((half + f(0.4 * LD)) / f(1.4 * LD))[None, :] ** power[:, None]
    both = lambda a: np.concatenate([a, a], axis=-1)
    cos, sin, scale = both(np.cos(freqs)), both(np.sin(freqs)), both(scale)
    sin[:, :LD // 2] *= -1
    return [np.stack([a * scale * f(8.0), a / scale], axis=1).astype(f) for a in (cos, sin)]


def constants():
    i, c = np.arange(P)[:, None], np.arange(P + WINDOW)[None, :]
    causal = np.where(np.arange(P)[None, :] > i, MASKED, 0.0).astype(np.float32)
    band = np.where((c >= i) & (c <= i + WINDOW), 0.0, MASKED).astype(np.float32)
    cos, sin = rope_tables()
    return {"ident": np.eye(P, dtype=np.float32), "causal": causal, "band": np.concatenate([band, band], axis=1),
            "rope_cos": cos, "rope_sin": sin}


_INS = ["L0_attn_x", "L0_attn_w_q", "L0_attn_w_k", "L0_attn_w_v", "L0_attn_w_o", "L0_ffn_wqkv", "L0_ffn_q_scale",
        "L0_ffn_k_scale", "L0_ffn_wo", "L0_ffn_ln_g", "L0_ffn_ln_b", "L0_ffn_w1", "L0_ffn_b1", "L0_ffn_w2", "L0_ffn_b2"]


def kernel(**inputs):
    import concourse.bacc as _bacc
    from concourse.bass_utils import run_bass_kernel_spmd as _run

    nc = _bacc.Bacc("TRN2", target_bir_lowering=False, num_devices=1)
    arrays, args = {}, []
    given = {**{n: inputs[n] for n in _INS}, **constants()}
    for name, a in given.items():
        a = np.ascontiguousarray(a)
        arrays[f"in_{name}"] = a
        args.append(nc.dram_tensor(f"in_{name}", a.shape, mybir.dt.from_np(a.dtype), kind="ExternalInput").ap())
    args.append(nc.dram_tensor("out_0", (BATCH, T, C), F32, kind="ExternalOutput").ap())
    sandwich(nc, *args)
    r = _run(nc, [arrays], core_ids=[0])
    return r.results[0]["out_0"]
```

```python
from contextlib import ExitStack

import numpy as np

import concourse.bass as bass
from concourse import mybir

F32 = mybir.dt.float32
F32R = mybir.dt.float32r
F16 = mybir.dt.float16
BF16 = mybir.dt.bfloat16
ALU = mybir.AluOpType
ACT = mybir.ActivationFunctionType
AX = mybir.AxisListType

P = 128
BATCH, T, C = 8, 512, 128
NT = T // P
H, DK = 16, 64
PAIRS = H // 2
DEPTH = 2
LH, LD = 8, 64
LPAIRS = LH // 2
INNER = LH * LD
WINDOW = 64
HID = int(C * 4 * 2 / 3)
HC = [(0, 128), (128, 128), (256, HID - 256)]
EPS = 1e-5
MASKED = -1e30

SW = [P * (j + 1) for j in range(NT)]
SO = [sum(SW[:j]) for j in range(NT)]
SCORES = sum(SW)
TG = [[(0, 0), (0, 1), (1, 1), (0, 2)], [(1, 2), (2, 2), (0, 3), (1, 3)], [(2, 3), (3, 3)]]
TG_NEEDS = [max(j for _, j in blks) for blks in TG]
TO = {blk: 512 * g + P * n for g, blks in enumerate(TG) for n, blk in enumerate(blks)}


POOL_STEPS = 9


class Signal:

    def __init__(self, nc, ctx, name, per, credit=0, over=0):
        self.sem, self.per, self.credit, self.over = ctx.enter_context(nc.semaphore(name)), per, credit, over

    def at(self, it, n):
        if isinstance(it, tuple):
            l, b = it
            return l * (BATCH * self.per + self.over) + b * self.per + (n + self.credit)
        return it * self.per + (n + self.credit)


class Steps:

    def __init__(self, eng, raised):
        self.eng, self.raised, self.n, self.it = eng, raised, 0, 0

    def start(self, it):
        self.it, self.n = it, 0

    def did(self, ins):
        ins.then_inc(self.raised.sem, 1)
        self.n += 1

    def settle(self):
        self.eng.wait_ge(self.raised.sem, self.raised.at(self.it, self.n))

    def end(self):
        assert self.n == self.raised.per, (self.n, self.raised.per)


def sandwich(nc, x, w_q, w_k, w_v, w_o, wqkv, q_scale, k_scale, wo, ln_g, ln_b, w1, b1, w2, b2,
             ident_c, causal_c, band_c, rope_cos_c, rope_sin_c, out):
    ctx = ExitStack()
    with ctx:
        def sb(name, shape, dt=F32):
            return ctx.enter_context(nc.sbuf_tensor(name, shape, dt))

        def sem(name):
            return ctx.enter_context(nc.semaphore(name))

        def sig(name, per, credit=0, over=0):
            return Signal(nc, ctx, name, per, credit, over)

        bank = [ctx.enter_context(nc.psum_tensor(f"bank{i}", [P, 512], F32)) for i in range(6)]
        wide = ctx.enter_context(nc.psum_tensor("wide", [P, 1024], F32))

        ypart = bank[3]

        x1 = sb("x1", [P, (BATCH + 1) * NT, C])
        xf = sb("xf", [P, (BATCH + 1) * NT, C])
        ident = sb("ident", [P, P])
        ident16 = sb("ident16", [P, P], BF16)
        causal = sb("causal", [P, P], BF16)
        band = sb("band", [P, 2, P + WINDOW], BF16)
        rope = sb("rope", [P, 2, NT, 2, LD])
        ropes = sb("ropes", [P, 2, NT, 2, LD])
        qks = sb("qks", [P, 2, 2, LD])
        stage = sb("stage", [P, 4096])

        big = [sb(f"big{n}", [P, 4096], F32R) for n in range(2)]
        mh = [big[0][:, H * C * n:H * C * (n + 1)].rearrange("p (h c) -> p h c", h=H) for n in range(2)]
        wv = [big[1][:, H * DK * n:H * DK * (n + 1)] for n in range(2)]
        wog = [big[1][:, 1024 * (2 + n):1024 * (3 + n)].rearrange("p (g c) -> p g c", g=PAIRS) for n in range(2)]
        wl = [sb(f"wqkv_{s}", [P, 3 * INNER], F32R) for s in ("hi", "lo")]
        wol = [sb(f"wol_{s}", [P, LPAIRS, C], F32R) for s in ("hi", "lo")]
        w1l = [sb(f"w1_{s}", [P, 2 * HID], F32R) for s in ("hi", "lo")]
        w2l = [sb(f"w2_{s}", [P, 3, C], F32R) for s in ("hi", "lo")]
        w1g = sb("w1g", [P, 2 * HID])
        cols = sb("cols", [P, 10])
        b1f = sb("b1f", [P, 6])

        stats = sb("stats", [P, NT, 6])
        mv = sb("mv", [P, NT, 2])
        vare = sb("vare", [P, NT])
        rstd = sb("rstd", [P, NT])
        mhalf = sb("mhalf", [P, 2 * LH])
        xh = sb("xh", [P, NT, C])
        xn = sb("xn", [P, NT, C])
        xt = [sb(f"xt_{s}", [P, T], F32R) for s in ("hi", "lo")]
        mid = [sb(f"mid{n}", [P, 2048], F32R) for n in range(2)]
        zt = [mid[0][:, 1024 * n:1024 * n + 1024].rearrange("p (a t) -> p a t", a=2) for n in range(2)]
        negmax = sb("negmax", [P, 2, NT])
        rsum = sb("rsum", [P, 2, 2, NT])
        rinv = sb("rinv", [P, 2, NT])
        yt = [mid[1][:, T * n:T * n + T] for n in range(2)]
        work = sb("work", [P, 4 * SCORES])
        prob = work[:, 0:2 * SCORES].rearrange("p (a n) -> p a n", a=2)
        pt = [work[:, (2 + n) * SCORES:(3 + n) * SCORES].bitcast(F16).rearrange("p (a n) -> p a n", a=2)
              for n in range(2)]
        vv = [sb(f"v_{s}", [P, NT, H * DK], F16) for s in ("hi", "lo")]
        ysb = sb("ysb", [P, 2, NT, 2, DK])
        tail = sb("tail", [P, T])

        xs = xh
        sq, rot_a, rot_b, qk0 = (work[:, 2 * INNER * n:2 * INNER * (n + 1)] for n in range(4))
        qk1 = sb("qk1", [P, 2 * INNER])
        qk = (qk0, qk1)
        ssq = sb("ssq", [P, 2 * LH])
        ssqc = sb("ssqc", [P, 2 * LH])
        rnorm = sb("rnorm", [P, 2 * LH])
        qt = [sb(f"qt_{s}", [P, 2, LPAIRS, P], F32R) for s in ("hi", "lo")]
        kt = [big[n][:, :].rearrange("p (c e t) -> p c e t", c=LPAIRS, e=2) for n in range(2)]
        vb = [v[:, :, :].rearrange("p t (a c n) -> p (t a) c n", a=2, c=LPAIRS) for v in vv]
        lprob = work[:, 8 * INNER:8 * INNER + 12 * LD].rearrange("p (a m e n) -> p a m e n", a=2, m=3, e=2)
        lpt = [sb(f"lpt_{s}", [P, 2, 3, P], F16) for s in ("hi", "lo")]
        lneg = sb("lneg", [P, 4, 2])
        lsum = sb("lsum", [P, 2, LH])
        linv = sb("linv", [P, LH])
        osb = ysb[:, :, :, :, :].rearrange("p a j e n -> p a (j e n)")
        ot = [mid[n][:, :].rearrange("p (c t) -> p c t", c=LPAIRS) for n in range(2)]

        hs = sb("hs", [P, NT, C])
        gel = prob[:, 0, 0:1024].rearrange("p (a n) -> p a n", a=2)
        ugl = prob[:, 1, 0:1024].rearrange("p (a n) -> p a n", a=2)
        ut = [big[n][:, 0:3 * T].rearrange("p (c t) -> p c t", c=3) for n in range(2)]

        phase, held = sem("phase"), sem("held")
        s_x, s_const, s_weights, s_out = sem("x_loaded"), sem("const_loaded"), sem("weights_loaded"), sem("out_stored")
        s_lw = sem("layer_weights_loaded")
        pre_pe, pre_act, pre_dve, pre_pool = sem("pre_pe"), sem("pre_act"), sem("pre_dve"), sem("pre_pool")
        lay_pe, lay_act, lay_dve = sem("lay_pe"), sem("lay_act"), sem("lay_dve")
        n_step = sig("n_step", 2 * NT)
        a_step = sig("a_step", 2 * NT * 2 + NT + PAIRS + 1)
        a_left = sig("a_left", NT, NT)
        xh_ready, xt_ps, xt_hi, xt_lo = sig("xh_ready", NT), sig("xt_ps", 1), sig("xt_hi", 1), sig("xt_lo", 1)
        v_ps, v_hi, v_lo = sig("v_ps", 8), sig("v_hi", 8), sig("v_lo", 8)
        z_ps, z_hi, z_lo = sig("z_ps", H), sig("z_hi", H), sig("z_lo", H)
        s_ps, s_max, s_exp = sig("scores_ps", H * NT), sig("scores_max", H * NT), sig("probs_ready", H * NT, H * NT)
        pt_ps, pt_hi, pt_lo = sig("pt_ps", 3 * H), sig("pt_hi", 3 * H), sig("pt_lo", 3 * H, 3 * H)
        y_ps, y_norm = sig("y_ps", PAIRS), sig("y_norm", PAIRS, PAIRS)
        yt_ps, yt_hi, yt_lo = sig("yt_ps", PAIRS), sig("yt_hi", PAIRS), sig("yt_lo", PAIRS)
        a_ps, a_sb, a_back = sig("a_ps", 1), sig("a_sb", 1), sig("a_back", 1)
        r_step = sig("r_step", 2 * NT, over=4)
        o_step = sig("o_step", NT)
        p_step = sig("p_step", POOL_STEPS * NT, 1, over=2 * POOL_STEPS)
        bxs, bxt_ps = sig("bxs", 1, over=1), sig("bxt_ps", 1, over=1)
        bh_hi, bh_lo = sig("bh_hi", 2, over=2), sig("bh_lo", 2, over=2)
        bqk_ps, bv_ps, bsq = sig("bqk_ps", NT, over=2), sig("bv_ps", NT, over=2), sig("bsq", NT, over=2)
        brot, bqk = sig("brot", NT, over=2), sig("bqk", NT, over=2)
        bqt_ps, bqt_hi = sig("bqt_ps", NT, over=1), sig("bqt_hi", 3 * NT, over=3)
        bqt_lo = sig("bqt_lo", 3 * NT, over=3)
        bv_hi, bv_lo = sig("bv_hi", 4 * NT, over=8), sig("bv_lo", 4 * NT, 4, over=8)
        bs_ps, bmax, bexp = sig("bs_ps", 16, over=1), sig("bmax", 16, over=1), sig("bexp", 32, 4, over=2)
        bpt_ps, bpt_hi, bpt_lo = sig("bpt_ps", 16), sig("bpt_hi", 16), sig("bpt_lo", 16, 1)
        by_ps, by_norm = sig("by_ps", NT), sig("by_norm", NT, NT)
        bot_ps, bot_hi, bot_lo = sig("bot_ps", NT), sig("bot_hi", NT), sig("bot_lo", NT)
        bo_ps, bo_sb, bo_back, bx = sig("bo_ps", 1), sig("bo_sb", 1), sig("bo_back", 1), sig("bx", 1, 1)
        c_step = sig("c_step", NT * 2)
        chs, chs_dma, chn = sig("chs", 1), sig("chs_dma", 32), sig("chn", NT, NT)
        ct_ps, ct_hi, ct_lo = sig("ct_ps", 1), sig("ct_hi", 1), sig("ct_lo", 1)
        cg_ps, ca_ps, cgel, cu = sig("cg_ps", 3), sig("ca_ps", 3), sig("cgel", 3), sig("cu", 3, 3)
        cu_hi, cu_lo = sig("cu_hi", 3), sig("cu_lo", 3)
        co_ps, co_sb, co_back, cx = sig("co_ps", 1), sig("co_sb", 1), sig("co_back", 1), sig("cx", 1, 1)
        d_step, d_out = sig("d_step", 3 * NT), sig("d_out", 1)

        n_root = sig("n_var", 1), sig("n_rstd", 1)
        a_root = sig("a_var", 2), sig("a_rstd", 2)
        c_root = sig("c_var", 1), sig("c_rstd", 1)
        d_root = sig("d_var", 1), sig("d_rstd", 1)

        def hold(eng, semaphore, value):
            eng.wait_ge(semaphore, value)
            eng.sem_inc(held, 1)

        def barrier(eng, n):
            eng.drain().then_inc(phase, 1)
            hold(eng, phase, n * 5)

        def layer_norm(dve, steps, src, root, it, k, dst, last):
            for j in range(NT):
                steps.did(dve.bn_stats(stats[:, j, :], src(j)))
            hold(dve, steps.raised.sem, steps.raised.at(steps.it, steps.n))
            for j in range(NT):
                steps.did(dve.bn_aggr(mv[:, j, :], stats[:, j, :]))
            steps.settle()
            dve.tensor_scalar(vare[:, :], mv[:, :, 1], EPS, None, ALU.add).then_inc(root[0].sem, 1)
            dve.wait_ge(root[1].sem, root[1].at(it, k + 1))
            for j in range(NT):
                ins = dve.tensor_scalar(dst(j), src(j), mv[:, j, 0:1], rstd[:, j:j + 1],
                                        ALU.subtract, ALU.mult)
                if last is None:
                    steps.did(ins)
                else:
                    ins.then_inc(last.sem, 1)

        def inverse_root(pool, root, it, k):
            pool.wait_ge(root[0].sem, root[0].at(it, k + 1))
            pool.tensor_tensor(rstd[:, :], vare[:, :], mhalf[:, 0:NT], ALU.pow).then_inc(root[1].sem, 1)

        def three(pe, acc, left, right, start=True, stop=True):
            pe.matmul(acc, left[0], right[0], start=start, stop=False)
            pe.matmul(acc, left[0], right[1], start=False, stop=False)
            return pe.matmul(acc, left[1], right[0], start=False, stop=stop)

        def cut(pair, f):
            return [f(t) for t in pair]

        block = ctx.enter_context(nc.Block())

        raw_q = stage[0:DK, 0:H * C].rearrange("d (h c) -> d h c", h=H)
        raw_k = stage[0:DK, H * C:2 * H * C].rearrange("d (h c) -> d h c", h=H)
        raw_v = sq[:, :].rearrange("p (g c) -> p g c", g=PAIRS)
        raw_o = rot_a[:, :].rearrange("p (g c) -> p g c", g=PAIRS)
        raw_causal, raw_band = rot_b[:, 0:P], rot_b[:, P:P + 2 * (P + WINDOW)]
        raw_qkv = stage[:, 0:3 * INNER]
        raw_wo = stage[:, 1536:2048].rearrange("p (g c) -> p g c", g=LPAIRS)
        raw_w1 = stage[:, 2048:2048 + 2 * HID]
        raw_w2 = stage[:, 2816:2816 + 3 * C].rearrange("p (g c) -> p g c", g=3)

        @block.sync
        def _(sp):
            sp.dma_start(ident[:, :], ident_c).then_inc(s_const, 16)
            sp.dma_start(raw_q, w_q.rearrange("h d c -> d h c")).then_inc(s_weights, 16)
            sp.dma_start(raw_k, w_k.rearrange("h d c -> d h c")).then_inc(s_weights, 16)
            sp.dma_start(raw_v, w_v.rearrange("(g a) d c -> (a d) g c", a=2)).then_inc(s_weights, 16)
            sp.dma_start(raw_o, w_o.rearrange("(g p) c -> p g c", p=P)).then_inc(s_weights, 16)
            sp.dma_start(raw_causal, causal_c).then_inc(s_const, 16)
            sp.dma_start(raw_band, band_c).then_inc(s_const, 16)
            sp.dma_start(x1[:, 0:BATCH * NT, :], x.rearrange("b (j p) c -> p (b j) c", p=P)).then_inc(s_x, 16)
            sp.dma_start(rope[:, 0, :, :, :], rope_cos_c.rearrange("(j p) a d -> p j a d", p=P)).then_inc(s_const, 16)
            sp.dma_start(rope[:, 1, :, :, :], rope_sin_c.rearrange("(j p) a d -> p j a d", p=P)).then_inc(s_const, 16)
            barrier(sp, 1)
            barrier(sp, 2)
            with sp.Fori(0, DEPTH) as l:
                def layer(w, pattern="o a b -> (o a) b", **kw):
                    return w[bass.ds(l, 1)].rearrange(pattern, **kw)
                sp.dma_start(raw_qkv, layer(wqkv)).then_inc(s_lw, 16)
                sp.dma_start(raw_wo, layer(wo, "o (g p) c -> p (o g) c", p=P)).then_inc(s_lw, 16)
                sp.dma_start(raw_w1, layer(w1)).then_inc(s_lw, 16)
                for n, (r0, rows) in enumerate(HC):
                    sp.dma_start(raw_w2[0:rows, n, :], layer(w2)[r0:r0 + rows, :]).then_inc(s_lw, 16)
                for n, v in enumerate((ln_g, ln_b, b2)):
                    sp.dma_start(cols[:, n:n + 1], layer(v, "o (c k) -> (o c) k", k=1)).then_inc(s_lw, 16)
                for n in range(6):
                    r0, rows = HC[n % 3]
                    r0 += HID * (n // 3)
                    sp.dma_start(cols[0:rows, 3 + n:4 + n],
                                 layer(b1, "o (c k) -> (o c) k", k=1)[r0:r0 + rows, :]).then_inc(s_lw, 16)
                for n, v in enumerate((q_scale, k_scale)):
                    row = v[bass.ds(l, 1), :]
                    sp.dma_start(qks[:, 0, n, :], row.to_broadcast([P, LD])).then_inc(s_lw, 16)
                    sp.dma_start(qks[:, 1, n, 0:LD // 2], row[:, LD // 2:].to_broadcast([P, LD // 2])).then_inc(s_lw, 16)
                    sp.dma_start(qks[:, 1, n, LD // 2:], row[:, 0:LD // 2].to_broadcast([P, LD // 2])).then_inc(s_lw, 16)
                barrier(sp, l * 3 + 3)
                barrier(sp, l * 3 + 4)
                with sp.Fori(0, BATCH) as b:
                    it = l * BATCH + b
                    sp.wait_ge(chn.sem, chn.at(it, 0))
                    sp.dma_start(hs[1:P, :, C // 2:], xf[0:P - 1, bass.ds(b * NT, NT), C // 2:]).then_inc(chs_dma.sem, 16)
                    sp.dma_start(hs[0:1, 1:NT, C // 2:], xf[P - 1:P, bass.ds(b * NT, NT - 1), C // 2:]).then_inc(chs_dma.sem, 16)
                barrier(sp, l * 3 + 5)
            with sp.Fori(0, BATCH) as b:
                sp.wait_ge(d_out.sem, d_out.at(b, 1))
                sp.dma_start(out[bass.ds(b, 1)].rearrange("o (j p) c -> p (o j) c", p=P),
                             x1[:, bass.ds(b * NT, NT), :]).then_inc(s_out, 16)
            sp.wait_ge(s_out, 16 * BATCH)

        @block.gpsimd
        def _(pool):
            pool.memset(hs[0:1, 0:1, C // 2:], 0.0).then_inc(pre_pool, 1)
            pool.memset(mhalf[:, :], -0.5).then_inc(pre_pool, 1)
            pool.sem_inc(p_step.sem, p_step.credit)
            for t in (x1, xf):
                pool.memset(t[:, BATCH * NT:, :], 0.0).then_inc(pre_pool, 1)
            barrier(pool, 1)
            inverse_root(pool, n_root, 0, 0)
            with pool.Fori(0, BATCH) as b:
                inverse_root(pool, n_root, b + 1, 0)
                for k in range(2):
                    inverse_root(pool, a_root, b, k)
            barrier(pool, 2)
            with pool.Fori(0, DEPTH) as l:
                for t in kt:
                    z = t[:, :, :, :].bitcast(F32)
                    pool.memset(z[0:DK, :, 1, :], 0.0).then_inc(pre_pool, 1)
                    pool.memset(z[DK:P, :, 0, :], 0.0).then_inc(pre_pool, 1)
                for t in xt:
                    pool.memset(t[DK:P, 0:1].bitcast(F32), 0.0).then_inc(pre_pool, 1)
                for t in vb:
                    pool.memset(t[0:DK, :, :, DK:P], 0.0).then_inc(pre_pool, 1)
                    pool.memset(t[DK:P, :, :, 0:DK], 0.0).then_inc(pre_pool, 1)
                barrier(pool, l * 3 + 3)

                def ahead(b):
                    pool.tensor_copy(xs[:, :, :], xf[:, bass.ds(b * NT, NT), :]).then_inc(bxs.sem, 1)

                def turn_qk(it, j):
                    steps = Steps(pool, p_step)
                    steps.start(it)
                    steps.n = POOL_STEPS * j
                    pool.wait_ge(bsq.sem, bsq.at(it, j + 1))
                    w = LD // 2
                    squares = sq.rearrange("p (h d) -> p h d", d=LD)
                    while w:
                        dst = squares[:, :, 0:w] if w > 1 else ssq[:, :, None]
                        steps.did(pool.tensor_tensor(dst, squares[:, :, 0:w], squares[:, :, w:2 * w], ALU.add))
                        if w > 1:
                            steps.settle()
                        else:
                            hold(pool, steps.raised.sem, steps.raised.at(steps.it, steps.n))
                        w //= 2
                    steps.did(pool.tensor_scalar(ssqc[:, :], ssq[:, :], 1e-24, None, ALU.max))
                    steps.settle()
                    steps.did(pool.tensor_tensor(rnorm[:, :], ssqc[:, :], mhalf[:, :], ALU.pow))
                    pool.wait_ge(brot.sem, brot.at(it, j + 1))
                    steps.did(pool.tensor_tensor(qk[j % 2][:, :], rot_a[:, :], rot_b[:, :], ALU.add))
                    steps.settle()
                    assert steps.n == POOL_STEPS * (j + 1)
                    v = qk[j % 2][:, :].rearrange("p (h d) -> p h d", d=LD)
                    pool.tensor_tensor(v, v, rnorm[:, :, None].to_broadcast([P, 2 * LH, LD]),
                                       ALU.mult).then_inc(bqk.sem, 1)

                ahead(0)
                for j in range(2):
                    turn_qk((l, 0), j)
                with pool.Fori(0, BATCH) as b:
                    ahead(b + 1)
                    for j in range(NT):
                        turn_qk((l, b), j + 2)
                barrier(pool, l * 3 + 4)
                with pool.Fori(0, BATCH) as b:
                    it = l * BATCH + b
                    pool.wait_ge(chn.sem, chn.at(it, 0))
                    pool.tensor_copy(hs[:, :, 0:C // 2], xf[:, bass.ds(b * NT, NT), 0:C // 2]).then_inc(chs.sem, 1)
                    inverse_root(pool, c_root, it, 0)
                    for n in range(3):
                        rows = HC[n][1]
                        pool.wait_ge(cu_hi.sem, cu_hi.at(it, n + 1))
                        pool.tensor_tensor(ut[1][0:rows, n, :], ugl[0:rows, n % 2, :],
                                           ut[0][0:rows, n, :].bitcast(F32), ALU.subtract).then_inc(cu_lo.sem, 1)
                barrier(pool, l * 3 + 5)
            with pool.Fori(0, BATCH) as b:
                inverse_root(pool, d_root, b, 0)

        @block.scalar
        def _(act):
            def copy(dst, src):
                return act.activation(dst, src, ACT.Copy)

            act.wait_ge(s_const, 80)
            act.wait_ge(s_weights, 64)
            copy(ident16[:, :], ident[:, :]).then_inc(pre_act, 1)
            copy(causal[:, :], raw_causal).then_inc(pre_act, 1)
            copy(band[:, :, :].rearrange("p a n -> p (a n)"), raw_band).then_inc(pre_act, 1)
            copy(wog[0][:, :, :], raw_o).then_inc(pre_act, 1)
            for n in range(4):
                act.wait_ge(pre_pe, n + 1)
                act.activation(mh[0][:, 4 * n:4 * n + 4, :].rearrange("p h c -> p (h c)"), bank[n][:, :],
                               ACT.Copy, scale=DK ** -0.5).then_inc(pre_act, 1)
            for n in range(2):
                act.wait_ge(pre_pe, n + 5)
                copy(wv[0][:, 512 * n:512 * n + 512], bank[4 + n][:, :]).then_inc(pre_act, 1)
            barrier(act, 1)

            def a_exp(b, h, j):
                n = h * NT + j
                act.wait_ge(s_max.sem, s_max.at(b, n + 1))
                act.activation(prob[:, h % 2, SO[j]:SO[j] + SW[j]], bank[n % 3][:, 0:SW[j]], ACT.Exp,
                               bias=negmax[:, h % 2, j:j + 1],
                               accum_out=rsum[:, h // 2 % 2, h % 2, j:j + 1]).then_inc(s_exp.sem, 1)

            def a_pt(b, h, g):
                n = 3 * h + g
                w = P * len(TG[g])
                act.wait_ge(pt_ps.sem, pt_ps.at(b, n + 1))
                copy(pt[0][:, h % 2, 512 * g:512 * g + w], bank[3 + n % 2][:, 0:w]).then_inc(pt_hi.sem, 1)

            def a_z(b, h):
                act.wait_ge(z_ps.sem, z_ps.at(b, h + 1))
                copy(zt[0][:, h % 2, :], bank[5][:, :]).then_inc(z_hi.sem, 1)

            def a_yt(b, p):
                act.wait_ge(yt_ps.sem, yt_ps.at(b, p + 1))
                copy(yt[0][:, :], bank[5][:, :]).then_inc(yt_hi.sem, 1)

            def a_xt(b):
                act.wait_ge(xt_ps.sem, xt_ps.at(b, 1))
                copy(xt[0][:, :], bank[5][:, :]).then_inc(xt_hi.sem, 1)

            def a_v(b, groups):
                for g in groups:
                    act.wait_ge(v_ps.sem, v_ps.at(b, g + 1))
                    copy(vv[0][:, g // 2, 512 * (g % 2):512 * (g % 2) + 512], bank[g % 3][:, :]).then_inc(v_hi.sem, 1)

            act.sem_inc(s_exp.sem, s_exp.credit)
            a_xt(0)
            a_v(0, range(8))
            a_z(0, 0)
            with act.Fori(0, BATCH) as b:
                for h in range(H):
                    if h:
                        a_pt(b, h - 1, 0)
                        a_pt(b, h - 1, 1)
                    a_exp(b, h, 0)
                    if h + 1 < H:
                        a_z(b, h + 1)
                    a_exp(b, h, 1)
                    if h:
                        a_pt(b, h - 1, 2)
                    a_exp(b, h, 2)
                    a_exp(b, h, 3)
                    if h >= 4 and h % 2 == 0:
                        a_yt(b, (h - 4) // 2)
                a_pt(b, H - 1, 0)
                a_pt(b, H - 1, 1)
                a_xt(b + 1)
                a_pt(b, H - 1, 2)
                a_yt(b, PAIRS - 2)
                a_v(b + 1, range(4))
                a_yt(b, PAIRS - 1)
                a_v(b + 1, range(4, 8))
                act.wait_ge(a_ps.sem, a_ps.at(b, 1))
                copy(tail[:, :], wide[:, 512:1024]).then_inc(a_sb.sem, 1)
                a_z(b + 1, 0)
            barrier(act, 2)

            def b_exp(it, j, p):
                q = j * LPAIRS + p
                act.wait_ge(bmax.sem, bmax.at(it, q + 1))
                m0 = 1 if j % NT == 0 else 0
                w = LD * (3 - m0)
                for e in range(2):
                    act.activation(lprob[:, q % 2, m0:3, e, :],
                                   bank[q % 2][:, e * w:(e + 1) * w].rearrange("p (m n) -> p m n", n=LD), ACT.Exp,
                                   bias=lneg[:, q % 4, e:e + 1],
                                   accum_out=lsum[:, j % 2, 2 * p + e:2 * p + e + 1]).then_inc(bexp.sem, 1)

            def b_pt(it, j, p):
                q = j * LPAIRS + p
                m0 = 1 if j == 0 else 0
                act.wait_ge(bpt_ps.sem, bpt_ps.at(it, q + 1))
                copy(lpt[0][:, q % 2, m0:3, :].rearrange("p m n -> p (m n)"),
                     bank[2][:, m0 * P:3 * P]).then_inc(bpt_hi.sem, 1)

            def b_sq(it, j):
                act.wait_ge(bqk_ps.sem, bqk_ps.at(it, j + 1))
                act.wait_ge(p_step.sem, p_step.at(it, POOL_STEPS * j))
                act.activation(sq[:, :], wide[:, :], ACT.Square).then_inc(bsq.sem, 1)

            def b_v(it, j):
                act.wait_ge(bv_ps.sem, bv_ps.at(it, j + 1))
                vp = bank[4][:, :].rearrange("p (c e n) -> p c e n", c=LPAIRS, e=2)
                for r in range(2):
                    for e in range(2):
                        copy(vb[0][DK * e:DK * e + DK, 2 * (j % NT) + r, :, DK * e:DK * e + DK],
                             vp[DK * r:DK * r + DK, :, e, :]).then_inc(bv_hi.sem, 1)

            def b_qt(it, j):
                act.wait_ge(bqt_ps.sem, bqt_ps.at(it, j + 1))
                copy(qt[0][:, j % 2, :, :].rearrange("p c n -> p (c n)"), wide[:, 0:512]).then_inc(bqt_hi.sem, 1)
                for e in range(2):
                    copy(kt[0][DK * e:DK * e + DK, :, e, P * (j % NT):P * (j % NT) + P],
                         wide[DK * e:DK * e + DK, 512:1024].rearrange("p (c n) -> p c n", c=LPAIRS)).then_inc(bqt_hi.sem, 1)

            def b_ot(it, j):
                act.wait_ge(bot_ps.sem, bot_ps.at(it, j + 1))
                copy(ot[0][:, :, P * j:P * j + P], bank[5][:, :].rearrange("p (c n) -> p c n", c=LPAIRS)).then_inc(bot_hi.sem, 1)

            act.sem_inc(bexp.sem, bexp.credit)
            with act.Fori(0, DEPTH) as l:
                act.wait_ge(s_lw, (l + 1) * 16 * 21)
                copy(wl[0][:, :], raw_qkv).then_inc(lay_act, 1)
                copy(wol[0][:, :, :], raw_wo).then_inc(lay_act, 1)
                copy(w2l[0][:, 0:2, :], raw_w2[:, 0:2, :]).then_inc(lay_act, 1)
                copy(w2l[0][0:HC[2][1], 2, :], raw_w2[0:HC[2][1], 2, :]).then_inc(lay_act, 1)
                act.wait_ge(lay_dve, l * 16 + 1)
                copy(w1l[0][:, :], w1g[:, :]).then_inc(lay_act, 1)
                barrier(act, l * 3 + 3)

                def b_xt(it, b):
                    act.wait_ge(bxt_ps.sem, bxt_ps.at(it, b + 1))
                    copy(xt[0][0:DK, :], bank[5][0:DK, :]).then_inc(bh_hi.sem, 1)
                    copy(xt[0][DK:P, 1:T], bank[5][DK:P, 0:T - 1]).then_inc(bh_hi.sem, 1)

                first = (l, 0)
                b_xt(first, 0)
                b_sq(first, 0)
                b_v(first, 0)
                b_sq(first, 1)
                b_v(first, 1)
                b_qt(first, 0)
                b_exp(first, 0, 0)
                with act.Fori(0, BATCH) as b:
                    it = (l, b)
                    for j in range(NT):
                        b_pt(it, j, 0)
                        b_exp(it, j, 1)
                        b_sq(it, j + 2)
                        b_pt(it, j, 1)
                        b_exp(it, j, 2)
                        if j:
                            b_ot(it, j - 1)
                        b_v(it, j + 2)
                        b_pt(it, j, 2)
                        b_exp(it, j, 3)
                        b_qt(it, j + 1)
                        if j == 1:
                            b_xt(it, 1)
                        b_pt(it, j, 3)
                        b_exp(it, j + 1, 0)
                    b_ot(it, NT - 1)
                    act.wait_ge(bo_ps.sem, bo_ps.at(it, 1))
                    copy(tail[:, :], bank[5][:, :]).then_inc(bo_sb.sem, 1)
                barrier(act, l * 3 + 4)
                with act.Fori(0, BATCH) as b:
                    it = l * BATCH + b
                    act.wait_ge(ct_ps.sem, ct_ps.at(it, 1))
                    copy(xt[0][:, :], bank[5][:, :]).then_inc(ct_hi.sem, 1)

                    def c_uhi(n):
                        rows = HC[n][1]
                        act.wait_ge(cu.sem, cu.at(it, n + 1))
                        copy(ut[0][0:rows, n, :], ugl[0:rows, n % 2, :]).then_inc(cu_hi.sem, 1)

                    for n in range(3):
                        rows = HC[n][1]
                        act.wait_ge(cg_ps.sem, cg_ps.at(it, n + 1))
                        act.activation(gel[0:rows, n % 2, :], bank[n % 2][0:rows, :], ACT.Gelu,
                                       bias=b1f[0:rows, 3 + n:4 + n]).then_inc(cgel.sem, 1)
                        if n:
                            c_uhi(n - 1)
                    c_uhi(2)
                    act.wait_ge(co_ps.sem, co_ps.at(it, 1))
                    act.activation(tail[:, :], bank[4][:, :], ACT.Identity, bias=cols[:, 2:3]).then_inc(co_sb.sem, 1)
                barrier(act, l * 3 + 5)

        @block.vector
        def _(dve):
            dve.wait_ge(s_const, 80)
            dve.wait_ge(s_weights, 64)
            dve.wait_ge(pre_act, 4)
            dve.tensor_tensor(wog[1][:, :, :], raw_o, wog[0][:, :, :].bitcast(F32), ALU.subtract).then_inc(pre_dve, 1)
            for n in range(4):
                dve.wait_ge(pre_act, n + 5)
                dve.scalar_tensor_tensor(mh[1][:, 4 * n:4 * n + 4, :].rearrange("p h c -> p (h c)"), bank[n][:, :],
                                         DK ** -0.5, mh[0][:, 4 * n:4 * n + 4, :].rearrange("p h c -> p (h c)").bitcast(F32),
                                         ALU.mult, ALU.subtract).then_inc(pre_dve, 1)
            for n in range(2):
                dve.wait_ge(pre_act, n + 9)
                dve.tensor_tensor(wv[1][:, 512 * n:512 * n + 512], bank[4 + n][:, :],
                                  wv[0][:, 512 * n:512 * n + 512].bitcast(F32), ALU.subtract).then_inc(pre_dve, 1)
            dve.wait_ge(s_x, 16)
            barrier(dve, 1)

            def low(dst, full, high):
                return dve.tensor_tensor(dst, full, high.bitcast(F32) if high.dtype == F32R else high, ALU.subtract)

            def a_max(b, h, j):
                n = h * NT + j
                dve.wait_ge(s_ps.sem, s_ps.at(b, n + 1))
                dve.tensor_reduce(negmax[:, h % 2, j:j + 1], bank[n % 3][:, 0:SW[j]], AX.X, ALU.max,
                                  negate=True).then_inc(s_max.sem, 1)

            def a_pt(b, h, g):
                n = 3 * h + g
                w = P * len(TG[g])
                dve.wait_ge(pt_hi.sem, pt_hi.at(b, n + 1))
                low(pt[1][:, h % 2, 512 * g:512 * g + w], bank[3 + n % 2][:, 0:w],
                    pt[0][:, h % 2, 512 * g:512 * g + w]).then_inc(pt_lo.sem, 1)

            def a_z(b, h):
                dve.wait_ge(z_hi.sem, z_hi.at(b, h + 1))
                low(zt[1][:, h % 2, :], bank[5][:, :], zt[0][:, h % 2, :]).then_inc(z_lo.sem, 1)

            def a_norm(b, p, steps):
                dve.wait_ge(y_ps.sem, y_ps.at(b, p + 1))
                steps.did(dve.reciprocal(rinv[:, :, :], rsum[:, p % 2, :, :]))
                steps.settle()
                dve.tensor_tensor(ysb[:, p % 2, :, :, :].rearrange("p j e n -> p e j n"),
                                  wide[:, 0:512].rearrange("p (e j n) -> p e j n", e=2, j=NT),
                                  rinv[:, :, :, None].to_broadcast([P, 2, NT, DK]), ALU.mult).then_inc(y_norm.sem, 1)

            def a_yt(b, p):
                dve.wait_ge(yt_hi.sem, yt_hi.at(b, p + 1))
                low(yt[1][:, :], bank[5][:, :], yt[0][:, :]).then_inc(yt_lo.sem, 1)

            dve.sem_inc(pt_lo.sem, pt_lo.credit)
            dve.sem_inc(y_norm.sem, y_norm.credit)
            def a_xt(b):
                dve.wait_ge(xt_hi.sem, xt_hi.at(b, 1))
                low(xt[1][:, :], bank[5][:, :], xt[0][:, :]).then_inc(xt_lo.sem, 1)

            def a_v(b, groups):
                for g in groups:
                    dve.wait_ge(v_hi.sem, v_hi.at(b, g + 1))
                    v = [t[:, g // 2, 512 * (g % 2):512 * (g % 2) + 512] for t in vv]
                    low(v[1], bank[g % 3][:, :], v[0]).then_inc(v_lo.sem, 1)

            def ahead(b):
                nsteps = Steps(dve, n_step)
                nsteps.start(b)
                layer_norm(dve, nsteps, lambda j: x1[:, bass.ds(b * NT + j, 1), :].rearrange("p o c -> p (o c)"),
                           n_root, b, 0, lambda j: xh[:, j, :], xh_ready)
                nsteps.end()

            dve.sem_inc(a_left.sem, a_left.credit)
            steps = Steps(dve, a_step)
            ahead(0)
            a_xt(0)
            a_v(0, range(8))
            a_z(0, 0)
            with dve.Fori(0, BATCH) as b:
                steps.start(b)
                here = bass.ds(b * NT, NT)

                def tile_of(t):
                    return lambda j: t[:, bass.ds(b * NT + j, 1), :].rearrange("p o c -> p (o c)")

                def at_step(h):
                    if h and h <= H:
                        a_pt(b, h - 1, 0)
                    if h < H:
                        a_max(b, h, 0)
                    if h and h <= H:
                        a_pt(b, h - 1, 1)
                    if h < H:
                        a_max(b, h, 1)
                    if h + 1 < H:
                        a_z(b, h + 1)
                    if h == H:
                        a_xt(b + 1)
                    if h < H:
                        a_max(b, h, 2)
                    if h and h <= H:
                        a_pt(b, h - 1, 2)
                    if h < H:
                        a_max(b, h, 3)
                    if h >= 4 and h % 2 == 0:
                        a_yt(b, (h - 4) // 2)
                    if h >= 3 and h % 2:
                        a_norm(b, (h - 3) // 2, steps)
                    if h == H // 2:
                        ahead(b + 1)

                for h in range(H + 2):
                    at_step(h)
                a_v(b + 1, range(4))
                a_yt(b, PAIRS - 1)
                a_v(b + 1, range(4, 8))
                a_z(b + 1, 0)
                hold(dve, a_back.sem, a_back.at(b, 1))
                back = bank[5][:, :].rearrange("p (j c) -> p j c", j=NT)
                layer_norm(dve, steps, lambda j: back[:, j, :], a_root, b, 0, lambda j: xn[:, j, :], a_left)
                dve.wait_ge(a_left.sem, a_left.at(b, NT))
                steps.did(dve.tensor_tensor(x1[:, here, :], x1[:, here, :], xn[:, :, :], ALU.add))
                hold(dve, steps.raised.sem, steps.raised.at(steps.it, steps.n))
                layer_norm(dve, steps, tile_of(x1), a_root, b, 1, tile_of(xf), None)
                steps.settle()
                steps.end()
            barrier(dve, 2)

            half = LD // 2

            def b_rot(it, j, part):
                src = wide[:, :].rearrange("p (a h d) -> p a h d", a=2, h=LH)
                ra = rot_a[:, :].rearrange("p (a h d) -> p a h d", a=2, h=LH)
                rb = rot_b[:, :].rearrange("p (a h d) -> p a h d", a=2, h=LH)

                def table(f, lo, hi):
                    return ropes[:, f, j % NT, :, None, lo:hi].to_broadcast([P, 2, LH, hi - lo])

                if part == 0:
                    dve.wait_ge(bsq.sem, bsq.at(it, j + 1))
                    dve.wait_ge(p_step.sem, p_step.at(it, POOL_STEPS * j))
                    dve.tensor_tensor(ra, src, table(0, 0, LD), ALU.mult).then_inc(r_step.sem, 1)
                else:
                    dve.tensor_tensor(rb[:, :, :, 0:half], src[:, :, :, half:LD], table(1, 0, half),
                                      ALU.mult).then_inc(r_step.sem, 1)
                    dve.wait_ge(r_step.sem, r_step.at(it, 2 * j + 2))
                    dve.tensor_tensor(rb[:, :, :, half:LD], src[:, :, :, 0:half], table(1, half, LD),
                                      ALU.mult).then_inc(brot.sem, 1)

            def b_max(it, j, p):
                q = j * LPAIRS + p
                w = P if j % NT == 0 else P + WINDOW
                dve.wait_ge(bs_ps.sem, bs_ps.at(it, q + 1))
                dve.tensor_reduce(lneg[:, q % 4, :], bank[q % 2][:, 0:2 * w].rearrange("p (e n) -> p e n", e=2),
                                  AX.X, ALU.max, negate=True).then_inc(bmax.sem, 1)

            def b_pt(it, j, p):
                q = j * LPAIRS + p
                m0 = 1 if j == 0 else 0
                dve.wait_ge(bpt_hi.sem, bpt_hi.at(it, q + 1))
                v = [t[:, q % 2, m0:3, :].rearrange("p m n -> p (m n)") for t in lpt]
                low(v[1], bank[2][:, m0 * P:3 * P], v[0]).then_inc(bpt_lo.sem, 1)

            def b_v(it, j):
                dve.wait_ge(bv_hi.sem, bv_hi.at(it, 4 * j + 4))
                vp = bank[4][:, :].rearrange("p (c e n) -> p c e n", c=LPAIRS, e=2)
                for r in range(2):
                    for e in range(2):
                        v = [t[DK * e:DK * e + DK, 2 * (j % NT) + r, :, DK * e:DK * e + DK] for t in vb]
                        low(v[1], vp[DK * r:DK * r + DK, :, e, :], v[0]).then_inc(bv_lo.sem, 1)

            def b_qt(it, j):
                dve.wait_ge(bqt_hi.sem, bqt_hi.at(it, 3 * j + 3))
                q = [t[:, j % 2, :, :].rearrange("p c n -> p (c n)") for t in qt]
                low(q[1], wide[:, 0:512], q[0]).then_inc(bqt_lo.sem, 1)
                for e in range(2):
                    k = [t[DK * e:DK * e + DK, :, e, P * (j % NT):P * (j % NT) + P] for t in kt]
                    low(k[1], wide[DK * e:DK * e + DK, 512:1024].rearrange("p (c n) -> p c n", c=LPAIRS), k[0]).then_inc(bqt_lo.sem, 1)

            def b_ot(it, j):
                dve.wait_ge(bot_hi.sem, bot_hi.at(it, j + 1))
                o = [t[:, :, P * j:P * j + P] for t in ot]
                low(o[1], bank[5][:, :].rearrange("p (c n) -> p c n", c=LPAIRS), o[0]).then_inc(bot_lo.sem, 1)

            def b_norm(it, j, steps):
                dve.wait_ge(by_ps.sem, by_ps.at(it, j + 1))
                steps.did(dve.reciprocal(linv[:, :], lsum[:, j % 2, :]))
                steps.settle()
                dve.tensor_tensor(osb[:, j % 2, :].rearrange("p (h d) -> p h d", d=LD),
                                  ypart[:, :].rearrange("p (h d) -> p h d", d=LD),
                                  linv[:, :, None].to_broadcast([P, LH, LD]), ALU.mult).then_inc(by_norm.sem, 1)

            for s in (bv_lo, bpt_lo, by_norm, bx, chn, cu, cx):
                dve.sem_inc(s.sem, s.credit)
            bsteps, csteps, dsteps = Steps(dve, o_step), Steps(dve, c_step), Steps(dve, d_step)
            with dve.Fori(0, DEPTH) as l:
                dve.wait_ge(s_lw, (l + 1) * 16 * 21)
                dve.tensor_scalar(w1g[:, :], raw_w1, cols[:, 0:1], None, ALU.mult).then_inc(lay_dve, 1)
                n = 1
                for f in range(2):
                    for j in range(NT):
                        dve.tensor_tensor(ropes[:, f, j, :, :], rope[:, f, j, :, :], qks[:, f, :, :], ALU.mult).then_inc(lay_dve, 1)
                        n += 1
                for k, (full, pair) in enumerate(((raw_qkv, cut(wl, lambda t: t[:, :])),
                                                  (raw_wo, cut(wol, lambda t: t[:, :, :])),
                                                  (raw_w2[:, 0:2, :], cut(w2l, lambda t: t[:, 0:2, :])),
                                                  (raw_w2[0:HC[2][1], 2, :], cut(w2l, lambda t: t[0:HC[2][1], 2, :])),
                                                  (w1g[:, :], cut(w1l, lambda t: t[:, :])))):
                    dve.wait_ge(lay_act, l * 5 + (k + 1))
                    low(pair[1], full, pair[0]).then_inc(lay_dve, 1)
                    n += 1
                dve.wait_ge(lay_pe, l + 1)
                for c0, r in ((0, P), (2, HC[2][1])):
                    w = 2 if c0 == 0 else 1
                    dve.tensor_tensor(b1f[0:r, :].rearrange("p (a c) -> p a c", a=2)[:, :, c0:c0 + w],
                                      bank[0][0:r, 0:6].rearrange("p (a c) -> p a c", a=2)[:, :, c0:c0 + w],
                                      cols[0:r, 3:9].rearrange("p (a c) -> p a c", a=2)[:, :, c0:c0 + w],
                                      ALU.add).then_inc(lay_dve, 1)
                    n += 1
                assert n == 16
                barrier(dve, l * 3 + 3)

                def b_xt(it, b):
                    dve.wait_ge(bh_hi.sem, bh_hi.at(it, 2 * b + 2))
                    low(xt[1][0:DK, :], bank[5][0:DK, :], xt[0][0:DK, :]).then_inc(bh_lo.sem, 1)
                    low(xt[1][DK:P, 1:T], bank[5][DK:P, 0:T - 1], xt[0][DK:P, 1:T]).then_inc(bh_lo.sem, 1)

                first = (l, 0)
                b_xt(first, 0)
                for j in range(2):
                    b_rot(first, j, 0)
                    b_rot(first, j, 1)
                    b_v(first, j)
                b_qt(first, 0)
                b_max(first, 0, 0)
                with dve.Fori(0, BATCH) as b:
                    it = (l, b)
                    bsteps.start(it)
                    here = bass.ds(b * NT, NT)
                    for j in range(NT):
                        b_max(it, j, 1)
                        b_pt(it, j, 0)
                        b_rot(it, j + 2, 0)
                        b_max(it, j, 2)
                        b_pt(it, j, 1)
                        if j:
                            b_ot(it, j - 1)
                        b_rot(it, j + 2, 1)
                        b_max(it, j, 3)
                        b_pt(it, j, 2)
                        b_v(it, j + 2)
                        b_qt(it, j + 1)
                        if j == 1:
                            b_xt(it, 1)
                        b_pt(it, j, 3)
                        b_max(it, j + 1, 0)
                        b_norm(it, j, bsteps)
                    bsteps.end()
                    b_ot(it, NT - 1)
                    dve.wait_ge(bo_back.sem, bo_back.at(it, 1))
                    dve.tensor_tensor(xf[:, here, :], bank[5][:, :].rearrange("p (j c) -> p j c", j=NT),
                                      xf[:, here, :], ALU.add).then_inc(bx.sem, 1)
                barrier(dve, l * 3 + 4)
                with dve.Fori(0, BATCH) as b:
                    it = l * BATCH + b
                    csteps.start(it)
                    here = bass.ds(b * NT, NT)
                    dve.wait_ge(chs.sem, chs.at(it, 1))
                    hold(dve, chs_dma.sem, chs_dma.at(it, 32))
                    layer_norm(dve, csteps, lambda j: hs[:, j, :], c_root, it, 0, lambda j: xh[:, j, :], chn)
                    csteps.end()
                    dve.wait_ge(ct_hi.sem, ct_hi.at(it, 1))
                    low(xt[1][:, :], bank[5][:, :], xt[0][:, :]).then_inc(ct_lo.sem, 1)
                    for n in range(3):
                        rows = HC[n][1]
                        dve.wait_ge(cgel.sem, cgel.at(it, n + 1))
                        dve.wait_ge(ca_ps.sem, ca_ps.at(it, n + 1))
                        if n == 2:
                            dve.wait_ge(cu_lo.sem, cu_lo.at(it, 1))
                        dve.scalar_tensor_tensor(ugl[0:rows, n % 2, :], bank[2 + n % 2][0:rows, :], b1f[0:rows, n:n + 1],
                                                 gel[0:rows, n % 2, :], ALU.add, ALU.mult).then_inc(cu.sem, 1)
                    dve.wait_ge(co_back.sem, co_back.at(it, 1))
                    dve.tensor_tensor(xf[:, here, :], bank[5][:, :].rearrange("p (j c) -> p j c", j=NT),
                                      xf[:, here, :], ALU.add).then_inc(cx.sem, 1)
                barrier(dve, l * 3 + 5)
            with dve.Fori(0, BATCH) as b:
                dsteps.start(b)
                here = bass.ds(b * NT, NT)
                layer_norm(dve, dsteps, lambda j: xf[:, bass.ds(b * NT + j, 1), :].rearrange("p o c -> p (o c)"), d_root, b, 0,
                           lambda j: xh[:, j, :], None)
                dsteps.settle()
                dsteps.end()
                dve.tensor_tensor(x1[:, here, :], x1[:, here, :], xh[:, :, :], ALU.add).then_inc(d_out.sem, 1)
                dve.wait_ge(d_out.sem, d_out.at(b, 1))

        @block.tensor
        def _(pe):
            pe.wait_ge(s_const, 80)
            pe.wait_ge(s_weights, 64)
            for n in range(4):
                for k in range(4):
                    h = 4 * n + k
                    mm = pe.matmul(bank[n][:, P * k:P * k + P], raw_q[:, h, :], raw_k[:, h, :], start=True, stop=True)
                mm.then_inc(pre_pe, 1)
            for n in range(2):
                for k in range(4):
                    mm = pe.transpose(bank[4 + n][:, P * k:P * k + P], raw_v[:, 4 * n + k, :], ident[:, :])
                mm.then_inc(pre_pe, 1)
            barrier(pe, 1)

            def a_z(b, h, first_free):
                pe.wait_ge(*first_free)
                three(pe, bank[5][:, :], cut(mh, lambda t: t[:, h, :]), cut(xt, lambda t: t[:, :])).then_inc(z_ps.sem, 1)

            def a_scores(b, h, j):
                n = h * NT + j
                if n >= 3:
                    pe.wait_ge(s_exp.sem, s_exp.at(b, n - 2))
                if n == 0:
                    pe.wait_ge(v_lo.sem, v_lo.at(b, 8))
                if j == 0:
                    pe.wait_ge(z_lo.sem, z_lo.at(b, h + 1))
                acc = bank[n % 3]
                z = cut(zt, lambda t: t[:, h % 2, P * j:P * j + P])
                three(pe, acc[:, 0:SW[j]], z, cut(xt, lambda t: t[:, 0:SW[j]]), stop=False)
                pe.matmul(acc[:, SW[j] - P:SW[j]], ident16[:, :], causal[:, :], start=False, stop=True).then_inc(s_ps.sem, 1)

            def a_turn(b, h, g):
                n = 3 * h + g
                pe.wait_ge(s_exp.sem, s_exp.at(b, NT * h + TG_NEEDS[g] + 1))
                pe.wait_ge(pt_lo.sem, pt_lo.at(b, n - 1))
                for k, (i, j) in enumerate(TG[g]):
                    mm = pe.transpose(bank[3 + n % 2][:, P * k:P * k + P],
                                      prob[:, h % 2, SO[j] + P * i:SO[j] + P * i + P], ident[:, :])
                mm.then_inc(pt_ps.sem, 1)

            def a_pv(b, h):
                if h % 2 == 0:
                    pe.wait_ge(y_norm.sem, y_norm.at(b, h // 2))
                pe.wait_ge(pt_lo.sem, pt_lo.at(b, 3 * h + 3))
                for j in range(NT):
                    for i in range(j + 1):
                        at = TO[(i, j)]
                        acc = wide[:, 256 * (h % 2) + DK * j:256 * (h % 2) + DK * j + DK]
                        mm = three(pe, acc, cut(pt, lambda t: t[:, h % 2, at:at + P]),
                                   cut(vv, lambda t: t[:, i, DK * h:DK * h + DK]), start=i == 0, stop=i == j)
                if h % 2:
                    mm.then_inc(y_ps.sem, 1)

            def a_yturn(b, p, first_free):
                pe.wait_ge(*first_free)
                pe.wait_ge(y_norm.sem, y_norm.at(b, p + 1))
                for j in range(NT):
                    mm = pe.transpose(bank[5][:, P * j:P * j + P],
                                      ysb[:, p % 2, j, :, :].rearrange("p e n -> p (e n)"), ident[:, :])
                mm.then_inc(yt_ps.sem, 1)

            def a_out(b, p):
                pe.wait_ge(yt_lo.sem, yt_lo.at(b, p + 1))
                mm = three(pe, wide[:, 512:1024], cut(wog, lambda t: t[:, p, :]), cut(yt, lambda t: t[:, :]),
                           start=p == 0, stop=p == PAIRS - 1)
                if p == PAIRS - 1:
                    mm.then_inc(a_ps.sem, 1)

            def a_xt(b):
                pe.wait_ge(xh_ready.sem, xh_ready.at(b, NT))
                for j in range(NT):
                    mm = pe.transpose(bank[5][:, P * j:P * j + P], xh[:, j, :], ident[:, :])
                mm.then_inc(xt_ps.sem, 1)

            def a_v(b, groups):
                for g in groups:
                    if g == 0:
                        pe.wait_ge(xt_lo.sem, xt_lo.at(b, 1))
                    if g >= 3:
                        pe.wait_ge(v_lo.sem, v_lo.at(b, g - 2))
                    i, n0 = g // 2, 512 * (g % 2)
                    three(pe, bank[g % 3][:, :], cut(xt, lambda t: t[:, P * i:P * i + P]),
                          cut(wv, lambda t: t[:, n0:n0 + 512])).then_inc(v_ps.sem, 1)

            a_xt(0)
            a_v(0, range(8))
            a_z(0, 0, (xt_lo.sem, xt_lo.at(0, 1)))
            with pe.Fori(0, BATCH) as b:
                for h in range(H):
                    if h:
                        a_turn(b, h - 1, 0)
                        a_turn(b, h - 1, 1)
                    a_scores(b, h, 0)
                    a_scores(b, h, 1)
                    if h + 1 < H:
                        a_z(b, h + 1, (a_left.sem, a_left.at(b, 0)) if h == 0 else
                            (yt_lo.sem, yt_lo.at(b, (h - 5) // 2 + 1)) if h >= 5 and h % 2 else
                            (z_lo.sem, z_lo.at(b, h + 1)))
                    a_scores(b, h, 2)
                    if h:
                        a_turn(b, h - 1, 2)
                    a_scores(b, h, 3)
                    if h >= 2:
                        a_pv(b, h - 2)
                    if h >= 4 and h % 2 == 0:
                        a_yturn(b, (h - 4) // 2, (z_lo.sem, z_lo.at(b, min(h + 2, H))))
                    if h >= 5 and h % 2:
                        a_out(b, (h - 5) // 2)
                a_turn(b, H - 1, 0)
                a_turn(b, H - 1, 1)
                pe.wait_ge(yt_lo.sem, yt_lo.at(b, PAIRS - 2))
                a_xt(b + 1)
                a_turn(b, H - 1, 2)
                a_pv(b, H - 2)
                a_yturn(b, PAIRS - 2, (xt_lo.sem, xt_lo.at(b + 1, 1)))
                a_pv(b, H - 1)
                a_out(b, PAIRS - 2)
                a_v(b + 1, range(4))
                a_yturn(b, PAIRS - 1, (yt_lo.sem, yt_lo.at(b, PAIRS - 1)))
                a_v(b + 1, range(4, 8))
                a_out(b, PAIRS - 1)
                a_z(b + 1, 0, (yt_lo.sem, yt_lo.at(b, PAIRS)))
                pe.wait_ge(a_sb.sem, a_sb.at(b, 1))
                pe.wait_ge(z_lo.sem, z_lo.at(b + 1, 1))
                for j in range(NT):
                    mm = pe.transpose(bank[5][:, P * j:P * j + P], tail[:, P * j:P * j + P], ident[:, :])
                mm.then_inc(a_back.sem, 1)
            barrier(pe, 2)

            def b_qk(it, j):
                h = cut(xt, lambda t: t[:, P * (j % NT):P * (j % NT) + P])
                if isinstance(it[1], int) and j == 1:
                    pe.wait_ge(brot.sem, brot.at(it, 1))
                elif j >= 2:
                    pe.wait_ge(bqt_lo.sem, bqt_lo.at(it, 3 * (j - 1)))
                for n in range(2):
                    mm = three(pe, wide[:, 512 * n:512 * n + 512], h, cut(wl, lambda t: t[:, 512 * n:512 * n + 512]))
                mm.then_inc(bqk_ps.sem, 1)

            def b_v(it, j):
                h = cut(xt, lambda t: t[:, P * (j % NT):P * (j % NT) + P])
                pe.wait_ge(bv_lo.sem, bv_lo.at(it, 4 * (j - 1) + 4))
                three(pe, bank[4][:, :], h, cut(wl, lambda t: t[:, 1024:1536])).then_inc(bv_ps.sem, 1)

            def b_turn(it, j):
                pe.wait_ge(bqk.sem, bqk.at(it, j + 1))
                pe.wait_ge(brot.sem, brot.at(it, j + 2))
                for n in range(8):
                    mm = pe.transpose(wide[:, P * n:P * n + P], qk[j % 2][:, P * n:P * n + P], ident[:, :])
                mm.then_inc(bqt_ps.sem, 1)

            def b_scores(it, j, p):
                q = j * LPAIRS + p
                if p == 0:
                    pe.wait_ge(bqt_lo.sem, bqt_lo.at(it, 3 * j + 3))
                pe.wait_ge(bexp.sem, bexp.at(it, 2 * q - 2))
                k0, w = (0, P) if j % NT == 0 else (P * (j % NT) - WINDOW, P + WINDOW)
                acc = bank[q % 2][:, 0:2 * w].rearrange("p (e n) -> p e n", e=2)
                three(pe, acc, cut(qt, lambda t: t[:, j % 2, p, :]), cut(kt, lambda t: t[:, p, :, k0:k0 + w]), stop=False)
                pe.matmul(acc, ident16[:, :], band[:, :, P + WINDOW - w:], start=False, stop=True).then_inc(bs_ps.sem, 1)

            def b_pt(it, j, p):
                q = j * LPAIRS + p
                m0 = 1 if j == 0 else 0
                pe.wait_ge(bexp.sem, bexp.at(it, 2 * q + 2))
                pe.wait_ge(bpt_lo.sem, bpt_lo.at(it, q))
                for m in range(m0, 3):
                    mm = pe.transpose(bank[2][:, P * m:P * m + P],
                                      lprob[:, q % 2, m, :, :].rearrange("p e n -> p (e n)"), ident[:, :])
                mm.then_inc(bpt_ps.sem, 1)

            def b_pv(it, j, p):
                q = j * LPAIRS + p
                m0 = 1 if j == 0 else 0
                pe.wait_ge(bpt_lo.sem, bpt_lo.at(it, q + 1))
                pe.wait_ge(bv_lo.sem, bv_lo.at(it, 4 * j + 4))
                if p == 0:
                    pe.wait_ge(by_norm.sem, by_norm.at(it, j))
                for m in range(m0, 3):
                    mm = three(pe, ypart[:, P * p:P * p + P], cut(lpt, lambda t: t[:, q % 2, m, :]),
                               cut(vb, lambda t: t[:, 2 * j - 1 + m, p, :]), start=m == m0, stop=m == 2)
                if p == LPAIRS - 1:
                    mm.then_inc(by_ps.sem, 1)

            def b_ot(it, j):
                pe.wait_ge(by_norm.sem, by_norm.at(it, j + 1))
                if j:
                    pe.wait_ge(bot_lo.sem, bot_lo.at(it, j))
                if j == 1:
                    pe.wait_ge(bh_lo.sem, bh_lo.at(it, 4))
                for n in range(LPAIRS):
                    mm = pe.transpose(bank[5][:, P * n:P * n + P], osb[:, j % 2, P * n:P * n + P], ident[:, :])
                mm.then_inc(bot_ps.sem, 1)

            with pe.Fori(0, DEPTH) as l:
                pe.wait_ge(s_lw, (l + 1) * 16 * 21)
                for n in range(6):
                    r0, rows = HC[n % 3]
                    r0 += HID * (n // 3)
                    mm = pe.matmul(bank[0][0:rows, n:n + 1], raw_w1[:, r0:r0 + rows], cols[:, 1:2], start=True, stop=True)
                mm.then_inc(lay_pe, 1)
                barrier(pe, l * 3 + 3)

                def b_xt(it, b):
                    pe.wait_ge(bxs.sem, bxs.at(it, b + 1))
                    for j in range(NT):
                        mm = pe.transpose(bank[5][:, P * j:P * j + P], xs[:, j, :], ident[:, :])
                    mm.then_inc(bxt_ps.sem, 1)

                first = (l, 0)
                b_xt(first, 0)
                pe.wait_ge(bh_lo.sem, bh_lo.at(first, 2))
                b_qk(first, 0)
                b_v(first, 0)
                b_qk(first, 1)
                b_v(first, 1)
                b_turn(first, 0)
                b_scores(first, 0, 0)
                with pe.Fori(0, BATCH) as b:
                    it = (l, b)
                    for j in range(NT):
                        b_pt(it, j, 0)
                        b_scores(it, j, 1)
                        if j == 2:
                            pe.wait_ge(bh_lo.sem, bh_lo.at(it, 4))
                        b_qk(it, j + 2)
                        b_pt(it, j, 1)
                        b_scores(it, j, 2)
                        b_pv(it, j, 0)
                        if j:
                            if j == 1:
                                pe.wait_ge(bx.sem, bx.at((l, b), 0))
                            b_ot(it, j - 1)
                        b_v(it, j + 2)
                        b_pt(it, j, 2)
                        b_scores(it, j, 3)
                        b_pv(it, j, 1)
                        b_turn(it, j + 1)
                        if j == 1:
                            pe.wait_ge(bot_lo.sem, bot_lo.at(it, 1))
                            b_xt(it, 1)
                        b_pt(it, j, 3)
                        b_pv(it, j, 2)
                        b_scores(it, j + 1, 0)
                        b_pv(it, j, 3)
                    b_ot(it, NT - 1)
                    pe.wait_ge(bot_lo.sem, bot_lo.at(it, NT))
                    for n in range(LPAIRS):
                        mm = three(pe, bank[5][:, :], cut(wol, lambda t: t[:, n, :]), cut(ot, lambda t: t[:, n, :]),
                                   start=n == 0, stop=n == LPAIRS - 1)
                    mm.then_inc(bo_ps.sem, 1)
                    pe.wait_ge(bo_sb.sem, bo_sb.at(it, 1))
                    for j in range(NT):
                        mm = pe.transpose(bank[5][:, P * j:P * j + P], tail[:, P * j:P * j + P], ident[:, :])
                    mm.then_inc(bo_back.sem, 1)
                barrier(pe, l * 3 + 4)
                with pe.Fori(0, BATCH) as b:
                    it = l * BATCH + b
                    pe.wait_ge(chn.sem, chn.at(it, NT))
                    pe.wait_ge(cx.sem, cx.at(it, 0))
                    for j in range(NT):
                        mm = pe.transpose(bank[5][:, P * j:P * j + P], xh[:, j, :], ident[:, :])
                    mm.then_inc(ct_ps.sem, 1)
                    pe.wait_ge(ct_lo.sem, ct_lo.at(it, 1))
                    for n in range(3):
                        r0, rows = HC[n]
                        if n == 2:
                            pe.wait_ge(cu.sem, cu.at(it, 1))
                        for a, s in ((HID, cg_ps), (0, ca_ps)):
                            acc = bank[(0 if a else 2) + n % 2][0:rows, :]
                            three(pe, acc, cut(w1l, lambda t: t[:, a + r0:a + r0 + rows]),
                                  cut(xt, lambda t: t[:, :])).then_inc(s.sem, 1)
                    for n in range(3):
                        rows = HC[n][1]
                        pe.wait_ge(cu_lo.sem, cu_lo.at(it, n + 1))
                        mm = three(pe, bank[4][:, :], cut(w2l, lambda t: t[0:rows, n, :]),
                                   cut(ut, lambda t: t[0:rows, n, :]), start=n == 0, stop=n == 2)
                    mm.then_inc(co_ps.sem, 1)
                    pe.wait_ge(co_sb.sem, co_sb.at(it, 1))
                    for j in range(NT):
                        mm = pe.transpose(bank[5][:, P * j:P * j + P], tail[:, P * j:P * j + P], ident[:, :])
                    mm.then_inc(co_back.sem, 1)
                barrier(pe, l * 3 + 5)


def rope_tables():
    f = np.float32
    half = np.arange(0, LD, 2, dtype=f)
    t = np.arange(T, dtype=f)
    freqs = t[:, None] * (f(1.0) / f(10000.0) ** (half / f(LD)))[None, :]
    power = (t - T // 2) / f(WINDOW // 2)
    scale = ((half + f(0.4 * LD)) / f(1.4 * LD))[None, :] ** power[:, None]
    both = lambda a: np.concatenate([a, a], axis=-1)
    cos, sin, scale = both(np.cos(freqs)), both(np.sin(freqs)), both(scale)
    sin[:, :LD // 2] *= -1
    return [np.stack([a * scale * f(8.0), a / scale], axis=1).astype(f) for a in (cos, sin)]


def constants():
    i, c = np.arange(P)[:, None], np.arange(P + WINDOW)[None, :]
    causal = np.where(np.arange(P)[None, :] > i, MASKED, 0.0).astype(np.float32)
    band = np.where((c >= i) & (c <= i + WINDOW), 0.0, MASKED).astype(np.float32)
    cos, sin = rope_tables()
    return {"ident": np.eye(P, dtype=np.float32), "causal": causal, "band": np.concatenate([band, band], axis=1),
            "rope_cos": cos, "rope_sin": sin}


_INS = ["L0_attn_x", "L0_attn_w_q", "L0_attn_w_k", "L0_attn_w_v", "L0_attn_w_o", "L0_ffn_wqkv", "L0_ffn_q_scale",
        "L0_ffn_k_scale", "L0_ffn_wo", "L0_ffn_ln_g", "L0_ffn_ln_b", "L0_ffn_w1", "L0_ffn_b1", "L0_ffn_w2", "L0_ffn_b2"]


def kernel(**inputs):
    import concourse.bacc as _bacc
    from concourse.bass_utils import run_bass_kernel_spmd as _run

    nc = _bacc.Bacc("TRN2", target_bir_lowering=False, num_devices=1)
    arrays, args = {}, []
    given = {**{n: inputs[n] for n in _INS}, **constants()}
    for name, a in given.items():
        a = np.ascontiguousarray(a)
        arrays[f"in_{name}"] = a
        args.append(nc.dram_tensor(f"in_{name}", a.shape, mybir.dt.from_np(a.dtype), kind="ExternalInput").ap())
    args.append(nc.dram_tensor("out_0", (BATCH, T, C), F32, kind="ExternalOutput").ap())
    sandwich(nc, *args)
    r = _run(nc, [arrays], core_ids=[0])
    return r.results[0]["out_0"]
```

```python
from contextlib import ExitStack

import numpy as np

import concourse.bass as bass
from concourse import mybir

F32 = mybir.dt.float32
F32R = mybir.dt.float32r
F16 = mybir.dt.float16
BF16 = mybir.dt.bfloat16
ALU = mybir.AluOpType
ACT = mybir.ActivationFunctionType
AX = mybir.AxisListType

P = 128
BATCH, T, C = 8, 512, 128
NT = T // P
H, DK = 16, 64
PAIRS = H // 2
DEPTH = 2
LH, LD = 8, 64
LPAIRS = LH // 2
INNER = LH * LD
WINDOW = 64
HID = int(C * 4 * 2 / 3)
HC = [(0, 128), (128, 128), (256, HID - 256)]
EPS = 1e-5
MASKED = -1e30

SW = [P * (j + 1) for j in range(NT)]
SO = [sum(SW[:j]) for j in range(NT)]
SCORES = sum(SW)
TG = [[(0, 0), (0, 1), (1, 1), (0, 2)], [(1, 2), (2, 2), (0, 3), (1, 3)], [(2, 3), (3, 3)]]
TG_NEEDS = [max(j for _, j in blks) for blks in TG]
TO = {blk: 512 * g + P * n for g, blks in enumerate(TG) for n, blk in enumerate(blks)}


LAYER_STEPS = 23
POOL_STEPS = 5


class Signal:

    def __init__(self, nc, ctx, name, per, credit=0, over=0):
        self.sem, self.per, self.credit, self.over = ctx.enter_context(nc.semaphore(name)), per, credit, over

    def at(self, it, n):
        if isinstance(it, tuple):
            l, b = it
            return l * (BATCH * self.per + self.over) + b * self.per + (n + self.credit)
        return it * self.per + (n + self.credit)


class Steps:

    def __init__(self, eng, raised):
        self.eng, self.raised, self.n, self.it = eng, raised, 0, 0

    def start(self, it):
        self.it, self.n = it, 0

    def did(self, ins):
        ins.then_inc(self.raised.sem, 1)
        self.n += 1

    def settle(self):
        self.eng.wait_ge(self.raised.sem, self.raised.at(self.it, self.n))

    def end(self):
        assert self.n == self.raised.per, (self.n, self.raised.per)


def sandwich(nc, x, w_q, w_k, w_v, w_o, wqkv, q_scale, k_scale, wo, ln_g, ln_b, w1, b1, w2, b2,
             ident_c, causal_c, band_c, rope_cos_c, rope_sin_c, out):
    ctx = ExitStack()
    with ctx:
        def sb(name, shape, dt=F32):
            return ctx.enter_context(nc.sbuf_tensor(name, shape, dt))

        def sem(name):
            return ctx.enter_context(nc.semaphore(name))

        def sig(name, per, credit=0, over=0):
            return Signal(nc, ctx, name, per, credit, over)

        bank = [ctx.enter_context(nc.psum_tensor(f"bank{i}", [P, 512], F32)) for i in range(6)]
        wide = ctx.enter_context(nc.psum_tensor("wide", [P, 1024], F32))

        ypart = bank[3]

        x1 = sb("x1", [P, (BATCH + 1) * NT, C])
        xf = sb("xf", [P, (BATCH + 2) * NT, C])
        ident = sb("ident", [P, P])
        ident16 = sb("ident16", [P, P], BF16)
        causal = sb("causal", [P, P], BF16)
        band = sb("band", [P, 2, P + WINDOW], BF16)
        rope = sb("rope", [P, 2, NT, 2, LD])
        ropes = sb("ropes", [P, 2, NT, 2, LD])
        qks = sb("qks", [P, 2, 2, LD])
        stage = sb("stage", [P, 4096])

        big = [sb(f"big{n}", [P, 4096], F32R) for n in range(2)]
        mh = [big[0][:, H * C * n:H * C * (n + 1)].rearrange("p (h c) -> p h c", h=H) for n in range(2)]
        wv = [big[1][:, H * DK * n:H * DK * (n + 1)] for n in range(2)]
        wog = [big[1][:, 1024 * (2 + n):1024 * (3 + n)].rearrange("p (g c) -> p g c", g=PAIRS) for n in range(2)]
        wl = [sb(f"wqkv_{s}", [P, 3 * INNER], F32R) for s in ("hi", "lo")]
        wol = [sb(f"wol_{s}", [P, LPAIRS, C], F32R) for s in ("hi", "lo")]
        w1l = [sb(f"w1_{s}", [P, 2 * HID], F32R) for s in ("hi", "lo")]
        w2l = [sb(f"w2_{s}", [P, 3, C], F32R) for s in ("hi", "lo")]
        w1g = sb("w1g", [P, 2 * HID])
        cols_raw = sb("cols_raw", [P, 9])
        cols = sb("cols", [P, 9])
        b1f = sb("b1f", [P, 6])

        stats = sb("stats", [P, NT, 6])
        mv = sb("mv", [P, NT, 2])
        vare = sb("vare", [P, NT])
        rstd = sb("rstd", [P, NT])
        mhalf = sb("mhalf", [P, 2 * LH])
        xh = sb("xh", [P, NT, C])
        xn = sb("xn", [P, NT, C])
        xt = [sb(f"xt_{s}", [P, T], F32R) for s in ("hi", "lo")]
        mid = [sb(f"mid{n}", [P, 2048], F32R) for n in range(2)]
        zt = [mid[0][:, 1024 * n:1024 * n + 1024].rearrange("p (a t) -> p a t", a=2) for n in range(2)]
        negmax = sb("negmax", [P, 2, NT])
        rsum = sb("rsum", [P, 2, 2, NT])
        rinv = sb("rinv", [P, 2, NT])
        yt = [mid[1][:, T * n:T * n + T] for n in range(2)]
        work = sb("work", [P, 4 * SCORES])
        prob = work[:, 0:2 * SCORES].rearrange("p (a n) -> p a n", a=2)
        pt = [work[:, (2 + n) * SCORES:(3 + n) * SCORES].bitcast(F16).rearrange("p (a n) -> p a n", a=2)
              for n in range(2)]
        vv = [sb(f"v_{s}", [P, NT, H * DK], F16) for s in ("hi", "lo")]
        ysb = sb("ysb", [P, 2, NT, 2, DK])
        tail = sb("tail", [P, T])

        xs = xh
        sq, rot_a, rot_b, qk0 = (work[:, 2 * INNER * n:2 * INNER * (n + 1)] for n in range(4))
        qk1 = sb("qk1", [P, 2 * INNER])
        qk = (qk0, qk1)
        ssq = sb("ssq", [P, 2 * LH])
        ssqc = sb("ssqc", [P, 2 * LH])
        rnorm = sb("rnorm", [P, 2 * LH])
        qt = [sb(f"qt_{s}", [P, 2, LPAIRS, P], F32R) for s in ("hi", "lo")]
        kt = [big[n][:, :].rearrange("p (c e t) -> p c e t", c=LPAIRS, e=2) for n in range(2)]
        vb = [v[:, :, :].rearrange("p t (a c n) -> p (t a) c n", a=2, c=LPAIRS) for v in vv]
        lprob = work[:, 8 * INNER:8 * INNER + 12 * LD].rearrange("p (a m e n) -> p a m e n", a=2, m=3, e=2)
        lpt = [sb(f"lpt_{s}", [P, 2, 3, P], F16) for s in ("hi", "lo")]
        lneg = sb("lneg", [P, 4, 2])
        lsum = sb("lsum", [P, 2, LH])
        linv = sb("linv", [P, LH])
        osb = ysb[:, :, :, :, :].rearrange("p a j e n -> p a (j e n)")
        ot = [mid[n][:, :].rearrange("p (c t) -> p c t", c=LPAIRS) for n in range(2)]

        hs = sb("hs", [P, NT, C])
        gel = prob[:, 0, 0:1024].rearrange("p (a n) -> p a n", a=2)
        ugl = prob[:, 1, 0:1024].rearrange("p (a n) -> p a n", a=2)
        ut = [mid[n][:, 0:3 * T].rearrange("p (c t) -> p c t", c=3) for n in range(2)]

        mean_out, vare_out, rstd_out = (stage[:, 512 * n:512 * n + BATCH * NT] for n in range(3))

        phase, held = sem("phase"), sem("held")
        s_qk, s_x0, s_rope = sem("qk_loaded"), sem("x0_loaded"), sem("rope_loaded")
        s_x, s_const, s_weights, s_out = sem("x_loaded"), sem("const_loaded"), sem("weights_loaded"), sem("out_stored")
        s_lw = sem("layer_weights_loaded")
        pre_pe, pre_act, pre_dve, pre_pool = sem("pre_pe"), sem("pre_act"), sem("pre_dve"), sem("pre_pool")
        lay_pe, lay_act, lay_dve = sem("lay_pe"), sem("lay_act"), sem("lay_dve")
        n_step = sig("n_step", 2 * NT)
        a_step = sig("a_step", 2 * NT * 2 + NT + 1)
        a_left = sig("a_left", NT, NT)
        xh_ready, xt_ps, xt_hi, xt_lo = sig("xh_ready", NT), sig("xt_ps", 1), sig("xt_hi", 1), sig("xt_lo", 1)
        v_ps, v_hi, v_lo = sig("v_ps", 8), sig("v_hi", 8), sig("v_lo", 8)
        z_ps, z_hi, z_lo = sig("z_ps", H), sig("z_hi", H), sig("z_lo", H)
        s_ps, s_max, s_exp = sig("scores_ps", H * NT), sig("scores_max", H * NT), sig("probs_ready", H * NT, H * NT)
        pt_ps, pt_hi, pt_lo = sig("pt_ps", 3 * H), sig("pt_hi", 3 * H), sig("pt_lo", 3 * H, 3 * H)
        rinv_ready = sig("rinv_ready", PAIRS)
        y_ps, y_norm = sig("y_ps", PAIRS), sig("y_norm", PAIRS, PAIRS)
        yt_ps, yt_hi, yt_lo = sig("yt_ps", PAIRS), sig("yt_hi", PAIRS), sig("yt_lo", PAIRS)
        a_ps, a_sb, a_back = sig("a_ps", 1), sig("a_sb", 1), sig("a_back", 1)
        r_step = sig("r_step", 2 * NT, over=7)
        o_step = sig("o_step", NT)
        p_step = sig("p_step", POOL_STEPS * NT, POOL_STEPS, over=3 * POOL_STEPS)
        bxs, bxt_ps = sig("bxs", 16, over=16), sig("bxt_ps", 1, over=1)
        bh_hi, bh_lo = sig("bh_hi", 2, over=2), sig("bh_lo", 2, over=2)
        bqk_ps, bv_ps, bsq = sig("bqk_ps", NT, over=4), sig("bv_ps", NT, over=3), sig("bsq", NT, over=4)
        bssq = sig("bssq", NT, 1, over=3)
        brot, bqk = sig("brot", NT, over=3), sig("bqk", NT, over=3)
        bqt_ps, bqt_hi = sig("bqt_ps", NT, over=2), sig("bqt_hi", 3 * NT, over=6)
        bqt_lo = sig("bqt_lo", 3 * NT, over=6)
        bv_hi, bv_lo = sig("bv_hi", 4 * NT, over=12), sig("bv_lo", 4 * NT, 4, over=12)
        bs_ps, bmax, bexp = sig("bs_ps", 16, over=6), sig("bmax", 16, over=6), sig("bexp", 32, 4, over=10)
        bpt_ps, bpt_hi, bpt_lo = sig("bpt_ps", 16, over=4), sig("bpt_hi", 16, over=4), sig("bpt_lo", 16, 2, over=4)
        by_ps, by_norm = sig("by_ps", 16, 2, over=2), sig("by_norm", NT, NT)
        bot_ps, bot_hi, bot_lo = sig("bot_ps", NT), sig("bot_hi", NT), sig("bot_lo", NT)
        bo_ps, bo_sb, bo_back, bx = sig("bo_ps", 1), sig("bo_sb", 1), sig("bo_back", 1), sig("bx", 1, 1)
        c_step = sig("c_step", NT * 2, over=NT * 4)
        chs, chs_dma, chn = sig("chs", 1, over=2), sig("chs_dma", 32, over=64), sig("chn", NT, NT, over=2 * NT)
        ct_ps, ct_hi, ct_lo = sig("ct_ps", 1, over=1), sig("ct_hi", 1, over=1), sig("ct_lo", 1, over=1)
        cg_ps, ca_ps, cgel, cu = sig("cg_ps", 3, over=2), sig("ca_ps", 3, over=2), sig("cgel", 3, over=2), sig("cu", 3, 3, over=2)
        cu_hi, cu_lo = sig("cu_hi", 3, over=1), sig("cu_lo", 3, 3, over=1)
        co_ps, co_sb, co_back, cx = sig("co_ps", 1), sig("co_sb", 1), sig("co_back", 1), sig("cx", 1, 1)
        d_mean = sig("d_mean", 1)
        d_step, d_norm, d_out = sig("d_step", 2 * NT), sig("d_norm", NT), sig("d_out", 1)

        n_root = sig("n_var", 1), sig("n_rstd", 1)
        a_root = sig("a_var", 2), sig("a_rstd", 2)
        c_root = sig("c_var", 1, over=2), sig("c_rstd", 1, over=2)
        d_var, d_rstd = sig("d_var", 1), sig("d_rstd", 1)

        def hold(eng, semaphore, value):
            eng.wait_ge(semaphore, value)
            eng.sem_inc(held, 1)

        def barrier(eng, n):
            eng.drain().then_inc(phase, 1)
            hold(eng, phase, n * 5)

        def variance(dve, steps, src, root):
            bn_stats(dve, steps, src, range(NT))
            aggregate(dve, steps, root)

        def bn_stats(dve, steps, src, tiles):
            for j in tiles:
                steps.did(dve.bn_stats(stats[:, j, :], src(j)))

        def aggregate(dve, steps, root):
            hold(dve, steps.raised.sem, steps.raised.at(steps.it, steps.n))
            for j in range(NT):
                steps.did(dve.bn_aggr(mv[:, j, :], stats[:, j, :]))
            steps.settle()
            dve.tensor_scalar(vare[:, :], mv[:, :, 1], EPS, None, ALU.add).then_inc(root[0].sem, 1)

        def normed(dve, steps, src, root, it, k, dst, last):
            dve.wait_ge(root[1].sem, root[1].at(it, k + 1))
            for j in range(NT):
                ins = dve.tensor_scalar(dst(j), src(j), mv[:, j, 0:1], rstd[:, j:j + 1],
                                        ALU.subtract, ALU.mult)
                if last is None:
                    steps.did(ins)
                else:
                    ins.then_inc(last.sem, 1)

        def inverse_root(pool, root, it, k):
            pool.wait_ge(root[0].sem, root[0].at(it, k + 1))
            pool.tensor_tensor(rstd[:, :], vare[:, :], mhalf[:, 0:NT], ALU.pow).then_inc(root[1].sem, 1)

        def three(pe, acc, left, right, start=True, stop=True):
            pe.matmul(acc, left[0], right[0], start=start, stop=False)
            pe.matmul(acc, left[0], right[1], start=False, stop=False)
            return pe.matmul(acc, left[1], right[0], start=False, stop=stop)

        def zero_blocks(eng, keys, values, done):
            for n in keys:
                z = kt[n][:, :, :, :].bitcast(F32)
                eng.memset(z[0:DK, :, 1, :], 0.0).then_inc(done, 1)
                eng.memset(z[DK:P, :, 0, :], 0.0).then_inc(done, 1)
            for n in values:
                eng.memset(vb[n][0:DK, :, :, DK:P], 0.0).then_inc(done, 1)
                eng.memset(vb[n][DK:P, :, :, 0:DK], 0.0).then_inc(done, 1)

        def slot_free(n):
            return (0, -1, 1)[n]

        def cut(pair, f):
            return [f(t) for t in pair]

        def score_bank(n):
            return bank[n % (H * NT) % 3]

        block = ctx.enter_context(nc.Block())

        raw_q = stage[0:DK, 0:H * C].rearrange("d (h c) -> d h c", h=H)
        raw_k = stage[0:DK, H * C:2 * H * C].rearrange("d (h c) -> d h c", h=H)
        raw_v = sq[:, :].rearrange("p (g c) -> p g c", g=PAIRS)
        raw_o = rot_a[:, :].rearrange("p (g c) -> p g c", g=PAIRS)
        raw_causal, raw_band = rot_b[:, 0:P], rot_b[:, P:P + 2 * (P + WINDOW)]
        raw_qkv = stage[:, 0:3 * INNER]
        raw_wo = stage[:, 1536:2048].rearrange("p (g c) -> p g c", g=LPAIRS)
        raw_w1 = stage[:, 2048:2048 + 2 * HID]
        raw_w2 = stage[:, 2816:2816 + 3 * C].rearrange("p (g c) -> p g c", g=3)

        @block.sync
        def _(sp):
            sp.dma_start(ident[:, :], ident_c).then_inc(s_qk, 16)
            sp.dma_start(raw_q, w_q.rearrange("h d c -> d h c")).then_inc(s_qk, 16)
            sp.dma_start(raw_k, w_k.rearrange("h d c -> d h c")).then_inc(s_qk, 16)
            sp.dma_start(raw_v, w_v.rearrange("(g a) d c -> (a d) g c", a=2)).then_inc(s_weights, 16)
            sp.dma_start(raw_o, w_o.rearrange("(g p) c -> p g c", p=P)).then_inc(s_weights, 16)
            sp.dma_start(raw_causal, causal_c).then_inc(s_const, 16)
            sp.dma_start(raw_band, band_c).then_inc(s_const, 16)
            sp.dma_start(x1[:, 0:NT, :], x[0:1].rearrange("b (j p) c -> p (b j) c", p=P)).then_inc(s_x0, 16)
            sp.dma_start(x1[:, NT:BATCH * NT, :], x[1:BATCH].rearrange("b (j p) c -> p (b j) c", p=P)).then_inc(s_x, 16)
            sp.dma_start(rope[:, 0, :, :, :], rope_cos_c.rearrange("(j p) a d -> p j a d", p=P)).then_inc(s_rope, 16)
            sp.dma_start(rope[:, 1, :, :, :], rope_sin_c.rearrange("(j p) a d -> p j a d", p=P)).then_inc(s_rope, 16)
            barrier(sp, 1)

            def load(l):
                def layer(w, pattern="o a b -> (o a) b", **kw):
                    return w[bass.ds(l, 1)].rearrange(pattern, **kw)
                sp.dma_start(raw_qkv, layer(wqkv)).then_inc(s_lw, 16)
                sp.dma_start(raw_wo, layer(wo, "o (g p) c -> p (o g) c", p=P)).then_inc(s_lw, 16)
                sp.dma_start(raw_w1, layer(w1)).then_inc(s_lw, 16)
                for n, (r0, rows) in enumerate(HC):
                    sp.dma_start(raw_w2[0:rows, n, :], layer(w2)[r0:r0 + rows, :]).then_inc(s_lw, 16)
                for n, v in enumerate((ln_g, ln_b, b2)):
                    sp.dma_start(cols_raw[:, n:n + 1], layer(v, "o (c k) -> (o c) k", k=1)).then_inc(s_lw, 16)
                for n in range(6):
                    r0, rows = HC[n % 3]
                    r0 += HID * (n // 3)
                    sp.dma_start(cols_raw[0:rows, 3 + n:4 + n],
                                 layer(b1, "o (c k) -> (o c) k", k=1)[r0:r0 + rows, :]).then_inc(s_lw, 16)
                for n, v in enumerate((q_scale, k_scale)):
                    row = v[bass.ds(l, 1), :]
                    sp.dma_start(qks[:, 0, n, :], row.to_broadcast([P, LD])).then_inc(s_lw, 16)
                    sp.dma_start(qks[:, 1, n, 0:LD // 2], row[:, LD // 2:].to_broadcast([P, LD // 2])).then_inc(s_lw, 16)
                    sp.dma_start(qks[:, 1, n, LD // 2:], row[:, 0:LD // 2].to_broadcast([P, LD // 2])).then_inc(s_lw, 16)

            def first_rows():
                sp.dma_start(xs[:, :, :], xf[:, 0:NT, :]).then_inc(bxs.sem, 16)

            def move_rows(l):
                with sp.Fori(0, BATCH) as b:
                    sp.wait_ge(bxt_ps.sem, bxt_ps.at((l, b), 1))
                    sp.dma_start(xs[:, :, :], xf[:, bass.ds(b * NT + NT, NT), :]).then_inc(bxs.sem, 16)
                barrier(sp, l * 3 + 4)

                def shift(it, b, d):
                    first = bass.ds((b + d) * NT, NT)
                    hold(sp, chn.sem, chn.at(it, NT * d))
                    sp.dma_start(hs[1:P, :, C // 2:], xf[0:P - 1, first, C // 2:]).then_inc(chs_dma.sem, 16)
                    sp.dma_start(hs[0:1, 1:NT, C // 2:], xf[P - 1:P, bass.ds((b + d) * NT, NT - 1), C // 2:]).then_inc(chs_dma.sem, 16)

                shift((l, 0), 0, 0)
                shift((l, 0), 0, 1)
                with sp.Fori(0, BATCH) as b:
                    shift((l, b), b, 2)
                barrier(sp, l * 3 + 5)

            load(0)
            barrier(sp, 2)
            with sp.Fori(0, DEPTH - 1) as l:
                first_rows()
                barrier(sp, l * 3 + 3)
                load(l + 1)
                move_rows(l)
            first_rows()
            barrier(sp, (DEPTH - 1) * 3 + 3)
            move_rows(DEPTH - 1)
            with sp.Fori(0, BATCH) as b:
                sp.wait_ge(d_out.sem, d_out.at(b, 1))
                sp.dma_start(out[bass.ds(b, 1)].rearrange("o (j p) c -> p (o j) c", p=P),
                             x1[:, bass.ds(b * NT, NT), :]).then_inc(s_out, 16)
            sp.wait_ge(s_out, 16 * BATCH)

        @block.gpsimd
        def _(pool):
            pool.memset(hs[0:1, 0:1, C // 2:], 0.0).then_inc(pre_pool, 1)
            pool.memset(mhalf[:, :], -0.5).then_inc(pre_pool, 1)
            pool.memset(cols[:, :], 0.0).then_inc(pre_pool, 1)
            pool.sem_inc(p_step.sem, p_step.credit)
            pool.sem_inc(cu_lo.sem, cu_lo.credit)
            for t in (x1, xf):
                pool.memset(t[:, BATCH * NT:, :], 0.0).then_inc(pre_pool, 1)
            barrier(pool, 1)
            inverse_root(pool, n_root, 0, 0)
            with pool.Fori(0, BATCH) as b:
                inverse_root(pool, n_root, b + 1, 0)
                for k in range(2):
                    inverse_root(pool, a_root, b, k)
            barrier(pool, 2)
            zero_blocks(pool, (0,), (0, 1), pre_pool)
            with pool.Fori(0, DEPTH) as l:
                for t in xt:
                    pool.memset(t[DK:P, 0:1].bitcast(F32), 0.0).then_inc(pre_pool, 1)
                barrier(pool, l * 3 + 3)

                def turn_qk(it, j):
                    steps = Steps(pool, p_step)
                    steps.start(it)
                    steps.n = POOL_STEPS * j
                    pool.wait_ge(bsq.sem, bsq.at(it, j + 1))
                    squares = sq.rearrange("p (h d) -> p h d", d=LD)
                    for w in (LD // 2, LD // 4):
                        steps.did(pool.tensor_tensor(squares[:, :, 0:w], squares[:, :, 0:w], squares[:, :, w:2 * w], ALU.add))
                        if w == LD // 2:
                            steps.settle()
                    pool.wait_ge(brot.sem, brot.at(it, j + 1))
                    steps.did(pool.tensor_tensor(qk[j % 2][:, :], rot_a[:, :], rot_b[:, :], ALU.add))
                    hold(pool, bssq.sem, bssq.at(it, j + 1))
                    steps.did(pool.tensor_scalar(ssqc[:, :], ssq[:, :], 1e-24, None, ALU.max))
                    steps.settle()
                    steps.did(pool.tensor_tensor(rnorm[:, :], ssqc[:, :], mhalf[:, :], ALU.pow))
                    steps.settle()
                    assert steps.n == POOL_STEPS * (j + 1)
                    v = qk[j % 2][:, :].rearrange("p (h d) -> p h d", d=LD)
                    pool.tensor_tensor(v, v, rnorm[:, :, None].to_broadcast([P, 2 * LH, LD]),
                                       ALU.mult).then_inc(bqk.sem, 1)

                for j in range(3):
                    turn_qk((l, 0), j)
                with pool.Fori(0, BATCH) as b:
                    for j in range(3, 3 + NT):
                        turn_qk((l, b), j)
                barrier(pool, l * 3 + 4)
                def c_copy(it, b, d):
                    hold(pool, chn.sem, chn.at(it, NT * d))
                    pool.tensor_copy(hs[:, :, 0:C // 2], xf[:, bass.ds((b + d) * NT, NT), 0:C // 2]).then_inc(chs.sem, 1)

                def c_low(it, d, n):
                    rows = HC[n][1]
                    pool.wait_ge(cu_hi.sem, cu_hi.at(it, 3 * d + n + 1))
                    pool.tensor_tensor(ut[1][0:rows, n, :], ugl[0:rows, n % 2, :],
                                       ut[0][0:rows, n, :].bitcast(F32), ALU.subtract).then_inc(cu_lo.sem, 1)

                for d in range(2):
                    c_copy((l, 0), 0, d)
                    inverse_root(pool, c_root, (l, 0), d)
                c_low((l, 0), 0, 0)
                with pool.Fori(0, BATCH) as b:
                    it = (l, b)
                    c_low(it, 0, 1)
                    c_copy(it, b, 2)
                    c_low(it, 0, 2)
                    inverse_root(pool, c_root, it, 2)
                    c_low(it, 1, 0)
                barrier(pool, l * 3 + 5)
            with pool.Fori(0, BATCH) as b:
                pool.wait_ge(d_var.sem, d_var.at(b, 1))
                pool.tensor_tensor(rstd_out[:, bass.ds(b * NT, NT)], vare_out[:, bass.ds(b * NT, NT)],
                                   mhalf[:, 0:NT], ALU.pow).then_inc(d_rstd.sem, 1)

        @block.scalar
        def _(act):
            def copy(dst, src):
                return act.activation(dst, src, ACT.Copy)

            act.wait_ge(s_qk, 48)
            copy(ident16[:, :], ident[:, :]).then_inc(pre_act, 1)
            act.wait_ge(s_const, 32)
            act.wait_ge(s_weights, 32)
            copy(causal[:, :], raw_causal).then_inc(pre_act, 1)
            copy(band[:, :, :].rearrange("p a n -> p (a n)"), raw_band).then_inc(pre_act, 1)
            copy(wog[0][:, :, :], raw_o).then_inc(pre_act, 1)
            for n in range(4):
                act.wait_ge(pre_pe, n + 1)
                act.activation(mh[0][:, 4 * n:4 * n + 4, :].rearrange("p h c -> p (h c)"), bank[n][:, :],
                               ACT.Copy, scale=DK ** -0.5).then_inc(pre_act, 1)
            for n in range(2):
                act.wait_ge(pre_pe, n + 5)
                copy(wv[0][:, 512 * n:512 * n + 512], bank[4 + n][:, :]).then_inc(pre_act, 1)
            barrier(act, 1)

            def a_exp(b, h, j):
                n = h * NT + j
                act.wait_ge(s_max.sem, s_max.at(b, n + 1))
                act.activation(prob[:, h % 2, SO[j]:SO[j] + SW[j]], score_bank(n)[:, 0:SW[j]], ACT.Exp,
                               bias=negmax[:, h % 2, j:j + 1],
                               accum_out=rsum[:, h // 2 % 2, h % 2, j:j + 1]).then_inc(s_exp.sem, 1)

            def a_pt(b, h, g):
                n = 3 * h + g
                w = P * len(TG[g])
                act.wait_ge(pt_ps.sem, pt_ps.at(b, n + 1))
                copy(pt[0][:, h % 2, 512 * g:512 * g + w], bank[3 + n % 2][:, 0:w]).then_inc(pt_hi.sem, 1)

            def a_z(b, h):
                act.wait_ge(z_ps.sem, z_ps.at(b, h + 1))
                copy(zt[0][:, h % 2, :], bank[5][:, :]).then_inc(z_hi.sem, 1)

            def a_yt(b, p):
                act.wait_ge(yt_ps.sem, yt_ps.at(b, p + 1))
                copy(yt[0][:, :], bank[5][:, :]).then_inc(yt_hi.sem, 1)

            def a_xt(b, d):
                act.wait_ge(xt_ps.sem, xt_ps.at(b, d + 1))
                copy(xt[0][:, :], bank[5][:, :]).then_inc(xt_hi.sem, 1)

            def a_v(b, d, groups):
                for g in groups:
                    act.wait_ge(v_ps.sem, v_ps.at(b, 8 * d + g + 1))
                    copy(vv[0][:, g // 2, 512 * (g % 2):512 * (g % 2) + 512], bank[3 + g % 2][:, :]).then_inc(v_hi.sem, 1)

            def begin(b, d):
                h = H * d
                if d:
                    a_yt(b, PAIRS - 2)
                    a_pt(b, H - 2, 2)
                    a_pt(b, H - 1, 0)
                a_xt(b, d)
                if d:
                    a_pt(b, H - 1, 1)
                    a_pt(b, H - 1, 2)
                a_z(b, h)
                a_v(b, d, (0, 1))
                a_z(b, h + 1)
                a_v(b, d, (2, 3))
                a_exp(b, h, 0)
                a_exp(b, h, 1)
                a_v(b, d, (4, 5))
                a_exp(b, h, 2)
                a_z(b, h + 2)
                a_exp(b, h, 3)
                a_v(b, d, (6, 7))
                a_exp(b, h + 1, 0)
                a_pt(b, h, 0)
                a_exp(b, h + 1, 1)
                a_exp(b, h + 1, 2)
                a_pt(b, h, 1)
                a_exp(b, h + 1, 3)

            def pair(b, p):
                if p:
                    a_yt(b, p - 1)
                a_pt(b, 2 * p, 2)
                a_pt(b, 2 * p + 1, 0)
                a_exp(b, 2 * p + 2, 0)
                a_exp(b, 2 * p + 2, 1)
                a_z(b, 2 * p + 3)
                a_pt(b, 2 * p + 1, 1)
                a_exp(b, 2 * p + 2, 2)
                a_pt(b, 2 * p + 1, 2)
                if p != PAIRS - 2:
                    a_z(b, 2 * p + 4)
                a_exp(b, 2 * p + 2, 3)
                if p == PAIRS:
                    act.wait_ge(a_ps.sem, a_ps.at(b, 1))
                    copy(tail[:, :], wide[:, 512:1024]).then_inc(a_sb.sem, 1)
                a_exp(b, 2 * p + 3, 0)
                a_pt(b, 2 * p + 2, 0)
                a_exp(b, 2 * p + 3, 1)
                a_exp(b, 2 * p + 3, 2)
                a_pt(b, 2 * p + 2, 1)
                a_exp(b, 2 * p + 3, 3)

            act.sem_inc(s_exp.sem, s_exp.credit)
            begin(0, 0)
            pair(0, 0)
            pair(0, 1)
            with act.Fori(0, BATCH) as b:
                for p in range(2, PAIRS - 1):
                    pair(b, p)
                begin(b, 1)
                pair(b, PAIRS)
                pair(b, PAIRS + 1)
            barrier(act, 2)

            def b_exp(it, j, p):
                q = j * LPAIRS + p
                act.wait_ge(bmax.sem, bmax.at(it, q + 1))
                m0 = 1 if j % NT == 0 else 0
                w = LD * (3 - m0)
                for e in range(2):
                    act.activation(lprob[:, q % 2, m0:3, e, :],
                                   bank[q % 2][:, e * w:(e + 1) * w].rearrange("p (m n) -> p m n", n=LD), ACT.Exp,
                                   bias=lneg[:, q % 4, e:e + 1],
                                   accum_out=lsum[:, j % 2, 2 * p + e:2 * p + e + 1]).then_inc(bexp.sem, 1)

            def b_pt(it, j, p):
                q = j * LPAIRS + p
                m0 = 1 if j % NT == 0 else 0
                act.wait_ge(bpt_ps.sem, bpt_ps.at(it, q + 1))
                act.wait_ge(by_ps.sem, by_ps.at(it, q - 1))
                copy(lpt[0][:, q % 2, m0:3, :].rearrange("p m n -> p (m n)"),
                     bank[2 + 2 * (q % 2)][:, m0 * P:3 * P]).then_inc(bpt_hi.sem, 1)

            def b_sq(it, j):
                act.wait_ge(bqk_ps.sem, bqk_ps.at(it, j + 1))
                act.wait_ge(bssq.sem, bssq.at(it, j))
                act.activation(sq[:, :], wide[:, :], ACT.Square).then_inc(bsq.sem, 1)

            def b_v(it, j):
                act.wait_ge(bv_ps.sem, bv_ps.at(it, j + 1))
                vp = bank[5][:, :].rearrange("p (c e n) -> p c e n", c=LPAIRS, e=2)
                for r in range(2):
                    for e in range(2):
                        copy(vb[0][DK * e:DK * e + DK, 2 * (j % NT) + r, :, DK * e:DK * e + DK],
                             vp[DK * r:DK * r + DK, :, e, :]).then_inc(bv_hi.sem, 1)

            def b_qt(it, j, parts):
                for n in parts:
                    if n == 0:
                        act.wait_ge(bqt_ps.sem, bqt_ps.at(it, j + 1))
                        copy(qt[0][:, j % 2, :, :].rearrange("p c n -> p (c n)"), wide[:, 0:512]).then_inc(bqt_hi.sem, 1)
                    else:
                        e = n - 1
                        copy(kt[0][DK * e:DK * e + DK, :, e, P * (j % NT):P * (j % NT) + P],
                             wide[DK * e:DK * e + DK, 512:1024].rearrange("p (c n) -> p c n", c=LPAIRS)).then_inc(bqt_hi.sem, 1)

            def b_ot(it, j):
                act.wait_ge(bot_ps.sem, bot_ps.at(it, j + 1))
                copy(ot[0][:, :, P * j:P * j + P], bank[5][:, :].rearrange("p (c n) -> p c n", c=LPAIRS)).then_inc(bot_hi.sem, 1)

            act.sem_inc(bexp.sem, bexp.credit)
            with act.Fori(0, DEPTH) as l:
                act.wait_ge(s_lw, (l + 1) * 16 * 21)
                copy(wl[0][:, :], raw_qkv).then_inc(lay_act, 1)
                copy(wol[0][:, :, :], raw_wo).then_inc(lay_act, 1)
                copy(w2l[0][:, 0:2, :], raw_w2[:, 0:2, :]).then_inc(lay_act, 1)
                copy(w2l[0][0:HC[2][1], 2, :], raw_w2[0:HC[2][1], 2, :]).then_inc(lay_act, 1)
                act.wait_ge(lay_dve, l * LAYER_STEPS + 8)
                copy(w1l[0][:, :], w1g[:, :]).then_inc(lay_act, 1)
                barrier(act, l * 3 + 3)

                def b_xt(it, b):
                    act.wait_ge(bxt_ps.sem, bxt_ps.at(it, b + 1))
                    copy(xt[0][0:DK, :], bank[5][0:DK, :]).then_inc(bh_hi.sem, 1)
                    copy(xt[0][DK:P, 1:T], bank[5][DK:P, 0:T - 1]).then_inc(bh_hi.sem, 1)

                first = (l, 0)
                def stretch(it, j):
                    b_pt(it, j, 0)
                    b_exp(it, j, 1)
                    b_v(it, j + 2)
                    b_qt(it, j + 1, (0, 1))
                    if j != 1:
                        b_pt(it, j, 1)
                    b_qt(it, j + 1, (2,))
                    if j == 1:
                        b_xt(it, 1)
                        b_pt(it, j, 1)
                    b_exp(it, j, 2)
                    if j >= 2:
                        b_ot(it, j - 1)
                    b_pt(it, j, 2)
                    b_exp(it, j, 3)
                    b_sq(it, j + 3)
                    b_exp(it, j + 1, 0)
                    if j == 1:
                        b_ot(it, 0)
                    if j == NT:
                        act.wait_ge(bo_ps.sem, bo_ps.at(it, 1))
                        copy(tail[:, :], bank[5][:, :]).then_inc(bo_sb.sem, 1)
                    b_pt(it, j, 3)

                b_xt(first, 0)
                b_sq(first, 0)
                b_v(first, 0)
                b_sq(first, 1)
                b_v(first, 1)
                b_qt(first, 0, (0, 1, 2))
                b_sq(first, 2)
                b_exp(first, 0, 0)
                stretch(first, 0)
                with act.Fori(0, BATCH) as b:
                    for j in range(1, NT + 1):
                        stretch((l, b), j)
                barrier(act, l * 3 + 4)
                def c_xt(it, d):
                    act.wait_ge(ct_ps.sem, ct_ps.at(it, d + 1))
                    copy(xt[0][:, :], bank[5][:, :]).then_inc(ct_hi.sem, 1)

                def c_gelu(it, d, n):
                    rows = HC[n][1]
                    act.wait_ge(cg_ps.sem, cg_ps.at(it, 3 * d + n + 1))
                    act.activation(gel[0:rows, n % 2, :], bank[n % 2][0:rows, :], ACT.Gelu,
                                   bias=b1f[0:rows, 3 + n:4 + n]).then_inc(cgel.sem, 1)

                def c_high(it, d, n):
                    rows = HC[n][1]
                    act.wait_ge(cu.sem, cu.at(it, 3 * d + n + 1))
                    copy(ut[0][0:rows, n, :], ugl[0:rows, n % 2, :]).then_inc(cu_hi.sem, 1)

                first = (l, 0)
                c_xt(first, 0)
                c_gelu(first, 0, 0)
                c_high(first, 0, 0)
                c_gelu(first, 0, 1)
                with act.Fori(0, BATCH) as b:
                    it = (l, b)
                    c_high(it, 0, 1)
                    c_gelu(it, 0, 2)
                    c_xt(it, 1)
                    c_high(it, 0, 2)
                    c_gelu(it, 1, 0)
                    c_high(it, 1, 0)
                    act.wait_ge(co_ps.sem, co_ps.at(it, 1))
                    act.activation(tail[:, :], bank[4][:, :], ACT.Identity, bias=cols[:, 2:3]).then_inc(co_sb.sem, 1)
                    c_gelu(it, 1, 1)
                barrier(act, l * 3 + 5)

        @block.vector
        def _(dve):
            dve.wait_ge(s_weights, 32)
            dve.wait_ge(pre_act, 4)
            dve.tensor_tensor(wog[1][:, :, :], raw_o, wog[0][:, :, :].bitcast(F32), ALU.subtract).then_inc(pre_dve, 1)
            for n in range(4):
                dve.wait_ge(pre_act, n + 5)
                dve.scalar_tensor_tensor(mh[1][:, 4 * n:4 * n + 4, :].rearrange("p h c -> p (h c)"), bank[n][:, :],
                                         DK ** -0.5, mh[0][:, 4 * n:4 * n + 4, :].rearrange("p h c -> p (h c)").bitcast(F32),
                                         ALU.mult, ALU.subtract).then_inc(pre_dve, 1)
            for n in range(2):
                dve.wait_ge(pre_act, n + 9)
                dve.tensor_tensor(wv[1][:, 512 * n:512 * n + 512], bank[4 + n][:, :],
                                  wv[0][:, 512 * n:512 * n + 512].bitcast(F32), ALU.subtract).then_inc(pre_dve, 1)
            dve.wait_ge(s_x0, 16)
            barrier(dve, 1)

            def low(dst, full, high):
                return dve.tensor_tensor(dst, full, high.bitcast(F32) if high.dtype == F32R else high, ALU.subtract)

            def a_max(b, h, j):
                n = h * NT + j
                dve.wait_ge(s_ps.sem, s_ps.at(b, n + 1))
                dve.tensor_reduce(negmax[:, h % 2, j:j + 1], score_bank(n)[:, 0:SW[j]], AX.X, ALU.max,
                                  negate=True).then_inc(s_max.sem, 1)

            def a_pt(b, h, g):
                n = 3 * h + g
                w = P * len(TG[g])
                dve.wait_ge(pt_hi.sem, pt_hi.at(b, n + 1))
                low(pt[1][:, h % 2, 512 * g:512 * g + w], bank[3 + n % 2][:, 0:w],
                    pt[0][:, h % 2, 512 * g:512 * g + w]).then_inc(pt_lo.sem, 1)

            def a_z(b, h):
                dve.wait_ge(z_hi.sem, z_hi.at(b, h + 1))
                low(zt[1][:, h % 2, :], bank[5][:, :], zt[0][:, h % 2, :]).then_inc(z_lo.sem, 1)

            def a_norm(b, p):
                dve.wait_ge(y_ps.sem, y_ps.at(b, p + 1))
                dve.reciprocal(rinv[:, :, :], rsum[:, p % 2, :, :]).then_inc(rinv_ready.sem, 1)
                dve.wait_ge(rinv_ready.sem, rinv_ready.at(b, p + 1))
                dve.tensor_tensor(ysb[:, p % 2, :, :, :].rearrange("p j e n -> p e j n"),
                                  wide[:, 0:512].rearrange("p (e j n) -> p e j n", e=2, j=NT),
                                  rinv[:, :, :, None].to_broadcast([P, 2, NT, DK]), ALU.mult).then_inc(y_norm.sem, 1)

            def a_yt(b, p):
                dve.wait_ge(yt_hi.sem, yt_hi.at(b, p + 1))
                low(yt[1][:, :], bank[5][:, :], yt[0][:, :]).then_inc(yt_lo.sem, 1)

            def a_xt(b, d):
                dve.wait_ge(xt_hi.sem, xt_hi.at(b, d + 1))
                low(xt[1][:, :], bank[5][:, :], xt[0][:, :]).then_inc(xt_lo.sem, 1)

            def a_v(b, d, groups):
                for g in groups:
                    dve.wait_ge(v_hi.sem, v_hi.at(b, 8 * d + g + 1))
                    v = [t[:, g // 2, 512 * (g % 2):512 * (g % 2) + 512] for t in vv]
                    low(v[1], bank[3 + g % 2][:, :], v[0]).then_inc(v_lo.sem, 1)

            steps, nsteps = Steps(dve, a_step), Steps(dve, n_step)

            def ahead(b, part):
                src = tile_of(x1, b)
                if part < 2:
                    if part == 0:
                        nsteps.start(b)
                    bn_stats(dve, nsteps, src, (2 * part, 2 * part + 1))
                if part == 2:
                    aggregate(dve, nsteps, n_root)
                    nsteps.end()
                if part == 3:
                    normed(dve, nsteps, src, n_root, b, 0, lambda j: xh[:, j, :], xh_ready)

            def tile_of(t, b):
                return lambda j: t[:, bass.ds(b * NT + j, 1), :].rearrange("p o c -> p (o c)")

            def begin(b, d):
                h = H * d
                if d:
                    a_max(b, H - 1, 3)
                    a_pt(b, H - 2, 0)
                    a_pt(b, H - 2, 1)
                    a_yt(b, PAIRS - 2)
                    a_pt(b, H - 2, 2)
                    a_pt(b, H - 1, 0)
                a_xt(b, d)
                if d:
                    a_pt(b, H - 1, 1)
                    a_pt(b, H - 1, 2)
                    a_norm(b, PAIRS - 1)
                a_z(b, h)
                a_v(b, d, (0, 1))
                a_z(b, h + 1)
                a_v(b, d, (2, 3))
                a_max(b, h, 0)
                a_max(b, h, 1)
                a_v(b, d, (4, 5))
                a_max(b, h, 2)
                a_max(b, h, 3)
                a_z(b, h + 2)
                a_v(b, d, (6,))
                a_max(b, h + 1, 0)
                a_v(b, d, (7,))
                a_max(b, h + 1, 1)
                a_max(b, h + 1, 2)

            def pair(b, p):
                behind = p == PAIRS + 1
                back = wide[:, 512:1024].rearrange("p (j c) -> p j c", j=NT)
                a_max(b, 2 * p + 1, 3)
                a_pt(b, 2 * p, 0)
                a_pt(b, 2 * p, 1)
                if behind:
                    hold(dve, a_back.sem, a_back.at(b, 1))
                    steps.start(b)
                    variance(dve, steps, lambda j: back[:, j, :], a_root)
                if p in (3, 4):
                    ahead(b + 1, 2 * (p - 3))
                a_max(b, 2 * p + 2, 0)
                if p:
                    a_yt(b, p - 1)
                a_pt(b, 2 * p, 2)
                a_max(b, 2 * p + 2, 1)
                a_pt(b, 2 * p + 1, 0)
                if behind:
                    here = bass.ds(b * NT, NT)
                    normed(dve, steps, lambda j: back[:, j, :], a_root, b, 0, lambda j: xn[:, j, :], a_left)
                    dve.wait_ge(a_left.sem, a_left.at(b, NT))
                    steps.did(dve.tensor_tensor(x1[:, here, :], x1[:, here, :], xn[:, :, :], ALU.add))
                a_max(b, 2 * p + 2, 2)
                a_z(b, 2 * p + 3)
                a_pt(b, 2 * p + 1, 1)
                a_pt(b, 2 * p + 1, 2)
                if behind:
                    hold(dve, a_step.sem, a_step.at(b, steps.n))
                    variance(dve, steps, tile_of(x1, b), a_root)
                if p in (3, 4):
                    ahead(b + 1, 2 * (p - 3) + 1)
                a_max(b, 2 * p + 2, 3)
                a_max(b, 2 * p + 3, 0)
                a_max(b, 2 * p + 3, 1)
                if p != PAIRS - 2:
                    a_z(b, 2 * p + 4)
                a_norm(b, p)
                a_max(b, 2 * p + 3, 2)
                if behind:
                    normed(dve, steps, tile_of(x1, b), a_root, b, 1, tile_of(xf, b), None)
                    steps.settle()
                    steps.end()

            dve.sem_inc(pt_lo.sem, pt_lo.credit)
            dve.sem_inc(y_norm.sem, y_norm.credit)
            dve.sem_inc(a_left.sem, a_left.credit)
            for part in range(4):
                ahead(0, part)
            begin(0, 0)
            pair(0, 0)
            pair(0, 1)
            dve.wait_ge(s_x, 16)
            with dve.Fori(0, BATCH) as b:
                for p in range(2, PAIRS - 1):
                    pair(b, p)
                begin(b, 1)
                pair(b, PAIRS)
                pair(b, PAIRS + 1)
            a_max(BATCH - 1, 2 * PAIRS + 5, 3)
            barrier(dve, 2)

            half = LD // 2

            def b_rot(it, j, part):
                src = wide[:, :].rearrange("p (a h d) -> p a h d", a=2, h=LH)
                ra = rot_a[:, :].rearrange("p (a h d) -> p a h d", a=2, h=LH)
                rb = rot_b[:, :].rearrange("p (a h d) -> p a h d", a=2, h=LH)

                def table(f, lo, hi):
                    return ropes[:, f, j % NT, :, None, lo:hi].to_broadcast([P, 2, LH, hi - lo])

                if part == 0:
                    dve.wait_ge(bsq.sem, bsq.at(it, j + 1))
                    dve.wait_ge(p_step.sem, p_step.at(it, POOL_STEPS * j - 2))
                    dve.tensor_tensor(ra, src, table(0, 0, LD), ALU.mult).then_inc(r_step.sem, 1)
                else:
                    dve.tensor_tensor(rb[:, :, :, 0:half], src[:, :, :, half:LD], table(1, 0, half),
                                      ALU.mult).then_inc(r_step.sem, 1)
                    dve.wait_ge(r_step.sem, r_step.at(it, 2 * j + 2))
                    dve.tensor_tensor(rb[:, :, :, half:LD], src[:, :, :, 0:half], table(1, half, LD),
                                      ALU.mult).then_inc(brot.sem, 1)

            def b_ssq(it, j):
                dve.wait_ge(p_step.sem, p_step.at(it, POOL_STEPS * j + 2))
                squares = sq.rearrange("p (h d) -> p h d", d=LD)
                dve.tensor_reduce(ssq[:, :], squares[:, :, 0:LD // 4], AX.X, ALU.add).then_inc(bssq.sem, 1)

            def b_max(it, j, p):
                q = j * LPAIRS + p
                w = P if j % NT == 0 else P + WINDOW
                dve.wait_ge(bs_ps.sem, bs_ps.at(it, q + 1))
                dve.tensor_reduce(lneg[:, q % 4, :], bank[q % 2][:, 0:2 * w].rearrange("p (e n) -> p e n", e=2),
                                  AX.X, ALU.max, negate=True).then_inc(bmax.sem, 1)

            def b_pt(it, j, p):
                q = j * LPAIRS + p
                m0 = 1 if j % NT == 0 else 0
                dve.wait_ge(bpt_hi.sem, bpt_hi.at(it, q + 1))
                v = [t[:, q % 2, m0:3, :].rearrange("p m n -> p (m n)") for t in lpt]
                low(v[1], bank[2 + 2 * (q % 2)][:, m0 * P:3 * P], v[0]).then_inc(bpt_lo.sem, 1)

            def b_v(it, j):
                dve.wait_ge(bv_hi.sem, bv_hi.at(it, 4 * j + 4))
                vp = bank[5][:, :].rearrange("p (c e n) -> p c e n", c=LPAIRS, e=2)
                for r in range(2):
                    for e in range(2):
                        v = [t[DK * e:DK * e + DK, 2 * (j % NT) + r, :, DK * e:DK * e + DK] for t in vb]
                        low(v[1], vp[DK * r:DK * r + DK, :, e, :], v[0]).then_inc(bv_lo.sem, 1)

            def b_qt(it, j):
                dve.wait_ge(bqt_hi.sem, bqt_hi.at(it, 3 * j + 1))
                q = [t[:, j % 2, :, :].rearrange("p c n -> p (c n)") for t in qt]
                low(q[1], wide[:, 0:512], q[0]).then_inc(bqt_lo.sem, 1)
                dve.wait_ge(bqt_hi.sem, bqt_hi.at(it, 3 * j + 3))
                for e in range(2):
                    k = [t[DK * e:DK * e + DK, :, e, P * (j % NT):P * (j % NT) + P] for t in kt]
                    low(k[1], wide[DK * e:DK * e + DK, 512:1024].rearrange("p (c n) -> p c n", c=LPAIRS), k[0]).then_inc(bqt_lo.sem, 1)

            def b_ot(it, j):
                dve.wait_ge(bot_hi.sem, bot_hi.at(it, j + 1))
                o = [t[:, :, P * j:P * j + P] for t in ot]
                low(o[1], bank[5][:, :].rearrange("p (c n) -> p c n", c=LPAIRS), o[0]).then_inc(bot_lo.sem, 1)

            def b_norm(it, j, steps):
                dve.wait_ge(by_ps.sem, by_ps.at(it, LPAIRS * (j + 1)))
                steps.did(dve.reciprocal(linv[:, :], lsum[:, j % 2, :]))
                steps.settle()
                dve.tensor_tensor(osb[:, j % 2, :].rearrange("p (h d) -> p h d", d=LD),
                                  ypart[:, :].rearrange("p (h d) -> p h d", d=LD),
                                  linv[:, :, None].to_broadcast([P, LH, LD]), ALU.mult).then_inc(by_norm.sem, 1)

            for s in (bssq, bv_lo, bpt_lo, by_norm, bx, chn, cu, cx):
                dve.sem_inc(s.sem, s.credit)
            bsteps, csteps, dsteps = Steps(dve, o_step), Steps(dve, c_step), Steps(dve, d_step)
            zero_blocks(dve, (1,), (), pre_dve)
            dve.wait_ge(s_rope, 32)
            with dve.Fori(0, DEPTH) as l:
                dve.wait_ge(s_lw, (l + 1) * 16 * 21)
                dve.tensor_copy(cols[:, 0:3], cols_raw[:, 0:3]).then_inc(lay_dve, 1)
                n = 1
                for k in range(6):
                    rows = HC[k % 3][1]
                    dve.tensor_copy(cols[0:rows, 3 + k:4 + k], cols_raw[0:rows, 3 + k:4 + k]).then_inc(lay_dve, 1)
                    n += 1
                hold(dve, lay_dve, l * LAYER_STEPS + n)
                dve.tensor_scalar(w1g[:, :], raw_w1, cols[:, 0:1], None, ALU.mult).then_inc(lay_dve, 1)
                n += 1
                for f in range(2):
                    for j in range(NT):
                        dve.tensor_tensor(ropes[:, f, j, :, :], rope[:, f, j, :, :], qks[:, f, :, :], ALU.mult).then_inc(lay_dve, 1)
                        n += 1
                for k, (full, pair) in enumerate(((raw_qkv, cut(wl, lambda t: t[:, :])),
                                                  (raw_wo, cut(wol, lambda t: t[:, :, :])),
                                                  (raw_w2[:, 0:2, :], cut(w2l, lambda t: t[:, 0:2, :])),
                                                  (raw_w2[0:HC[2][1], 2, :], cut(w2l, lambda t: t[0:HC[2][1], 2, :])),
                                                  (w1g[:, :], cut(w1l, lambda t: t[:, :])))):
                    dve.wait_ge(lay_act, l * 5 + (k + 1))
                    low(pair[1], full, pair[0]).then_inc(lay_dve, 1)
                    n += 1
                dve.wait_ge(lay_pe, l + 1)
                for c0, r in ((0, P), (2, HC[2][1])):
                    w = 2 if c0 == 0 else 1
                    dve.tensor_tensor(b1f[0:r, :].rearrange("p (a c) -> p a c", a=2)[:, :, c0:c0 + w],
                                      bank[0][0:r, 0:6].rearrange("p (a c) -> p a c", a=2)[:, :, c0:c0 + w],
                                      cols[0:r, 3:9].rearrange("p (a c) -> p a c", a=2)[:, :, c0:c0 + w],
                                      ALU.add).then_inc(lay_dve, 1)
                    n += 1
                assert n == LAYER_STEPS
                barrier(dve, l * 3 + 3)

                def b_xt(it, b):
                    dve.wait_ge(bh_hi.sem, bh_hi.at(it, 2 * b + 2))
                    low(xt[1][0:DK, :], bank[5][0:DK, :], xt[0][0:DK, :]).then_inc(bh_lo.sem, 1)
                    low(xt[1][DK:P, 1:T], bank[5][DK:P, 0:T - 1], xt[0][DK:P, 1:T]).then_inc(bh_lo.sem, 1)

                first = (l, 0)
                def stretch(it, j):
                    b_rot(it, j + 2, 1)
                    if j:
                        b_norm(it, j - 1, bsteps)
                    b_max(it, j, 2)
                    b_pt(it, j, 0)
                    b_v(it, j + 2)
                    b_qt(it, j + 1)
                    b_max(it, j, 3)
                    if j == 1:
                        b_xt(it, 1)
                    b_pt(it, j, 1)
                    b_ssq(it, j + 2)
                    b_pt(it, j, 2)
                    if j >= 2:
                        b_ot(it, j - 1)
                    b_max(it, j + 1, 0)
                    b_rot(it, j + 3, 0)
                    b_max(it, j + 1, 1)
                    if j == 1:
                        b_ot(it, 0)
                    b_pt(it, j, 3)

                b_xt(first, 0)
                for j in range(2):
                    b_rot(first, j, 0)
                    b_rot(first, j, 1)
                    b_v(first, j)
                    b_ssq(first, j)
                b_qt(first, 0)
                b_rot(first, 2, 0)
                b_max(first, 0, 0)
                b_max(first, 0, 1)
                stretch(first, 0)
                with dve.Fori(0, BATCH) as b:
                    it = (l, b)
                    bsteps.start(it)
                    here = bass.ds(b * NT, NT)
                    for j in range(1, NT + 1):
                        stretch(it, j)
                    bsteps.end()
                    dve.wait_ge(bo_back.sem, bo_back.at(it, 1))
                    dve.tensor_tensor(xf[:, here, :], bank[5][:, :].rearrange("p (j c) -> p j c", j=NT),
                                      xf[:, here, :], ALU.add).then_inc(bx.sem, 1)
                barrier(dve, l * 3 + 4)
                def c_variance(it, d):
                    csteps.start(it)
                    csteps.n = 2 * NT * d
                    dve.wait_ge(chs.sem, chs.at(it, d + 1))
                    hold(dve, chs_dma.sem, chs_dma.at(it, 32 * (d + 1)))
                    variance(dve, csteps, lambda j: hs[:, j, :], c_root)
                    assert csteps.n == 2 * NT * (d + 1)

                def c_normed(it, d):
                    normed(dve, csteps, lambda j: hs[:, j, :], c_root, it, d, lambda j: xh[:, j, :], chn)

                def c_xt(it, d):
                    dve.wait_ge(ct_hi.sem, ct_hi.at(it, d + 1))
                    low(xt[1][:, :], bank[5][:, :], xt[0][:, :]).then_inc(ct_lo.sem, 1)

                def c_gate(it, d, n):
                    rows, m = HC[n][1], 3 * d + n
                    dve.wait_ge(cgel.sem, cgel.at(it, m + 1))
                    dve.wait_ge(ca_ps.sem, ca_ps.at(it, m + 1))
                    dve.wait_ge(cu_lo.sem, cu_lo.at(it, 3 * d + slot_free(n)))
                    dve.scalar_tensor_tensor(ugl[0:rows, n % 2, :], bank[2 + n % 2][0:rows, :], b1f[0:rows, n:n + 1],
                                             gel[0:rows, n % 2, :], ALU.add, ALU.mult).then_inc(cu.sem, 1)

                first = (l, 0)
                c_variance(first, 0)
                c_normed(first, 0)
                c_xt(first, 0)
                c_variance(first, 1)
                c_gate(first, 0, 0)
                c_gate(first, 0, 1)
                c_normed(first, 1)
                with dve.Fori(0, BATCH) as b:
                    it = (l, b)
                    here = bass.ds(b * NT, NT)
                    c_gate(it, 0, 2)
                    c_xt(it, 1)
                    c_variance(it, 2)
                    c_gate(it, 1, 0)
                    c_normed(it, 2)
                    c_gate(it, 1, 1)
                    dve.wait_ge(co_back.sem, co_back.at(it, 1))
                    dve.tensor_tensor(xf[:, here, :], bank[5][:, :].rearrange("p (j c) -> p j c", j=NT),
                                      xf[:, here, :], ALU.add).then_inc(cx.sem, 1)
                barrier(dve, l * 3 + 5)
            with dve.Fori(0, BATCH) as b:
                dsteps.start(b)
                for j in range(NT):
                    dsteps.did(dve.bn_stats(stats[:, j, :], tile_of(xf, b)(j)))
                hold(dve, d_step.sem, d_step.at(b, NT))
                for j in range(NT):
                    dsteps.did(dve.bn_aggr(mv[:, j, :], stats[:, j, :]))
                hold(dve, d_step.sem, d_step.at(b, 2 * NT))
                dsteps.end()
                dve.tensor_scalar(vare_out[:, bass.ds(b * NT, NT)], mv[:, :, 1], EPS, None, ALU.add).then_inc(d_var.sem, 1)
                dve.tensor_copy(mean_out[:, bass.ds(b * NT, NT)], mv[:, :, 0]).then_inc(d_mean.sem, 1)
            with dve.Fori(0, BATCH) as b:
                here = bass.ds(b * NT, NT)
                dve.wait_ge(d_mean.sem, d_mean.at(b, 1))
                dve.wait_ge(d_rstd.sem, d_rstd.at(b, 1))
                for j in range(NT):
                    t = bass.ds(b * NT + j, 1)
                    dve.tensor_scalar(tile_of(xf, b)(j), tile_of(xf, b)(j), mean_out[:, t],
                                      rstd_out[:, t], ALU.subtract, ALU.mult).then_inc(d_norm.sem, 1)
                dve.wait_ge(d_norm.sem, d_norm.at(b, NT))
                dve.tensor_tensor(x1[:, here, :], x1[:, here, :], xf[:, here, :], ALU.add).then_inc(d_out.sem, 1)

        @block.tensor
        def _(pe):
            pe.sem_inc(by_ps.sem, by_ps.credit)
            pe.wait_ge(s_qk, 48)
            for n in range(4):
                for k in range(4):
                    h = 4 * n + k
                    mm = pe.matmul(bank[n][:, P * k:P * k + P], raw_q[:, h, :], raw_k[:, h, :], start=True, stop=True)
                mm.then_inc(pre_pe, 1)
            pe.wait_ge(s_weights, 32)
            for n in range(2):
                for k in range(4):
                    mm = pe.transpose(bank[4 + n][:, P * k:P * k + P], raw_v[:, 4 * n + k, :], ident[:, :])
                mm.then_inc(pre_pe, 1)
            barrier(pe, 1)

            def a_z(b, h, first_free):
                pe.wait_ge(*first_free)
                three(pe, bank[5][:, :], cut(mh, lambda t: t[:, h % H, :]), cut(xt, lambda t: t[:, :])).then_inc(z_ps.sem, 1)

            def a_scores(b, h, j):
                n = h * NT + j
                pe.wait_ge(s_exp.sem, s_exp.at(b, n - 2 if n % (H * NT) else n))
                if j == 0:
                    pe.wait_ge(z_lo.sem, z_lo.at(b, h + 1))
                acc = score_bank(n)
                z = cut(zt, lambda t: t[:, h % 2, P * j:P * j + P])
                three(pe, acc[:, 0:SW[j]], z, cut(xt, lambda t: t[:, 0:SW[j]]), stop=False)
                pe.matmul(acc[:, SW[j] - P:SW[j]], ident16[:, :], causal[:, :], start=False, stop=True).then_inc(s_ps.sem, 1)

            def a_turn(b, h, g):
                n = 3 * h + g
                pe.wait_ge(s_exp.sem, s_exp.at(b, NT * h + TG_NEEDS[g] + 1))
                if n % (3 * H) < 2:
                    pe.wait_ge(v_lo.sem, v_lo.at(b, 8 * (h // H) + 7 + g))
                else:
                    pe.wait_ge(pt_lo.sem, pt_lo.at(b, n - 1))
                for k, (i, j) in enumerate(TG[g]):
                    mm = pe.transpose(bank[3 + n % 2][:, P * k:P * k + P],
                                      prob[:, h % 2, SO[j] + P * i:SO[j] + P * i + P], ident[:, :])
                mm.then_inc(pt_ps.sem, 1)

            def a_pv(b, h):
                if h % 2 == 0:
                    pe.wait_ge(y_norm.sem, y_norm.at(b, h // 2))
                pe.wait_ge(pt_lo.sem, pt_lo.at(b, 3 * h + 3))
                c0 = DK * (h % H)
                for j in range(NT):
                    for i in range(j + 1):
                        at = TO[(i, j)]
                        acc = wide[:, 256 * (h % 2) + DK * j:256 * (h % 2) + DK * j + DK]
                        mm = three(pe, acc, cut(pt, lambda t: t[:, h % 2, at:at + P]),
                                   cut(vv, lambda t: t[:, i, c0:c0 + DK]), start=i == 0, stop=i == j)
                if h % 2:
                    mm.then_inc(y_ps.sem, 1)

            def a_yturn(b, p, first_free):
                pe.wait_ge(*first_free)
                pe.wait_ge(y_norm.sem, y_norm.at(b, p + 1))
                for j in range(NT):
                    mm = pe.transpose(bank[5][:, P * j:P * j + P],
                                      ysb[:, p % 2, j, :, :].rearrange("p e n -> p (e n)"), ident[:, :])
                mm.then_inc(yt_ps.sem, 1)

            def a_out(b, p):
                if p == PAIRS:
                    pe.wait_ge(a_left.sem, a_left.at(b, NT))
                pe.wait_ge(yt_lo.sem, yt_lo.at(b, p + 1))
                mm = three(pe, wide[:, 512:1024], cut(wog, lambda t: t[:, p % PAIRS, :]), cut(yt, lambda t: t[:, :]),
                           start=p % PAIRS == 0, stop=p % PAIRS == PAIRS - 1)
                if p % PAIRS == PAIRS - 1:
                    mm.then_inc(a_ps.sem, 1)

            def a_xt(b, d):
                pe.wait_ge(xh_ready.sem, xh_ready.at(b, NT * (d + 1)))
                for j in range(NT):
                    mm = pe.transpose(bank[5][:, P * j:P * j + P], xh[:, j, :], ident[:, :])
                mm.then_inc(xt_ps.sem, 1)

            def a_v(b, d, groups):
                for g in groups:
                    if g >= 2:
                        pe.wait_ge(v_lo.sem, v_lo.at(b, 8 * d + g - 1))
                    elif d:
                        pe.wait_ge(pt_lo.sem, pt_lo.at(b, 3 * H - 1 + g))
                    i, n0 = g // 2, 512 * (g % 2)
                    three(pe, bank[3 + g % 2][:, :], cut(xt, lambda t: t[:, P * i:P * i + P]),
                          cut(wv, lambda t: t[:, n0:n0 + 512])).then_inc(v_ps.sem, 1)

            def begin(b, d):
                h = H * d
                if d:
                    a_turn(b, H - 2, 2)
                    a_turn(b, H - 1, 0)
                    pe.wait_ge(yt_lo.sem, yt_lo.at(b, PAIRS - 1))
                a_xt(b, d)
                if d:
                    a_turn(b, H - 1, 1)
                    a_turn(b, H - 1, 2)
                    a_pv(b, H - 2)
                    a_out(b, PAIRS - 2)
                    a_pv(b, H - 1)
                a_z(b, h, (xt_lo.sem, xt_lo.at(b, d + 1)))
                a_v(b, d, (0, 1))
                a_z(b, h + 1, (z_lo.sem, z_lo.at(b, h + 1)))
                a_v(b, d, (2, 3))
                a_scores(b, h, 0)
                a_scores(b, h, 1)
                a_v(b, d, (4, 5))
                a_scores(b, h, 2)
                a_scores(b, h, 3)
                a_z(b, h + 2, (z_lo.sem, z_lo.at(b, h + 2)))
                a_v(b, d, (6, 7))
                a_scores(b, h + 1, 0)
                a_scores(b, h + 1, 1)
                if d:
                    a_yturn(b, PAIRS - 1, (z_lo.sem, z_lo.at(b, h + 3)))
                a_turn(b, h, 0)
                a_scores(b, h + 1, 2)
                a_scores(b, h + 1, 3)
                a_turn(b, h, 1)

            def pair(b, p):
                a_scores(b, 2 * p + 2, 0)
                a_scores(b, 2 * p + 2, 1)
                a_turn(b, 2 * p, 2)
                a_turn(b, 2 * p + 1, 0)
                a_scores(b, 2 * p + 2, 2)
                a_z(b, 2 * p + 3, (yt_lo.sem, yt_lo.at(b, p)) if p else (z_lo.sem, z_lo.at(b, 3)))
                a_turn(b, 2 * p + 1, 1)
                if p == PAIRS:
                    a_out(b, PAIRS - 1)
                a_scores(b, 2 * p + 2, 3)
                a_turn(b, 2 * p + 1, 2)
                a_pv(b, 2 * p)
                a_scores(b, 2 * p + 3, 0)
                if p != PAIRS - 2:
                    a_z(b, 2 * p + 4, (z_lo.sem, z_lo.at(b, 2 * p + 4)))
                a_scores(b, 2 * p + 3, 1)
                a_pv(b, 2 * p + 1)
                a_turn(b, 2 * p + 2, 0)
                if p == PAIRS:
                    pe.wait_ge(a_sb.sem, a_sb.at(b, 1))
                    for j in range(NT):
                        mm = pe.transpose(wide[:, 512 + P * j:512 + P * j + P], tail[:, P * j:P * j + P], ident[:, :])
                    mm.then_inc(a_back.sem, 1)
                a_scores(b, 2 * p + 3, 2)
                a_scores(b, 2 * p + 3, 3)
                a_turn(b, 2 * p + 2, 1)
                if p and p != PAIRS:
                    a_out(b, p - 1)
                a_yturn(b, p, (z_lo.sem, z_lo.at(b, 2 * p + (4 if p == PAIRS - 2 else 5))))

            begin(0, 0)
            pair(0, 0)
            pair(0, 1)
            with pe.Fori(0, BATCH) as b:
                for p in range(2, PAIRS - 1):
                    pair(b, p)
                begin(b, 1)
                pair(b, PAIRS)
                pair(b, PAIRS + 1)
            pe.matmul(wide[:, 512:1024], wog[0][:, 0, :], yt[0][:, :], start=False, stop=True)
            barrier(pe, 2)

            def b_qk(it, j):
                h = cut(xt, lambda t: t[:, P * (j % NT):P * (j % NT) + P])
                if j == 1:
                    pe.wait_ge(brot.sem, brot.at(it, 1))
                elif j >= 2:
                    pe.wait_ge(bqt_lo.sem, bqt_lo.at(it, 3 * (j - 1)))
                for n in range(2):
                    mm = three(pe, wide[:, 512 * n:512 * n + 512], h, cut(wl, lambda t: t[:, 512 * n:512 * n + 512]))
                mm.then_inc(bqk_ps.sem, 1)

            def b_v(it, j):
                h = cut(xt, lambda t: t[:, P * (j % NT):P * (j % NT) + P])
                if j in (1, 2):
                    pe.wait_ge(bv_lo.sem, bv_lo.at(it, 4 * j))
                elif j == 3:
                    pe.wait_ge(bx.sem, bx.at(it, 0))
                elif j > 3:
                    pe.wait_ge(bot_lo.sem, bot_lo.at(it, j - 3))
                three(pe, bank[5][:, :], h, cut(wl, lambda t: t[:, 1024:1536])).then_inc(bv_ps.sem, 1)

            def b_turn(it, j):
                pe.wait_ge(bqk.sem, bqk.at(it, j + 1))
                pe.wait_ge(brot.sem, brot.at(it, j + 2))
                for n in range(8):
                    mm = pe.transpose(wide[:, P * n:P * n + P], qk[j % 2][:, P * n:P * n + P], ident[:, :])
                mm.then_inc(bqt_ps.sem, 1)

            def b_scores(it, j, p):
                q = j * LPAIRS + p
                if p == 0:
                    pe.wait_ge(bqt_lo.sem, bqt_lo.at(it, 3 * j + 3))
                pe.wait_ge(bexp.sem, bexp.at(it, 2 * q - 2))
                k0, w = (0, P) if j % NT == 0 else (P * (j % NT) - WINDOW, P + WINDOW)
                acc = bank[q % 2][:, 0:2 * w].rearrange("p (e n) -> p e n", e=2)
                three(pe, acc, cut(qt, lambda t: t[:, j % 2, p, :]), cut(kt, lambda t: t[:, p, :, k0:k0 + w]), stop=False)
                pe.matmul(acc, ident16[:, :], band[:, :, P + WINDOW - w:], start=False, stop=True).then_inc(bs_ps.sem, 1)

            def b_pt(it, j, p):
                q = j * LPAIRS + p
                m0 = 1 if j % NT == 0 else 0
                pe.wait_ge(bexp.sem, bexp.at(it, 2 * q + 2))
                pe.wait_ge(bpt_lo.sem, bpt_lo.at(it, q - 1))
                for m in range(m0, 3):
                    mm = pe.transpose(bank[2 + 2 * (q % 2)][:, P * m:P * m + P],
                                      lprob[:, q % 2, m, :, :].rearrange("p e n -> p (e n)"), ident[:, :])
                mm.then_inc(bpt_ps.sem, 1)

            def b_pv(it, j, p):
                q = j * LPAIRS + p
                m0 = 1 if j % NT == 0 else 0
                pe.wait_ge(bpt_lo.sem, bpt_lo.at(it, q + 1))
                pe.wait_ge(bv_lo.sem, bv_lo.at(it, 4 * j + 4))
                if p == 0:
                    pe.wait_ge(by_norm.sem, by_norm.at(it, j))
                for m in range(m0, 3):
                    mm = three(pe, ypart[:, P * p:P * p + P], cut(lpt, lambda t: t[:, q % 2, m, :]),
                               cut(vb, lambda t: t[:, 2 * (j % NT) - 1 + m, p, :]), start=m == m0, stop=m == 2)
                mm.then_inc(by_ps.sem, 1)

            def b_ot(it, j):
                pe.wait_ge(by_norm.sem, by_norm.at(it, j + 1))
                if j:
                    pe.wait_ge(bv_lo.sem, bv_lo.at(it, 4 * (j + 4)))
                for n in range(LPAIRS):
                    mm = pe.transpose(bank[5][:, P * n:P * n + P], osb[:, j % 2, P * n:P * n + P], ident[:, :])
                mm.then_inc(bot_ps.sem, 1)

            with pe.Fori(0, DEPTH) as l:
                pe.wait_ge(s_lw, (l + 1) * 16 * 21)
                for n in range(6):
                    r0, rows = HC[n % 3]
                    r0 += HID * (n // 3)
                    mm = pe.matmul(bank[0][0:rows, n:n + 1], raw_w1[:, r0:r0 + rows], cols_raw[:, 1:2], start=True, stop=True)
                mm.then_inc(lay_pe, 1)
                barrier(pe, l * 3 + 3)

                def b_xt(it, b):
                    hold(pe, bxs.sem, bxs.at(it, 16 * b + 16))
                    for j in range(NT):
                        mm = pe.transpose(bank[5][:, P * j:P * j + P], xs[:, j, :], ident[:, :])
                    mm.then_inc(bxt_ps.sem, 1)

                first = (l, 0)
                def stretch(it, j):
                    if j:
                        b_pv(it, j - 1, 2)
                    b_scores(it, j, 2)
                    b_pt(it, j, 0)
                    if j:
                        b_pv(it, j - 1, 3)
                    b_v(it, j + 2)
                    b_turn(it, j + 1)
                    b_scores(it, j, 3)
                    if j == 1:
                        pe.wait_ge(bv_lo.sem, bv_lo.at(it, 16))
                        b_xt(it, 1)
                    b_pt(it, j, 1)
                    if j >= 2:
                        b_ot(it, j - 1)
                    b_pv(it, j, 0)
                    b_pt(it, j, 2)
                    if j == 1:
                        pe.wait_ge(bh_lo.sem, bh_lo.at(it, 4))
                    b_qk(it, j + 3)
                    b_scores(it, j + 1, 0)
                    if j == 1:
                        b_ot(it, 0)
                    if j == NT:
                        pe.wait_ge(bot_lo.sem, bot_lo.at(it, NT))
                        for n in range(LPAIRS):
                            mm = three(pe, bank[5][:, :], cut(wol, lambda t: t[:, n, :]), cut(ot, lambda t: t[:, n, :]),
                                       start=n == 0, stop=n == LPAIRS - 1)
                        mm.then_inc(bo_ps.sem, 1)
                    b_pt(it, j, 3)
                    b_scores(it, j + 1, 1)
                    b_pv(it, j, 1)

                b_xt(first, 0)
                pe.wait_ge(bh_lo.sem, bh_lo.at(first, 2))
                b_qk(first, 0)
                b_v(first, 0)
                b_qk(first, 1)
                b_v(first, 1)
                b_turn(first, 0)
                b_qk(first, 2)
                b_scores(first, 0, 0)
                b_scores(first, 0, 1)
                stretch(first, 0)
                with pe.Fori(0, BATCH) as b:
                    it = (l, b)
                    for j in range(1, NT + 1):
                        stretch(it, j)
                    pe.wait_ge(bo_sb.sem, bo_sb.at(it, 1))
                    for j in range(NT):
                        mm = pe.transpose(bank[5][:, P * j:P * j + P], tail[:, P * j:P * j + P], ident[:, :])
                    mm.then_inc(bo_back.sem, 1)
                barrier(pe, l * 3 + 4)
                def c_xt(it, d):
                    pe.wait_ge(chn.sem, chn.at(it, NT * (d + 1)))
                    pe.wait_ge(cx.sem, cx.at(it, 0))
                    for j in range(NT):
                        mm = pe.transpose(bank[5][:, P * j:P * j + P], xh[:, j, :], ident[:, :])
                    mm.then_inc(ct_ps.sem, 1)

                def c_in(it, d, n):
                    r0, rows = HC[n]
                    if n == 0:
                        pe.wait_ge(ct_lo.sem, ct_lo.at(it, d + 1))
                    pe.wait_ge(cu.sem, cu.at(it, 3 * d + slot_free(n)))
                    for a, s in ((HID, cg_ps), (0, ca_ps)):
                        acc = bank[(0 if a else 2) + n % 2][0:rows, :]
                        three(pe, acc, cut(w1l, lambda t: t[:, a + r0:a + r0 + rows]),
                              cut(xt, lambda t: t[:, :])).then_inc(s.sem, 1)

                def c_out(it, n):
                    rows = HC[n][1]
                    pe.wait_ge(cu_lo.sem, cu_lo.at(it, n + 1))
                    mm = three(pe, bank[4][:, :], cut(w2l, lambda t: t[0:rows, n, :]),
                               cut(ut, lambda t: t[0:rows, n, :]), start=n == 0, stop=n == 2)
                    if n == 2:
                        mm.then_inc(co_ps.sem, 1)

                c_xt(first, 0)
                c_in(first, 0, 0)
                c_in(first, 0, 1)
                with pe.Fori(0, BATCH) as b:
                    it = (l, b)
                    c_in(it, 0, 2)
                    c_xt(it, 1)
                    c_out(it, 0)
                    c_out(it, 1)
                    c_in(it, 1, 0)
                    c_out(it, 2)
                    c_in(it, 1, 1)
                    pe.wait_ge(co_sb.sem, co_sb.at(it, 1))
                    for j in range(NT):
                        mm = pe.transpose(bank[5][:, P * j:P * j + P], tail[:, P * j:P * j + P], ident[:, :])
                    mm.then_inc(co_back.sem, 1)
                barrier(pe, l * 3 + 5)


def rope_tables():
    f = np.float32
    half = np.arange(0, LD, 2, dtype=f)
    t = np.arange(T, dtype=f)
    freqs = t[:, None] * (f(1.0) / f(10000.0) ** (half / f(LD)))[None, :]
    power = (t - T // 2) / f(WINDOW // 2)
    scale = ((half + f(0.4 * LD)) / f(1.4 * LD))[None, :] ** power[:, None]
    both = lambda a: np.concatenate([a, a], axis=-1)
    cos, sin, scale = both(np.cos(freqs)), both(np.sin(freqs)), both(scale)
    sin[:, :LD // 2] *= -1
    return [np.stack([a * scale * f(8.0), a / scale], axis=1).astype(f) for a in (cos, sin)]


def constants():
    i, c = np.arange(P)[:, None], np.arange(P + WINDOW)[None, :]
    causal = np.where(np.arange(P)[None, :] > i, MASKED, 0.0).astype(np.float32)
    band = np.where((c >= i) & (c <= i + WINDOW), 0.0, MASKED).astype(np.float32)
    cos, sin = rope_tables()
    return {"ident": np.eye(P, dtype=np.float32), "causal": causal, "band": np.concatenate([band, band], axis=1),
            "rope_cos": cos, "rope_sin": sin}


_INS = ["L0_attn_x", "L0_attn_w_q", "L0_attn_w_k", "L0_attn_w_v", "L0_attn_w_o", "L0_ffn_wqkv", "L0_ffn_q_scale",
        "L0_ffn_k_scale", "L0_ffn_wo", "L0_ffn_ln_g", "L0_ffn_ln_b", "L0_ffn_w1", "L0_ffn_b1", "L0_ffn_w2", "L0_ffn_b2"]


def kernel(**inputs):
    import concourse.bacc as _bacc
    from concourse.bass_utils import run_bass_kernel_spmd as _run

    nc = _bacc.Bacc("TRN2", target_bir_lowering=False, num_devices=1)
    arrays, args = {}, []
    given = {**{n: inputs[n] for n in _INS}, **constants()}
    for name, a in given.items():
        a = np.ascontiguousarray(a)
        arrays[f"in_{name}"] = a
        args.append(nc.dram_tensor(f"in_{name}", a.shape, mybir.dt.from_np(a.dtype), kind="ExternalInput").ap())
    args.append(nc.dram_tensor("out_0", (BATCH, T, C), F32, kind="ExternalOutput").ap())
    sandwich(nc, *args)
    r = _run(nc, [arrays], core_ids=[0])
    return r.results[0]["out_0"]
```
